# Optimizing a Trainium2 kernel written in Bass

```python
import numpy as np
import jax
import jax.numpy as jnp

def _softmax(x, axis=-1):
    return jax.nn.softmax(x, axis=axis)

def _gelu(x):
    return jax.nn.gelu(x, approximate=True)

def _silu(x):
    return jax.nn.silu(x)

def _sigmoid(x):
    return jax.nn.sigmoid(x)

def _layernorm(x, axis=-1, eps=1e-05):
    m = jnp.mean(x, axis=axis, keepdims=True)
    v = jnp.var(x, axis=axis, keepdims=True)
    return (x - m) / jnp.sqrt(v + eps)

def _scatter_add(tgt, idx, src, axis=0):
    return tgt.at[idx].add(src)

def _segment_sum(src, seg, n):
    return jax.ops.segment_sum(src, seg, n)
kernel_name = 'mk_flamingo_gated_d4_seqx_r8_2bd6b6'

def setup_inputs(seed: int=0):
    np.random.seed(seed)
    _w = jnp.asarray

    def _rec_inputs():
        import jax
        import jax.numpy as jnp
        _rk = jax.random.key(seed)
        x = -0.0002928 + 1 * jax.random.normal(jax.random.fold_in(_rk, 1), (4, 512, 128), jnp.float32)
        _lenS = 512 - jax.random.randint(jax.random.fold_in(_rk, 7), (4,), 0, max(1, 512 // 4) + 1, jnp.int32)
        _lenS2 = 77 - jax.random.randint(jax.random.fold_in(_rk, 8), (4,), 0, max(1, 77 // 4) + 1, jnp.int32)
        _ctx_1024P = jax.random.normal(jax.random.fold_in(_rk, 11), (4, 16, 128), jnp.float32)
        _ctx_1024c = jax.random.dirichlet(jax.random.fold_in(_rk, 511), 0.3 * jnp.ones((16,), jnp.float32), (4, 77))
        _ctx_1024t = jnp.einsum('bsk,bkd->bsd', _ctx_1024c, _ctx_1024P)
        _ctx_1024t = _ctx_1024t * jax.lax.rsqrt(jnp.mean(jnp.square(_ctx_1024t)) + 1e-12) * 0.953939
        ctx_1024 = -1.39393e-06 + 0.999914 * (_ctx_1024t + 0.3 * jax.random.normal(jax.random.fold_in(_rk, 611), (4, 77, 128), jnp.float32))
        _validS = jnp.arange(512)[None, :] < _lenS[:, None]
        _validS2 = jnp.arange(77)[None, :] < _lenS2[:, None]
        _causal = jnp.tril(jnp.ones((512, 512), dtype=bool))
        mask_1x1xSxS2_ik0 = jnp.where(jnp.broadcast_to(_validS2[0:1, None, None, :], (1, 1, 512, 77)), 0, 1).astype(jnp.int32)
        _g = jax.random.normal(jax.random.fold_in(_rk, 9001), (2, 4), jnp.float32)
        _g = jnp.sign(_g) * jnp.maximum(jnp.abs(_g), 1.0) + (_g == 0) * 1.0
        g_xattn = _g[0]
        g_ffn = _g[1]
        return (x, ctx_1024, mask_1x1xSxS2_ik0, g_xattn, g_ffn)
    x, ctx_1024, mask_1x1xSxS2_ik0, g_xattn, g_ffn = _rec_inputs()

    def _L0_xattn_setup():
        import jax, jax.numpy as jnp
        import numpy as np
        N_HEADS = 16
        KQ_DIM = 64
        EMB_DIM = 128
        CTX_DIM = 128
        EPS = 1e-05

        def _layernorm(x, w, b):
            mu = jnp.mean(x, axis=-1, keepdims=True)
            var = jnp.mean(jnp.square(x - mu), axis=-1, keepdims=True)
            return (x - mu) * jax.lax.rsqrt(var + EPS) * w + b
        key = jax.random.key(seed)
        ks = jax.random.split(key, 10)
        B, SQ, SK = (2, 256, 256)
        inner = N_HEADS * KQ_DIM
        s_e = 1.0 / np.sqrt(EMB_DIM)
        s_c = 1.0 / np.sqrt(CTX_DIM)
        s_i = 1.0 / np.sqrt(inner)
        return {'emb': jax.random.normal(ks[0], (B, SQ, EMB_DIM), jnp.float32), 'context': jax.random.normal(ks[1], (B, SK, CTX_DIM), jnp.float32), 'Wq': jax.random.uniform(ks[2], (inner, EMB_DIM), jnp.float32, -s_e, s_e), 'Wk': jax.random.uniform(ks[3], (inner, CTX_DIM), jnp.float32, -s_c, s_c), 'Wv': jax.random.uniform(ks[4], (inner, CTX_DIM), jnp.float32, -s_c, s_c), 'Wu': jax.random.uniform(ks[5], (EMB_DIM, inner), jnp.float32, -s_i, s_i), 'bu': jax.random.uniform(ks[6], (EMB_DIM,), jnp.float32, -s_i, s_i), 'qn_w': jnp.ones((KQ_DIM,), jnp.float32), 'qn_b': jnp.zeros((KQ_DIM,), jnp.float32), 'kn_w': jnp.ones((KQ_DIM,), jnp.float32), 'kn_b': jnp.zeros((KQ_DIM,), jnp.float32)}
    _L0_xattn_all = _L0_xattn_setup()
    _L0_xattn_in = {k: v for k, v in _L0_xattn_all.items() if k in ('Wq', 'Wk', 'Wv', 'Wu', 'bu', 'qn_w', 'qn_b', 'kn_w', 'kn_b')}
    del _L0_xattn_all

    def _L0_ffn_setup():
        import jax, jax.numpy as jnp
        import numpy as np
        HIDDEN = 128
        INTER = 512
        key = jax.random.key(seed)
        k1, k2, k3, k4, k5 = jax.random.split(key, 5)
        hidden_states = jax.random.normal(k1, (4, 256, HIDDEN), dtype=jnp.float32)
        W1 = jax.random.normal(k2, (HIDDEN, INTER), dtype=jnp.float32) * (1.0 / np.sqrt(HIDDEN))
        b1 = jax.random.normal(k3, (INTER,), dtype=jnp.float32) * 0.02
        W2 = jax.random.normal(k4, (INTER, HIDDEN), dtype=jnp.float32) * (1.0 / np.sqrt(INTER))
        b2 = jax.random.normal(k5, (HIDDEN,), dtype=jnp.float32) * 0.02
        return {'hidden_states': hidden_states, 'W1': W1, 'b1': b1, 'W2': W2, 'b2': b2}
    _L0_ffn_all = _L0_ffn_setup()
    _L0_ffn_in = {k: v for k, v in _L0_ffn_all.items() if k in ('W1', 'b1', 'W2', 'b2')}
    del _L0_ffn_all

    def _L1_xattn_setup():
        import jax, jax.numpy as jnp
        import numpy as np
        B, M, N, DIM, DH, H = (8, 512, 64, 128, 128, 8)
        INNER = DH * H
        EPS = 1e-05

        def _layernorm(x, g, b):
            mu = jnp.mean(x, axis=-1, keepdims=True)
            var = jnp.var(x, axis=-1, keepdims=True)
            return (x - mu) * jax.lax.rsqrt(var + EPS) * g + b
        key = jax.random.key(seed)
        ks = jax.random.split(key, 8)
        sd = 0.02
        return {'x': jax.random.normal(ks[0], (B, M, DIM), jnp.float32), 'latents': jax.random.normal(ks[1], (B, N, DIM), jnp.float32), 'gamma_media': jnp.ones((DIM,), jnp.float32), 'beta_media': jnp.zeros((DIM,), jnp.float32), 'gamma_lat': jnp.ones((DIM,), jnp.float32), 'beta_lat': jnp.zeros((DIM,), jnp.float32), 'Wq': jax.random.normal(ks[2], (DIM, INNER), jnp.float32) * sd, 'bq': jnp.zeros((INNER,), jnp.float32), 'Wkv': jax.random.normal(ks[3], (DIM, 2 * INNER), jnp.float32) * sd, 'bkv': jnp.zeros((2 * INNER,), jnp.float32), 'Wo': jax.random.normal(ks[4], (INNER, DIM), jnp.float32) * sd, 'bo': jnp.zeros((DIM,), jnp.float32)}
    _L1_xattn_all = _L1_xattn_setup()
    _L1_xattn_in = {k: v for k, v in _L1_xattn_all.items() if k in ('gamma_media', 'beta_media', 'gamma_lat', 'beta_lat', 'Wq', 'bq', 'Wkv', 'bkv', 'Wo', 'bo')}
    del _L1_xattn_all

    def _L1_ffn_setup():
        import jax, jax.numpy as jnp
        import numpy as np
        E = 8
        K = 2
        D = 128
        key = jax.random.key(seed)
        k0, k1, k2, k3 = jax.random.split(key, 4)
        x = jax.random.normal(k0, (2, 256, D), dtype=jnp.float32)
        gate_w = jax.random.normal(k1, (D, E), dtype=jnp.float32) * 0.02
        fc_w = jax.random.normal(k2, (E, D, 4 * D), dtype=jnp.float32) * 0.02
        proj_w = jax.random.normal(k3, (E, 4 * D, D), dtype=jnp.float32) * 0.02
        return {'x': x, 'gate_w': gate_w, 'fc_w': fc_w, 'proj_w': proj_w}
    _L1_ffn_all = _L1_ffn_setup()
    _L1_ffn_in = {k: v for k, v in _L1_ffn_all.items() if k in ('gate_w', 'fc_w', 'proj_w')}
    del _L1_ffn_all

    def _L2_xattn_setup():
        import jax, jax.numpy as jnp
        import numpy as np
        HIDDEN = 128
        N_HEAD = 16
        HEAD_DIM = HIDDEN // N_HEAD

        def _rope(x):
            L, d = (x.shape[-2], x.shape[-1])
            pos = jnp.arange(L, dtype=x.dtype)[:, None]
            ids = jnp.arange(d // 2, dtype=x.dtype)
            theta = jnp.power(jnp.asarray(10000.0, x.dtype), 2.0 * ids / d)
            ang = pos / theta
            sin = jnp.repeat(jnp.sin(ang), 2, axis=-1)
            cos = jnp.repeat(jnp.cos(ang), 2, axis=-1)
            x_rot = jnp.stack([-x[..., 1::2], x[..., 0::2]], axis=-1).reshape(x.shape)
            return x * cos + x_rot * sin
        key = jax.random.key(seed)
        ks = jax.random.split(key, 5)
        B, LQ, LK = (8, 128, 256)
        scale = 1.0 / np.sqrt(HIDDEN)
        return {'x': jax.random.normal(ks[0], (B, LQ, HIDDEN), dtype=jnp.float32), 'y': jax.random.normal(ks[1], (B, LK, HIDDEN), dtype=jnp.float32), 'Wq': jax.random.normal(ks[2], (HIDDEN, HIDDEN), dtype=jnp.float32) * scale, 'Wkv': jax.random.normal(ks[3], (2 * HIDDEN, HIDDEN), dtype=jnp.float32) * scale, 'Wo': jax.random.normal(ks[4], (HIDDEN, HIDDEN), dtype=jnp.float32) * scale}
    _L2_xattn_all = _L2_xattn_setup()
    _L2_xattn_in = {k: v for k, v in _L2_xattn_all.items() if k in ('Wq', 'Wkv', 'Wo')}
    del _L2_xattn_all

    def _L2_ffn_setup():
        import jax, jax.numpy as jnp
        import numpy as np
        B, S, DIM = (4, 512, 128)
        BASE_COUPLING = 0.1
        NUM_CYCLES = 3

        def _gelu(x):
            return jax.nn.gelu(x, approximate=False)

        def _coupling_net(h, w1, b1, w2, b2, w3, b3, w4, b4):
            h = _gelu(h @ w1 + b1)
            h = _gelu(h @ w2 + b2)
            h = _gelu(h @ w3 + b3)
            return jax.nn.sigmoid(h @ w4 + b4)

        def _global_net(h, w1, b1, w2, b2, w3, b3):
            h = _gelu(h @ w1 + b1)
            h = _gelu(h @ w2 + b2)
            return jax.nn.sigmoid(h @ w3 + b3)

        def _twist(x):
            o_r, o_i, p_r, p_i = jnp.split(x, 4, axis=-1)
            return jnp.concatenate([p_r, -p_i, -o_r, o_i], axis=-1)
        key = jax.random.key(seed)
        ks = jax.random.split(key, 9)
        d = DIM

        def w(k, fan_in, fan_out):
            return jax.random.normal(k, (fan_in, fan_out), dtype=jnp.float32) / np.sqrt(fan_in).astype(np.float32)
        inp = {'x': jax.random.normal(ks[0], (B, S, d), dtype=jnp.float32)}
        cn_dims = [(d, d), (d, d // 2), (d // 2, d // 4), (d // 4, 1)]
        for i, (a, b) in enumerate(cn_dims):
            inp[f'cn_w{i + 1}'] = w(ks[1 + i], a, b)
            inp[f'cn_b{i + 1}'] = jnp.zeros((b,), dtype=jnp.float32)
        gc_dims = [(d, d // 2), (d // 2, d // 4), (d // 4, 1)]
        for i, (a, b) in enumerate(gc_dims):
            inp[f'gc_w{i + 1}'] = w(ks[5 + i], a, b)
            inp[f'gc_b{i + 1}'] = jnp.zeros((b,), dtype=jnp.float32)
        inp['adaptive_range'] = jnp.full((1,), 0.2, dtype=jnp.float32)
        return inp
    _L2_ffn_all = _L2_ffn_setup()
    _L2_ffn_in = {k: v for k, v in _L2_ffn_all.items() if k in ('cn_w1', 'cn_b1', 'cn_w2', 'cn_b2', 'cn_w3', 'cn_b3', 'cn_w4', 'cn_b4', 'gc_w1', 'gc_b1', 'gc_w2', 'gc_b2', 'gc_w3', 'gc_b3', 'adaptive_range')}
    del _L2_ffn_all

    def _L3_xattn_setup():
        import jax, jax.numpy as jnp
        import numpy as np
        B, S, D, H = (2, 256, 128, 16)
        DK = D // H

        def _split_heads(x):
            b, s, _ = x.shape
            return x.reshape(b, s, H, DK).transpose(0, 2, 1, 3)
        key = jax.random.key(seed)
        ks = jax.random.split(key, 12)
        scale = 1.0 / np.sqrt(D)
        inp = {'q': jax.random.normal(ks[0], (B, S, D), dtype=jnp.float32), 'k': jax.random.normal(ks[1], (B, S, D), dtype=jnp.float32), 'v': jax.random.normal(ks[2], (B, S, D), dtype=jnp.float32), 'mask': jnp.tril(jnp.ones((S, S), dtype=jnp.int32))[None, None, :, :], 'wq_w': jax.random.normal(ks[3], (D, D), dtype=jnp.float32) * scale, 'wq_b': jax.random.normal(ks[4], (D,), dtype=jnp.float32) * scale, 'wk_w': jax.random.normal(ks[5], (D, D), dtype=jnp.float32) * scale, 'wk_b': jax.random.normal(ks[6], (D,), dtype=jnp.float32) * scale, 'wv_w': jax.random.normal(ks[7], (D, D), dtype=jnp.float32) * scale, 'wv_b': jax.random.normal(ks[8], (D,), dtype=jnp.float32) * scale, 'wo_w': jax.random.normal(ks[9], (D, D), dtype=jnp.float32) * scale, 'wo_b': jax.random.normal(ks[10], (D,), dtype=jnp.float32) * scale}
        return inp
    _L3_xattn_all = _L3_xattn_setup()
    _L3_xattn_in = {k: v for k, v in _L3_xattn_all.items() if k in ('wq_w', 'wq_b', 'wk_w', 'wk_b', 'wv_w', 'wv_b', 'wo_w', 'wo_b')}
    del _L3_xattn_all

    def _L3_ffn_setup():
        import jax, jax.numpy as jnp
        import numpy as np
        TOP_P = 0.8
        B, T, H, F, E = (2, 256, 128, 512, 8)
        key = jax.random.key(seed)
        k0, k1, k2, k3 = jax.random.split(key, 4)
        x = jax.random.normal(k0, (B, T, H), jnp.float32)
        Wr = jax.random.normal(k1, (H, E), jnp.float32) * 0.02
        br = jnp.zeros((E,), jnp.float32)
        W1 = jax.random.normal(k2, (E, H, F), jnp.float32) * 0.02
        b1 = jnp.zeros((E, F), jnp.float32)
        W2 = jax.random.normal(k3, (E, F, H), jnp.float32) * 0.02
        b2 = jnp.zeros((E, H), jnp.float32)
        return {'x': x, 'Wr': Wr, 'br': br, 'W1': W1, 'b1': b1, 'W2': W2, 'b2': b2}
    _L3_ffn_all = _L3_ffn_setup()
    _L3_ffn_in = {k: v for k, v in _L3_ffn_all.items() if k in ('Wr', 'br', 'W1', 'b1', 'W2', 'b2')}
    del _L3_ffn_all
    return {'x': x, 'ctx_1024': ctx_1024, 'mask_1x1xSxS2_ik0': mask_1x1xSxS2_ik0, 'g_xattn': g_xattn, 'g_ffn': g_ffn, 'L0_xattn_Wq': _L0_xattn_in['Wq'], 'L0_xattn_Wk': _L0_xattn_in['Wk'], 'L0_xattn_Wv': _L0_xattn_in['Wv'], 'L0_xattn_Wu': _L0_xattn_in['Wu'], 'L0_xattn_bu': _L0_xattn_in['bu'], 'L0_xattn_qn_w': _L0_xattn_in['qn_w'], 'L0_xattn_qn_b': _L0_xattn_in['qn_b'], 'L0_xattn_kn_w': _L0_xattn_in['kn_w'], 'L0_xattn_kn_b': _L0_xattn_in['kn_b'], 'L0_ffn_W1': _L0_ffn_in['W1'], 'L0_ffn_b1': _L0_ffn_in['b1'], 'L0_ffn_W2': _L0_ffn_in['W2'], 'L0_ffn_b2': _L0_ffn_in['b2'], 'L1_xattn_gamma_media': _L1_xattn_in['gamma_media'], 'L1_xattn_beta_media': _L1_xattn_in['beta_media'], 'L1_xattn_gamma_lat': _L1_xattn_in['gamma_lat'], 'L1_xattn_beta_lat': _L1_xattn_in['beta_lat'], 'L1_xattn_Wq': _L1_xattn_in['Wq'], 'L1_xattn_bq': _L1_xattn_in['bq'], 'L1_xattn_Wkv': _L1_xattn_in['Wkv'], 'L1_xattn_bkv': _L1_xattn_in['bkv'], 'L1_xattn_Wo': _L1_xattn_in['Wo'], 'L1_xattn_bo': _L1_xattn_in['bo'], 'L1_ffn_gate_w': _L1_ffn_in['gate_w'], 'L1_ffn_fc_w': _L1_ffn_in['fc_w'], 'L1_ffn_proj_w': _L1_ffn_in['proj_w'], 'L2_xattn_Wq': _L2_xattn_in['Wq'], 'L2_xattn_Wkv': _L2_xattn_in['Wkv'], 'L2_xattn_Wo': _L2_xattn_in['Wo'], 'L2_ffn_cn_w1': _L2_ffn_in['cn_w1'], 'L2_ffn_cn_b1': _L2_ffn_in['cn_b1'], 'L2_ffn_cn_w2': _L2_ffn_in['cn_w2'], 'L2_ffn_cn_b2': _L2_ffn_in['cn_b2'], 'L2_ffn_cn_w3': _L2_ffn_in['cn_w3'], 'L2_ffn_cn_b3': _L2_ffn_in['cn_b3'], 'L2_ffn_cn_w4': _L2_ffn_in['cn_w4'], 'L2_ffn_cn_b4': _L2_ffn_in['cn_b4'], 'L2_ffn_gc_w1': _L2_ffn_in['gc_w1'], 'L2_ffn_gc_b1': _L2_ffn_in['gc_b1'], 'L2_ffn_gc_w2': _L2_ffn_in['gc_w2'], 'L2_ffn_gc_b2': _L2_ffn_in['gc_b2'], 'L2_ffn_gc_w3': _L2_ffn_in['gc_w3'], 'L2_ffn_gc_b3': _L2_ffn_in['gc_b3'], 'L2_ffn_adaptive_range': _L2_ffn_in['adaptive_range'], 'L3_xattn_wq_w': _L3_xattn_in['wq_w'], 'L3_xattn_wq_b': _L3_xattn_in['wq_b'], 'L3_xattn_wk_w': _L3_xattn_in['wk_w'], 'L3_xattn_wk_b': _L3_xattn_in['wk_b'], 'L3_xattn_wv_w': _L3_xattn_in['wv_w'], 'L3_xattn_wv_b': _L3_xattn_in['wv_b'], 'L3_xattn_wo_w': _L3_xattn_in['wo_w'], 'L3_xattn_wo_b': _L3_xattn_in['wo_b'], 'L3_ffn_Wr': _L3_ffn_in['Wr'], 'L3_ffn_br': _L3_ffn_in['br'], 'L3_ffn_W1': _L3_ffn_in['W1'], 'L3_ffn_b1': _L3_ffn_in['b1'], 'L3_ffn_W2': _L3_ffn_in['W2'], 'L3_ffn_b2': _L3_ffn_in['b2']}

def reference(x, ctx_1024, mask_1x1xSxS2_ik0, g_xattn, g_ffn, L0_xattn_Wq, L0_xattn_Wk, L0_xattn_Wv, L0_xattn_Wu, L0_xattn_bu, L0_xattn_qn_w, L0_xattn_qn_b, L0_xattn_kn_w, L0_xattn_kn_b, L0_ffn_W1, L0_ffn_b1, L0_ffn_W2, L0_ffn_b2, L1_xattn_gamma_media, L1_xattn_beta_media, L1_xattn_gamma_lat, L1_xattn_beta_lat, L1_xattn_Wq, L1_xattn_bq, L1_xattn_Wkv, L1_xattn_bkv, L1_xattn_Wo, L1_xattn_bo, L1_ffn_gate_w, L1_ffn_fc_w, L1_ffn_proj_w, L2_xattn_Wq, L2_xattn_Wkv, L2_xattn_Wo, L2_ffn_cn_w1, L2_ffn_cn_b1, L2_ffn_cn_w2, L2_ffn_cn_b2, L2_ffn_cn_w3, L2_ffn_cn_b3, L2_ffn_cn_w4, L2_ffn_cn_b4, L2_ffn_gc_w1, L2_ffn_gc_b1, L2_ffn_gc_w2, L2_ffn_gc_b2, L2_ffn_gc_w3, L2_ffn_gc_b3, L2_ffn_adaptive_range, L3_xattn_wq_w, L3_xattn_wq_b, L3_xattn_wk_w, L3_xattn_wk_b, L3_xattn_wv_w, L3_xattn_wv_b, L3_xattn_wo_w, L3_xattn_wo_b, L3_ffn_Wr, L3_ffn_br, L3_ffn_W1, L3_ffn_b1, L3_ffn_W2, L3_ffn_b2):
    import jax
    import jax.numpy as jnp

    def _L0_xattn_ref(emb, context, Wq, Wk, Wv, Wu, bu, qn_w, qn_b, kn_w, kn_b):
        import jax, jax.numpy as jnp
        import numpy as np
        N_HEADS = 16
        KQ_DIM = 64
        EMB_DIM = 128
        CTX_DIM = 128
        EPS = 1e-05

        def _layernorm(x, w, b):
            mu = jnp.mean(x, axis=-1, keepdims=True)
            var = jnp.mean(jnp.square(x - mu), axis=-1, keepdims=True)
            return (x - mu) * jax.lax.rsqrt(var + EPS) * w + b
        B, SQ, _ = emb.shape
        SK = context.shape[1]
        q = (emb @ Wq.T).reshape(B, SQ, N_HEADS, KQ_DIM).transpose(0, 2, 1, 3)
        k = (context @ Wk.T).reshape(B, SK, N_HEADS, KQ_DIM).transpose(0, 2, 1, 3)
        v = (context @ Wv.T).reshape(B, SK, N_HEADS, KQ_DIM).transpose(0, 2, 1, 3)
        q = _layernorm(q, qn_w, qn_b)
        k = _layernorm(k, kn_w, kn_b)
        scale = 1.0 / jnp.sqrt(jnp.asarray(KQ_DIM, emb.dtype))
        attn = jnp.einsum('bhqd,bhkd->bhqk', q, k) * scale
        attn = jax.nn.softmax(attn, axis=-1)
        out = jnp.einsum('bhqk,bhkd->bhqd', attn, v)
        out = out.transpose(0, 2, 1, 3).reshape(B, SQ, N_HEADS * KQ_DIM)
        return out @ Wu.T + bu

    def _L0_ffn_ref(hidden_states, W1, b1, W2, b2):
        import jax, jax.numpy as jnp
        import numpy as np
        HIDDEN = 128
        INTER = 512
        h = jax.nn.relu(jnp.einsum('bsh,hi->bsi', hidden_states, W1) + b1)
        return jnp.einsum('bsi,ih->bsh', h, W2) + b2

    def _L1_xattn_ref(x, latents, gamma_media, beta_media, gamma_lat, beta_lat, Wq, bq, Wkv, bkv, Wo, bo):
        import jax, jax.numpy as jnp
        import numpy as np
        B, M, N, DIM, DH, H = (8, 512, 64, 128, 128, 8)
        INNER = DH * H
        EPS = 1e-05

        def _layernorm(x, g, b):
            mu = jnp.mean(x, axis=-1, keepdims=True)
            var = jnp.var(x, axis=-1, keepdims=True)
            return (x - mu) * jax.lax.rsqrt(var + EPS) * g + b
        b = x.shape[0]
        xn = _layernorm(x, gamma_media, beta_media)
        ln = _layernorm(latents, gamma_lat, beta_lat)
        q = ln @ Wq + bq
        kv_input = jnp.concatenate([xn, ln], axis=1)
        kv = kv_input @ Wkv + bkv
        k, v = jnp.split(kv, 2, axis=-1)

        def to_heads(t):
            return t.reshape(b, t.shape[1], H, DH).transpose(0, 2, 1, 3)
        q, k, v = (to_heads(q), to_heads(k), to_heads(v))
        q = q * DH ** (-0.5)
        sim = jnp.einsum('bhid,bhjd->bhij', q, k)
        attn = jax.nn.softmax(sim, axis=-1)
        out = jnp.einsum('bhij,bhjd->bhid', attn, v)
        out = out.transpose(0, 2, 1, 3).reshape(b, -1, INNER)
        return out @ Wo + bo

    def _L1_ffn_ref(x, gate_w, fc_w, proj_w):
        import jax, jax.numpy as jnp
        import numpy as np
        E = 8
        K = 2
        D = 128
        orig_shape = x.shape
        d = orig_shape[-1]
        xt = x.reshape(-1, d)
        gates = jax.nn.softmax(xt @ gate_w, axis=-1)
        top_v, top_i = jax.lax.top_k(gates, K)
        top_v = top_v / jnp.sum(top_v, axis=-1, keepdims=True)
        h = jnp.einsum('nd,edf->enf', xt, fc_w)
        h = jax.nn.gelu(h, approximate=False)
        eo = jnp.einsum('enf,efd->end', h, proj_w)
        eo_nt = jnp.swapaxes(eo, 0, 1)
        sel = jnp.take_along_axis(eo_nt, top_i[:, :, None], axis=1)
        out = jnp.sum(sel * top_v[:, :, None], axis=1)
        return out.reshape(orig_shape)

    def _L2_xattn_ref(x, y, Wq, Wkv, Wo):
        import jax, jax.numpy as jnp
        import numpy as np
        HIDDEN = 128
        N_HEAD = 16
        HEAD_DIM = HIDDEN // N_HEAD

        def _rope(x):
            L, d = (x.shape[-2], x.shape[-1])
            pos = jnp.arange(L, dtype=x.dtype)[:, None]
            ids = jnp.arange(d // 2, dtype=x.dtype)
            theta = jnp.power(jnp.asarray(10000.0, x.dtype), 2.0 * ids / d)
            ang = pos / theta
            sin = jnp.repeat(jnp.sin(ang), 2, axis=-1)
            cos = jnp.repeat(jnp.cos(ang), 2, axis=-1)
            x_rot = jnp.stack([-x[..., 1::2], x[..., 0::2]], axis=-1).reshape(x.shape)
            return x * cos + x_rot * sin
        B, LQ, _ = x.shape
        LK = y.shape[1]
        q = (x @ Wq.T).reshape(B, LQ, N_HEAD, HEAD_DIM).transpose(0, 2, 1, 3)
        kv = (y @ Wkv.T).reshape(B, LK, N_HEAD, 2 * HEAD_DIM).transpose(0, 2, 1, 3)
        k, v = jnp.split(kv, 2, axis=-1)
        q = _rope(q)
        k = _rope(k)
        scores = jnp.einsum('bhqd,bhkd->bhqk', q, k)
        probs = jax.nn.softmax(scores, axis=-1)
        out = jnp.einsum('bhqk,bhkd->bhqd', probs, v)
        out = out.transpose(0, 2, 1, 3).reshape(B, LQ, HIDDEN)
        return out @ Wo.T

    def _L2_ffn_ref(x, cn_w1, cn_b1, cn_w2, cn_b2, cn_w3, cn_b3, cn_w4, cn_b4, gc_w1, gc_b1, gc_w2, gc_b2, gc_w3, gc_b3, adaptive_range):
        import jax, jax.numpy as jnp
        import numpy as np
        B, S, DIM = (4, 512, 128)
        BASE_COUPLING = 0.1
        NUM_CYCLES = 3

        def _gelu(x):
            return jax.nn.gelu(x, approximate=False)

        def _coupling_net(h, w1, b1, w2, b2, w3, b3, w4, b4):
            h = _gelu(h @ w1 + b1)
            h = _gelu(h @ w2 + b2)
            h = _gelu(h @ w3 + b3)
            return jax.nn.sigmoid(h @ w4 + b4)

        def _global_net(h, w1, b1, w2, b2, w3, b3):
            h = _gelu(h @ w1 + b1)
            h = _gelu(h @ w2 + b2)
            return jax.nn.sigmoid(h @ w3 + b3)

        def _twist(x):
            o_r, o_i, p_r, p_i = jnp.split(x, 4, axis=-1)
            return jnp.concatenate([p_r, -p_i, -o_r, o_i], axis=-1)
        global_context = x.mean(axis=1, keepdims=True)
        gf = _global_net(global_context, gc_w1, gc_b1, gc_w2, gc_b2, gc_w3, gc_b3)
        out = x
        for _ in range(NUM_CYCLES):
            tf = _coupling_net(out, cn_w1, cn_b1, cn_w2, cn_b2, cn_w3, cn_b3, cn_w4, cn_b4)
            combined = 0.7 * gf + 0.3 * tf
            coupling = BASE_COUPLING + adaptive_range * (combined - 0.5) * 2.0
            out = out + coupling * _twist(out)
        return out

    def _L3_xattn_ref(q, k, v, mask, wq_w, wq_b, wk_w, wk_b, wv_w, wv_b, wo_w, wo_b):
        import jax, jax.numpy as jnp
        import numpy as np
        B, S, D, H = (2, 256, 128, 16)
        DK = D // H

        def _split_heads(x):
            b, s, _ = x.shape
            return x.reshape(b, s, H, DK).transpose(0, 2, 1, 3)
        Q = _split_heads(q @ wq_w.T + wq_b)
        K = _split_heads(k @ wk_w.T + wk_b)
        V = _split_heads(v @ wv_w.T + wv_b)
        scale = 1.0 / jnp.sqrt(jnp.asarray(DK, dtype=Q.dtype))
        scores = jnp.einsum('bhqd,bhkd->bhqk', Q, K) * scale
        scores = jnp.where(mask == 0, jnp.asarray(-1000000000.0, dtype=scores.dtype), scores)
        attn = jax.nn.softmax(scores, axis=-1)
        out = jnp.einsum('bhqk,bhkd->bhqd', attn, V)
        out = out.transpose(0, 2, 1, 3).reshape(out.shape[0], -1, D)
        return out @ wo_w.T + wo_b

    def _L3_ffn_ref(x, Wr, br, W1, b1, W2, b2):
        import jax, jax.numpy as jnp
        import numpy as np
        TOP_P = 0.8
        B, T, H, F, E = (2, 256, 128, 512, 8)
        probs = jax.nn.softmax(x @ Wr + br, axis=-1)
        sorted_idx = jnp.argsort(-probs, axis=-1)
        sorted_probs = jnp.take_along_axis(probs, sorted_idx, axis=-1)
        cum = jnp.cumsum(sorted_probs, axis=-1)
        mask = cum < TOP_P
        mask = mask.at[..., 0].set(True)
        inv = jnp.argsort(sorted_idx, axis=-1)
        keep = jnp.take_along_axis(mask, inv, axis=-1)
        gate = probs * keep
        h = jax.nn.relu(jnp.einsum('bth,ehf->betf', x, W1) + b1[None, :, None, :])
        y = jnp.einsum('betf,efh->beth', h, W2) + b2[None, :, None, :]
        return jnp.einsum('bte,beth->bth', gate, y)
    x = x + jnp.tanh(g_xattn[0]) * _L0_xattn_ref(_layernorm(x, axis=-1), ctx_1024, L0_xattn_Wq, L0_xattn_Wk, L0_xattn_Wv, L0_xattn_Wu, L0_xattn_bu, L0_xattn_qn_w, L0_xattn_qn_b, L0_xattn_kn_w, L0_xattn_kn_b)
    x = x + jnp.tanh(g_ffn[0]) * _L0_ffn_ref(_layernorm(x, axis=-1), L0_ffn_W1, L0_ffn_b1, L0_ffn_W2, L0_ffn_b2)
    x = x + jnp.tanh(g_xattn[1]) * _L1_xattn_ref(ctx_1024, _layernorm(x, axis=-1), L1_xattn_gamma_media, L1_xattn_beta_media, L1_xattn_gamma_lat, L1_xattn_beta_lat, L1_xattn_Wq, L1_xattn_bq, L1_xattn_Wkv, L1_xattn_bkv, L1_xattn_Wo, L1_xattn_bo)
    x = x + jnp.tanh(g_ffn[1]) * _L1_ffn_ref(_layernorm(x, axis=-1), L1_ffn_gate_w, L1_ffn_fc_w, L1_ffn_proj_w)
    x = x + jnp.tanh(g_xattn[2]) * _L2_xattn_ref(_layernorm(x, axis=-1), ctx_1024, L2_xattn_Wq, L2_xattn_Wkv, L2_xattn_Wo)
    x = x + jnp.tanh(g_ffn[2]) * _L2_ffn_ref(_layernorm(x, axis=-1), L2_ffn_cn_w1, L2_ffn_cn_b1, L2_ffn_cn_w2, L2_ffn_cn_b2, L2_ffn_cn_w3, L2_ffn_cn_b3, L2_ffn_cn_w4, L2_ffn_cn_b4, L2_ffn_gc_w1, L2_ffn_gc_b1, L2_ffn_gc_w2, L2_ffn_gc_b2, L2_ffn_gc_w3, L2_ffn_gc_b3, L2_ffn_adaptive_range)
    x = x + jnp.tanh(g_xattn[3]) * _L3_xattn_ref(_layernorm(x, axis=-1), ctx_1024, ctx_1024, mask_1x1xSxS2_ik0, L3_xattn_wq_w, L3_xattn_wq_b, L3_xattn_wk_w, L3_xattn_wk_b, L3_xattn_wv_w, L3_xattn_wv_b, L3_xattn_wo_w, L3_xattn_wo_b)
    x = x + jnp.tanh(g_ffn[3]) * _L3_ffn_ref(_layernorm(x, axis=-1), L3_ffn_Wr, L3_ffn_br, L3_ffn_W1, L3_ffn_b1, L3_ffn_W2, L3_ffn_b2)
    return x

_drawn_inputs = setup_inputs


def setup_inputs(seed=0):
    import zlib

    import numpy as np

    out = dict(_drawn_inputs(seed))
    spreads = {'L0_xattn_qn_w': (1.0, 0.6),
     'L0_xattn_qn_b': (0.0, 0.8),
     'L0_xattn_kn_w': (1.0, 0.6),
     'L0_xattn_kn_b': (0.0, 2.0),
     'L1_xattn_gamma_media': (1.0, 0.6),
     'L1_xattn_beta_media': (0.0, 0.8),
     'L1_xattn_gamma_lat': (1.0, 0.6),
     'L1_xattn_beta_lat': (0.0, 0.8),
     'L1_xattn_bq': (0.0, 2.0),
     'L1_xattn_bkv': (0.0, 0.1),
     'L1_xattn_bo': (0.0, 0.1),
     'L2_ffn_cn_b1': (0.0, 0.8),
     'L2_ffn_cn_b2': (0.0, 0.8),
     'L2_ffn_cn_b3': (0.0, 2.0),
     'L2_ffn_gc_b1': (0.0, 0.8),
     'L2_ffn_gc_b2': (0.0, 0.8),
     'L3_ffn_br': (0.0, 0.497),
     'L3_ffn_b1': (0.0, 0.765),
     'L3_ffn_b2': (0.0, 0.1)}
    factors = {'g_ffn': 8.0,
     'L0_xattn_bu': 4.872,
     'L0_ffn_b1': 7.312,
     'L0_ffn_b2': 4.829,
     'L1_xattn_Wq': 8.0,
     'L2_ffn_cn_w1': 3.944,
     'L2_ffn_cn_w2': 3.419,
     'L2_ffn_cn_w3': 3.55,
     'L2_ffn_cn_w4': 2.885,
     'L2_ffn_gc_w1': 2.745,
     'L3_xattn_wk_b': 64.0,
     'L3_ffn_W1': 2.945}
    for name, (base, spread) in spreads.items():
        noise = np.random.default_rng([zlib.crc32(name.encode()), seed]).standard_normal(out[name].shape)
        drawn = base * np.exp(spread * noise) if base else spread * noise
        out[name] = jnp.asarray(drawn.astype(out[name].dtype))
    for name, factor in factors.items():
        out[name] = (out[name] * factor).astype(out[name].dtype)
    return out
```

```python
from contextlib import ExitStack

import numpy as np

import concourse.bass as bass
from concourse import mybir

B, L, D = 4, 512, 128
PAIRS, NS = 2, 2
NT = L // 128
KEYS = 77
H0, DH0 = 16, 64
H1 = 8
E, FT = 8, 4
PC = 8
EPS = 1e-5
NEG = -1e9

ALU = mybir.AluOpType
ACT = mybir.ActivationFunctionType
F32 = mybir.dt.float32
I32 = mybir.dt.int32
AX = mybir.AxisListType.X

W_FIRST = [("ident", 128), ("wk0", 1024), ("wq0", 1024), ("wv0", 1024), ("wu0", 1024), ("f0a", 512), ("f0b", 512)]
W_L1 = [("wq1", 1024), ("wk1", 1024), ("wv1", 1024), ("wo1", 1024)]
W_MOE = [("fc", 4096), ("pj", 4096)]
W_L2 = [("wq2", 128), ("wqr2", 128), ("wk2", 128), ("wkr2", 128), ("wv2", 128), ("wo2", 128),
        ("cw1", 128), ("cw2", 64), ("cw3", 32), ("cw4", 128), ("gw1", 64), ("gw2", 32), ("gw3", 128),
        ("twist", 128), ("cos", 512), ("sin", 512), ("block", 4), ("before", 64), ("gate1", 8)]
W_L3 = [("wq3", 128), ("wk3", 128), ("wv3", 128), ("wo3", 128), ("gate3", 8)]
W_GROUPS = [("first", W_FIRST), ("l1", W_L1), ("l2", W_L2), ("l3", W_L3)]
VECS = [("qw", 1), ("qb", 1), ("kw", 1), ("kb", 1), ("b1_0", 4), ("gm", 1), ("bm", 1), ("gl", 1), ("bl", 1),
        ("bq1", 8), ("bk1", 8), ("bv1", 8), ("cb1", 1), ("cb2", 1), ("cb3", 1), ("cb4", 1), ("gb1", 1),
        ("gb2", 1), ("gb3", 1), ("ar", 1), ("qb3", 1), ("kb3", 1), ("vb3", 1), ("b1_3", 32), ("g", 8)]
ROWS = [("bu", 128), ("b2_0", 128), ("bo1", 128), ("bo3", 128), ("b2_3", 128), ("br3", 8)]


def columns(parts):
    at, out = 0, {}
    for name, n in parts:
        out[name] = (at, n)
        at += n
    return out, at


class Signal:

    def __init__(self, sem, known, it, name, order=None, credit=0):
        self.sem, self.known, self.it, self.credit = sem, known.setdefault(name, {}), it, credit
        self.order = known.setdefault(order or name, {})
        self.n = 0
        self.seen = {}

    def mark(self, *event):
        self.n += 1
        assert event not in self.seen
        self.seen[event] = self.n
        return self.sem, 1

    def at(self, *event):
        return self.value(self.order.get(event, 1) + self.credit)

    def value(self, n):
        it = self.it[0]
        return (self.sem, n if isinstance(it, int) else it * self.known.get("total", 0) + n)


S0, S1, T0, T1, G0, G1 = range(6)


class Rotor:
    def __init__(self, *slots):
        self.slots, self.n = slots, 0

    def __call__(self):
        self.n += 1
        return self.slots[(self.n - 1) % len(self.slots)]


def schedule():
    big, turn, gen = Rotor(S0, S1), Rotor(T0, T1), Rotor(G0, G1)
    wide = Rotor(S0, S1, T0, T1)
    st = []

    def do(kind, *args):
        st.append((kind, args))

    def norm(l, s):
        do("norm_stats", l, s)
        if l == 2:
            do("norm_again", l, s)
        do("norm_apply", l, s)

    def norm_turn(l, s):
        do("norm_turn", l, s, gen())

    def small_attention(l, s, extra):
        units = [(hf, t) for hf in range(2) for t in range(NT)]
        slots = {}
        for k in range(len(units) + 4):
            if k < 8:
                slots[k] = big()
                do("scores", l, s, *units[k], slots[k])
                do("less_max", l, s, *units[k], slots[k], k)
                do("exp", l, s, *units[k], k)
            if 1 <= k < 9:
                do("normalise", l, s, *units[k - 1], k - 1)
            if 3 <= k < 11:
                for r in range(2):
                    do("turn_probs", l, s, *units[k - 3], k - 3, r, turn())
            if k in extra:
                for e in extra[k]:
                    do(*e)
            if k in (7, 11):
                hf = 0 if k == 7 else 1
                for j in range(4 if l == 0 else 1):
                    do("mix_values", l, s, hf, j, gen())

    def project(l, s):
        do("project", l, s, gen())

    for s in range(NS):
        norm(0, s)
    for s in range(NS):
        norm_turn(0, s)
        for h in range(2):
            do("values0", s, h, gen())
        for t in range(NT + 1):
            k = [4, 0, 1, 2, 3][t]
            slot = big()
            do("queries0", s, k, slot)
            do("head_norm", s, k, slot)
            if t:
                for h in range(2):
                    do("turn_queries", s, [4, 0, 1, 2, 3][t - 1], h, turn())
        for h in range(2):
            do("turn_queries", s, 3, h, turn())
        small_attention(0, s, {})
        project(0, s)
        norm(1, s)
    for s in range(NS):
        norm_turn(1, s)
        for f in range(FT):
            do("hidden", 1, s, 0, f, wide())
        do("ffn_out", s, gen())
        norm(2, s)
        do("media_norm", s)
    for s in range(NS):
        norm_turn(2, s)
        do("media_turn", s, gen())
        for c in range(5):
            for h in range(2):
                do("values1", s, c, h, gen())
        for h in range(2):
            do("media_keys1", s, h, gen())
        do("queries1", s, 0, gen())
        do("keys1", s, 0, gen())
        for h in range(H1 + 1):
            for t in range(NT):
                if h < H1:
                    slot = big()
                    do("scores1", s, h, t, slot)
                    do("softmax1", s, h, t, slot)
                if h:
                    for c in {0: (0, 1), 1: (2, 3), 2: (4,), 3: ()}[t]:
                        do("turn_probs1", s, h - 1, c, turn())
            if h:
                do("mix_values1", s, h - 1, gen())
            if h + 1 < H1:
                do("queries1", s, h + 1, gen())
                do("keys1", s, h + 1, gen())
        project(2, s)
        norm(3, s)

    def moe(l, s):
        norm_turn(l, s)
        do("logits", l, s, gen())
        do("gates", l, s)
        for e in range(E + 1):
            if e < E:
                for f in range(FT):
                    do("hidden", l, s, e, f, wide())
            if e == 1 and l == 7:
                do("gate_bias", s, gen())
            if e:
                do("expert_out", l, s, e - 1, gen())

    for s in range(NS):
        moe(3, s)
        norm(4, s)
    for s in range(NS):
        norm_turn(4, s)
        do("project_heads", 4, s, gen(), gen(), gen())
        small_attention(4, s, {})
        project(4, s)
        norm(5, s)
    for s in range(NS):
        norm_turn(5, s)
        do("global_net", s, gen())
    for c in range(3):
        for stage in range(5):
            for s in range(NS):
                do("cycle", s, c, stage, wide() if stage < 3 else gen())
    for s in range(NS):
        do("cycle_out", s, gen())
        norm(6, s)
    for s in range(NS):
        norm_turn(6, s)
        do("project_heads", 6, s, gen(), gen(), gen())
        small_attention(6, s, {})
        project(6, s)
        norm(7, s)
    for s in range(NS):
        moe(7, s)
        do("store", s)
    return st


def program(nc, dram, known):
    steps = schedule()
    it = [0]
    signals = {}
    with ExitStack() as ctx:
        def sb(name, shape, dt=F32):
            return ctx.enter_context(nc.sbuf_tensor(name, shape, dt))

        def signal(name, order=None, credit=0):
            signals[name] = Signal(ctx.enter_context(nc.semaphore(name)), known, it, name, order, credit)
            return signals[name]

        W = {}
        group_of = {}
        group_tiles = {}
        for gname, parts in W_GROUPS:
            cols, total = columns(parts)
            group_tiles[gname] = sb("w_" + gname, [128, total])
            for name, (a, n) in cols.items():
                W[name] = group_tiles[gname][:, a:a + n]
                group_of[name] = gname
        vcols, nv = columns(VECS)
        vec = sb("vec", [128, nv])
        rcols, nr = columns(ROWS)
        rows = sb("rows", [E, nr])

        def V(name, i=0, p=128):
            a = vcols[name][0] + i
            return vec[0:p, a:a + 1]

        def R(name, p=1):
            a, n = rcols[name]
            return rows[0:p, a:a + n]

        ident = W["ident"]
        ones = sb("ones", [1, 128])
        half_power = sb("half_power", [128, 16])
        low = sb("low", [128, 1])
        mask = sb("mask", [128, NT * KEYS], I32)
        moe = sb("moe", [128, 8192])
        centre = sb("centre", [128, 16])
        scaled = sb("scaled", [128, 16])
        gates_t = sb("gates_t", [128, 8])
        x = sb("x", [128, NS, NT, 128])
        ctxT = sb("ctxT", [128, NS * KEYS])
        ctx_rows = sb("ctx_rows", [KEYS, NS, 128])
        xn = sb("xn", [128, NS, NT, 128])
        xnT = sb("xnT", [128, NS, L])
        stat = sb("stat", [128, NS, NT, 6])
        mv = sb("mv", [128, NS, NT, 2])
        ve = sb("ve", [128, NS, 2, NT])
        rs = sb("rs", [128, NS, 3, NT])
        mstat = sb("mstat", [KEYS, NS, 6])
        mmv = sb("mmv", [KEYS, NS, 4])
        mn = sb("mn", [KEYS, NS, 128])
        mnT = sb("mnT", [128, NS, KEYS])
        hn = sb("hn", [128, 3, 16])
        arenaA = sb("arenaA", [128, 5120])
        arenaB = sb("arenaB", [128, 2, 8 * L])
        arenaC = sb("arenaC", [128, 8 * L])
        probs = sb("probs", [128, 8 * 616])
        nmax = sb("nmax", [128, 4, 8])
        rsum = sb("rsum", [128, 4, 2, 8])
        qh = sb("qh", [128, 2, L])
        kh = sb("kh", [128, 2, L])
        kmedia = sb("kmedia", [128, H1, KEYS])
        vpad = sb("vpad", [KEYS, 16, 32])
        gt = sb("gt", [128, NS, 8, NT * E])
        gl = sb("gl", [128, NS, 8])
        psum = ctx.enter_context(nc.psum_tensor("psum", [128, 8 * 512], F32))

        qT0 = arenaA[:, 0:4096].rearrange("p (m q) -> p m q", m=8)
        sq = arenaC[:, 0:1024]
        qn = arenaC[:, 1024:3072].rearrange("p (i n) -> p i n", i=2)
        rot, cur = qh, kh
        W["fc"], W["pj"] = moe[:, 0:4096], moe[:, 4096:8192]
        v0 = arenaA[0:KEYS, 4096:5120]
        kT0 = kmedia
        kbd = arenaA[:, 0:4 * KEYS].rearrange("p (j k) -> p j k", j=4)
        cmp = arenaB[:, 0, 0:3 * NT * E * E].rearrange("p (n c) -> p n c", n=3)
        gT = arenaB[0:E, 1, 0:L]
        v1 = arenaA[:, :].rearrange("p (c n) -> p c n", c=5)
        pT = [arenaB[0:KEYS, i, :].rearrange("p (r j q) -> p r j q", r=2, j=4) for i in range(2)]
        pT1 = [arenaB[:, i, 0:5 * L].rearrange("p (c q) -> p c q", c=5) for i in range(2)]
        oT = arenaC[:, :].rearrange("p (m q) -> p m q", m=8)
        hid = arenaC[:, :].rearrange("p (i f q) -> p i f q", i=2, f=FT)
        net = arenaC[:, :].rearrange("p (i q) -> p i q", i=8)
        unit_probs = [probs[:, i * 616:(i + 1) * 616] for i in range(4)]
        row_probs = [probs[:, i * 589:(i + 1) * 589] for i in range(8)]

        def slot(i, cols=None, p=128, at=0, p0=0):
            base = 1024 * i if i < 2 else 2048 + 512 * (i - 2)
            cols = cols if cols is not None else (1024 if i < 2 else 512)
            return psum[p0:p0 + p, base + at:base + at + cols]

        def scores_of(i):
            return slot(i).rearrange("p (r c) -> p r c", r=2)[:, :, 0:4 * KEYS]

        loaded = {g: signal("loaded_" + g) for g, _ in W_GROUPS}
        held_dve = signal("held_dve")
        held_pe = signal("held_pe")
        loaded_moe = signal("loaded_moe")
        loaded_small = signal("loaded_small")
        loaded_x = signal("loaded_x")
        loaded_ctx = signal("loaded_ctx")
        stored = signal("stored")
        consts_ready = signal("consts_ready")
        gates_tanh = signal("gates_tanh")
        centred = signal("centred")
        centring = signal("centring")
        centred_small = signal("centred_small")
        filled = [signal(f"filled_{i}") for i in range(6)]
        free = [signal(f"free_{i}", order=f"filled_{i}", credit=1) for i in range(6)]
        dve_step = signal("dve_step")
        act_step = signal("act_step")
        var_ready = signal("var_ready")
        rstd_ready = signal("rstd_ready")
        xn_ready = signal("xn_ready")
        xnT_ready = signal("xnT_ready")
        mvar_ready = signal("mvar_ready")
        mrstd_ready = signal("mrstd_ready")
        mn_ready = signal("mn_ready")
        mnT_ready = signal("mnT_ready")
        squares = signal("squares")
        hvar_ready = signal("hvar_ready")
        hrstd_ready = signal("hrstd_ready")
        qn_ready = signal("qn_ready")
        qT_ready = signal("qT_ready")
        v_ready = signal("v_ready")
        less_ready = signal("less_ready")
        exp_ready = signal("exp_ready")
        rsum_ready = signal("rsum_ready")
        probs_ready = signal("probs_ready")
        pT_ready = signal("pT_ready")
        oT_ready = signal("oT_ready")
        oT1_ready = signal("oT1_ready")
        probs1_ready = signal("probs1_ready")
        res_ready = signal("res_ready")
        hid_ready = signal("hid_ready")
        nmax_ready = signal("nmax_ready")
        qh_ready = signal("qh_ready")
        kh_ready = signal("kh_ready")
        km_ready = signal("km_ready")
        pT1_ready = signal("pT1_ready")
        gate_less = signal("gate_less")
        gate_exp = signal("gate_exp")
        gate_ready = signal("gate_ready")
        gT_ready = signal("gT_ready")
        heads_ready = signal("heads_ready")
        gnet_ready = signal("gnet_ready")
        gnet_scaled = signal("gnet_scaled")
        mean_ready = signal("mean_ready")
        stage_ready = signal("stage_ready")
        coup_ready = signal("coup_ready")
        cur_ready = signal("cur_ready")

        def tensor_did(*event):
            for i in range(6):
                if event in known[f"filled_{i}"]:
                    return filled[i].at(*event)
            return filled[0].at(*event)

        def turn_of(k):
            return (k + 1) % 5 % 2

        def need(eng, *names):
            for g in sorted({group_of[n] for n in names}):
                eng.wait_ge(loaded[g].sem, 16)

        NSMALL = 3
        block = ctx.enter_context(nc.Block())

        @block.sync
        def _(sp):
            sp.dma_start(vec[:], dram["vec"]).then_inc(loaded_small.sem, 16)
            sp.dma_start(rows[:], dram["rows"]).then_inc(loaded_small.sem, 16)
            sp.dma_start(mask[:], dram["mask"]).then_inc(loaded_small.sem, 16)
            sp.dma_start(group_tiles["first"][:], dram["w_first"]).then_inc(loaded["first"].sem, 16)
            with sp.Fori(0, PAIRS) as pair:
                it[0] = pair
                sp.wait_ge(stored.sem, pair * (16 * NS) + 16)
                sp.dma_start(x[:].rearrange("p s t d -> p (s t d)"),
                             dram["x"][:, bass.ds(pair * (NS * L), NS * L)]).then_inc(loaded_x.sem, 16)
                sp.dma_start(ctxT[:], dram["ctxT"][:, bass.ds(pair * (NS * KEYS), NS * KEYS)]).then_inc(loaded_ctx.sem, 16)
                sp.dma_start(ctx_rows[:].rearrange("p s d -> p (s d)"),
                             dram["ctx"][:, bass.ds(pair * (NS * 128), NS * 128)]).then_inc(loaded_ctx.sem, 16)
                sp.dma_start(moe[:], dram["w_moe1"]).then_inc(loaded_moe.sem, 16)
                sp.wait_ge(*res_ready.at("moe1"))
                sp.dma_start(moe[:], dram["w_moe3"]).then_inc(loaded_moe.sem, 16)
                for s in range(NS):
                    sp.wait_ge(*res_ready.at("done", s))
                    sp.dma_start(dram["out"][:, bass.ds(pair * (NS * L) + s * L, L)],
                                 x[:, s, :, :].rearrange("p t d -> p (t d)")).then_inc(stored.sem, 16)
            it[0] = 0
            sp.wait_ge(stored.sem, 16 * NS * PAIRS + 16)

        @block.tensor
        def _(pe):
            used = [0] * 6

            def take(i):
                used[i] += 1
                pe.wait_ge(*free[i].value(used[i]))

            def mm(out, lhsT, rhs, start=True, stop=True):
                return nc.tensor.matmul(out, lhsT, rhs, start=start, stop=stop)

            def tr(out, in_, p):
                return nc.tensor.transpose(out, in_, ident[0:p, 0:p])

            def norm_turn(l, s, i):
                pe.wait_ge(*xn_ready.at(l, s))
                take(i)
                for t in range(NT):
                    last = tr(slot(i, 128, at=128 * t), xn[:, s, t, :], 128)
                last.then_inc(*filled[i].mark("norm", l, s))

            def values0(s, h, i):
                if s == 0 and h == 0:
                    pe.wait_ge(loaded_ctx.sem, it[0] * 32 + 32)
                    need(pe, "wv0")
                take(i)
                mm(slot(i, 512, KEYS), ctxT[:, s * KEYS:(s + 1) * KEYS], W["wv0"][:, h * 512:(h + 1) * 512])\
                    .then_inc(*filled[i].mark("v0", s, h))

            def queries0(s, k, i):
                pe.wait_ge(centred.sem, 2)
                pe.wait_ge(*xnT_ready.at(0, s))
                take(i)
                lhs, p, w = (ctxT[:, s * KEYS:(s + 1) * KEYS], KEYS, "wk0") if k == 4 else \
                    (xnT[:, s, k * 128:(k + 1) * 128], 128, "wq0")
                for h in range(2):
                    last = mm(slot(i, 512, p, 512 * h), lhs, W[w][:, h * 512:(h + 1) * 512])
                last.then_inc(*filled[i].mark("q0", s, k))

            def turn_queries(s, k, h, i):
                p = KEYS if k == 4 else 128
                pe.wait_ge(*qn_ready.at(s, k))
                take(i)
                for m in range(4):
                    c = 512 * h + 128 * m
                    last = tr(slot(i, p, at=128 * m), qn[0:p, turn_of(k), c:c + 128], p)
                last.then_inc(*filled[i].mark("tq", s, k, h))

            def scores(l, s, hf, t, i):
                if l == 0:
                    pe.wait_ge(*qT_ready.at(s, 3, 1))
                else:
                    pe.wait_ge(*heads_ready.at(l, s, "q"))
                    pe.wait_ge(*heads_ready.at(l, s, "k"))
                take(i)
                if l == 0:
                    for j in range(4):
                        for r in range(2):
                            m = 4 * hf + j
                            last = mm(slot(i, KEYS, at=512 * r + KEYS * j),
                                      qT0[64 * r:64 * r + 64, m, t * 128:(t + 1) * 128],
                                      kT0[64 * r:64 * r + 64, m, :])
                else:
                    for r in range(2):
                        g = 32 * (2 * hf + r)
                        last = mm(slot(i, 4 * KEYS, at=512 * r), rot[g:g + 32, 0, t * 128:(t + 1) * 128],
                                  kbd[g:g + 32, :, :].rearrange("p j k -> p (j k)"))
                last.then_inc(*filled[i].mark("sc", l, s, hf, t))

            def turn_probs(l, s, hf, t, k, r, i):
                pe.wait_ge(*probs_ready.at(l, s, hf, t))
                take(i)
                for j in range(4):
                    c = 308 * r + KEYS * j
                    last = tr(slot(i, 128, KEYS, 128 * j), unit_probs[k % 4][:, c:c + KEYS], 128)
                last.then_inc(*filled[i].mark("tp", l, s, hf, t, r))

            def mix_values(l, s, hf, j, i):
                pe.wait_ge(*pT_ready.at(l, s, hf, 3, 1))
                if l == 0:
                    pe.wait_ge(*v_ready.at(s, 1))
                    take(i)
                    for r in range(2):
                        h = 2 * (4 * hf + j) + r
                        last = mm(slot(i, L, 64, p0=64 * r), v0[:, 64 * h:64 * h + 64], pT[hf][:, r, j, :])
                else:
                    pe.wait_ge(*heads_ready.at(l, s, "v"))
                    take(i)
                    for jj in range(4):
                        for r in range(2):
                            g = 2 * hf + r
                            last = mm(slot(i, L, 32, p0=32 * g), vpad[:, 4 * g + jj, :], pT[hf][:, r, jj, :],
                                      start=jj == 0, stop=jj == 3)
                last.then_inc(*filled[i].mark("pv", l, s, hf, j))

            def project(l, s, i):
                w, n, bias = {0: ("wu0", 8, "bu"), 2: ("wo1", 8, "bo1"), 4: ("wo2", 1, None), 6: ("wo3", 1, "bo3")}[l]
                need(pe, w)
                pe.wait_ge(*(oT1_ready.at(s) if l == 2 else oT_ready.at(l, s, "last")))
                take(i)
                for t in range(NT):
                    out = slot(i, 128, at=128 * t)
                    for m in range(n):
                        last = mm(out, oT[:, m, t * 128:(t + 1) * 128], W[w][:, m * 128:(m + 1) * 128],
                                  start=m == 0, stop=bias is None and m == n - 1)
                    if bias:
                        last = mm(out, ones[:, :], R(bias), start=False)
                last.then_inc(*filled[i].mark("proj", l, s))

            def hidden(l, s, e, f, i):
                w = {1: "f0a", 3: "fc", 7: "fc"}[l]
                if l == 1:
                    need(pe, w)
                elif e == 0 and f == 0:
                    pe.wait_ge(loaded_moe.sem, it[0] * 32 + (16 if l == 3 else 32))
                pe.wait_ge(*xnT_ready.at(l, s))
                take(i)
                c = 512 * e + 128 * f
                mm(slot(i, L), W[w][:, c:c + 128], xnT[:, s, :]).then_inc(*filled[i].mark("hid", l, s, e, f))

            def out_of(l, s, e, i, w, bias):
                pe.wait_ge(*hid_ready.at(l, s, e, FT - 1))
                take(i)
                for t in range(NT):
                    out = slot(i, 128, at=128 * t)
                    for f in range(FT):
                        c = 512 * e + 128 * f
                        last = mm(out, hid[:, (e + s) % 2, f, t * 128:(t + 1) * 128], W[w][:, c:c + 128],
                                  start=f == 0, stop=not bias and f == FT - 1)
                    if bias:
                        last = mm(out, ones[:, :], R(bias), start=False)
                last.then_inc(*filled[i].mark("out", l, s, e))

            def ffn_out(s, i):
                out_of(1, s, 0, i, "f0b", "b2_0")

            def expert_out(l, s, e, i):
                out_of(l, s, e, i, "pj", None)

            def media_turn(s, i):
                pe.wait_ge(*mn_ready.at(s))
                take(i)
                tr(slot(i, KEYS), mn[:, s, :], KEYS).then_inc(*filled[i].mark("media", s))

            def values1(s, c, h, i):
                need(pe, "wv1")
                pe.wait_ge(*xnT_ready.at(2, s))
                if c == 4:
                    pe.wait_ge(*mnT_ready.at(s))
                take(i)
                lhs, p = (mnT[:, s, :], KEYS) if c == 4 else (xnT[:, s, c * 128:(c + 1) * 128], 128)
                mm(slot(i, 512, p), lhs, W["wv1"][:, 512 * h:512 * h + 512]).then_inc(*filled[i].mark("v1", s, c, h))

            def media_keys1(s, h, i):
                take(i)
                for m in range(4):
                    c = 128 * (4 * h + m)
                    last = mm(slot(i, KEYS, at=KEYS * m), W["wk1"][:, c:c + 128], mnT[:, s, :])
                last.then_inc(*filled[i].mark("km1", s, h))

            def queries1(s, h, i):
                take(i)
                mm(slot(i, L), W["wq1"][:, 128 * h:128 * h + 128], xnT[:, s, :]).then_inc(*filled[i].mark("q1", s, h))

            def keys1(s, h, i):
                take(i)
                mm(slot(i, L), W["wk1"][:, 128 * h:128 * h + 128], xnT[:, s, :]).then_inc(*filled[i].mark("k1", s, h))

            def scores1(s, h, t, i):
                pe.wait_ge(*qh_ready.at(s, h))
                pe.wait_ge(*kh_ready.at(s, h))
                pe.wait_ge(*km_ready.at(s, 1))
                take(i)
                q = qh[:, h % 2, t * 128:(t + 1) * 128]
                mm(slot(i, L), q, kh[:, h % 2, :])
                mm(slot(i, KEYS, at=512), q, kmedia[:, h, :]).then_inc(*filled[i].mark("s1", s, h, t))

            def turn_probs1(s, h, c, i):
                pe.wait_ge(*probs1_ready.at(s, h, NT - 1))
                take(i)
                p = KEYS if c == 4 else 128
                for t in range(NT):
                    last = tr(slot(i, 128, p, 128 * t), row_probs[4 * (h % 2) + t][:, 128 * c:128 * c + p], 128)
                last.then_inc(*filled[i].mark("tp1", s, h, c))

            def mix_values1(s, h, i):
                pe.wait_ge(*v_ready.at(2, s))
                pe.wait_ge(*pT1_ready.at(s, h, 4))
                take(i)
                for c in range(5):
                    p = KEYS if c == 4 else 128
                    last = mm(slot(i, L), v1[0:p, c, 128 * h:128 * h + 128], pT1[h % 2][0:p, c, :],
                              start=c == 0, stop=c == 4)
                last.then_inc(*filled[i].mark("pv1", s, h))

            def logits(l, s, i):
                w = {3: "gate1", 7: "gate3"}[l]
                need(pe, w)
                pe.wait_ge(*xnT_ready.at(l, s))
                take(i)
                for t in range(NT):
                    last = mm(slot(i, E, at=E * t), xnT[:, s, t * 128:(t + 1) * 128], W[w], stop=l == 3)
                    if l == 7:
                        last = mm(slot(i, E, at=E * t), ones[:, :], R("br3"), start=False)
                last.then_inc(*filled[i].mark("logits", l, s))

            def gate_bias(s, i):
                pe.wait_ge(*gate_ready.at(7, s))
                take(i)
                for t in range(NT):
                    last = tr(slot(i, 128, E, 128 * t), gt[:, s, 7, E * t:E * t + E], 128)
                last.then_inc(*filled[i].mark("gT", s))
                pe.wait_ge(*gT_ready.at(s))
                take(i)
                for t in range(NT):
                    last = mm(slot(i, 128, at=128 * t), gT[:, t * 128:(t + 1) * 128], R("b2_3", E))
                last.then_inc(*filled[i].mark("gb", s))

            def project_heads(l, s, i, j, k):
                wq, wqr, wk, wkr, wv = ("wq2", "wqr2", "wk2", "wkr2", "wv2") if l == 4 else ("wq3", None, "wk3", None, "wv3")
                need(pe, wq)
                cT = ctxT[:, s * KEYS:(s + 1) * KEYS]
                pe.wait_ge(*xnT_ready.at(l, s))
                take(i)
                last = mm(slot(i, KEYS), W[wk], cT)
                if l == 4:
                    last = mm(slot(i, KEYS, at=KEYS), W[wkr], cT)
                last = mm(slot(i, 128, KEYS, at=256), cT, W[wv])
                last.then_inc(*filled[i].mark("kv", l, s))
                take(j)
                mm(slot(j, L), W[wq], xnT[:, s, :]).then_inc(*filled[j].mark("q", l, s))
                if l == 4:
                    take(k)
                    mm(slot(k, L), W[wqr], xnT[:, s, :]).then_inc(*filled[k].mark("qr", l, s))

            def global_net(s, i):
                pe.wait_ge(*mean_ready.at(s))
                take(i)
                mm(slot(i, 1, 64), W["gw1"], gl[:, s, 0:1]).then_inc(*filled[i].mark("g", s, 0))
                pe.wait_ge(*gnet_ready.at(s, 0))
                take(i)
                pe.sem_inc(held_pe.sem, 1)
                mm(slot(i, 1, 32), W["gw2"][0:64, :], gl[0:64, s, 1:2]).then_inc(*filled[i].mark("g", s, 1))
                pe.wait_ge(*gnet_ready.at(s, 1))
                take(i)
                mm(slot(i, 1), W["gw3"][0:32, :], gl[0:32, s, 2:3]).then_inc(*filled[i].mark("g", s, 2))

            def cycle(s, c, stage, i):
                src = xnT[:, s, :] if c == 0 else cur[:, s, :]
                if stage == 0 and c:
                    pe.wait_ge(*cur_ready.at(s, c - 1))
                if stage in (1, 2, 3):
                    pe.wait_ge(*stage_ready.at(s, c, stage - 1))
                take(i)
                if stage == 0:
                    last = mm(slot(i, L), W["cw1"], src)
                elif stage == 1:
                    last = mm(slot(i, L, 64), W["cw2"], net[:, 4 * s, :])
                elif stage == 2:
                    pe.sem_inc(held_pe.sem, 1)
                    last = mm(slot(i, L, 32), W["cw3"][0:64, :], net[0:64, 4 * s + 1, :])
                elif stage == 3:
                    last = mm(slot(i, L), W["cw4"][0:32, :], net[0:32, 4 * s + 2, :])
                else:
                    last = mm(slot(i, L), W["twist"], src)
                last.then_inc(*filled[i].mark("cy", s, c, stage))

            def cycle_out(s, i):
                pe.wait_ge(*cur_ready.at(s, 2))
                take(i)
                for t in range(NT):
                    last = tr(slot(i, 128, at=128 * t), cur[:, s, t * 128:(t + 1) * 128], 128)
                last.then_inc(*filled[i].mark("cyo", s))

            parts = dict(norm_turn=norm_turn, values0=values0, queries0=queries0, turn_queries=turn_queries,
                         scores=scores, turn_probs=turn_probs, mix_values=mix_values, project=project,
                         hidden=hidden, ffn_out=ffn_out, expert_out=expert_out, media_turn=media_turn,
                         values1=values1, media_keys1=media_keys1, queries1=queries1, keys1=keys1,
                         scores1=scores1, turn_probs1=turn_probs1, mix_values1=mix_values1, logits=logits,
                         gate_bias=gate_bias, project_heads=project_heads, global_net=global_net,
                         cycle=cycle, cycle_out=cycle_out)
            need(pe, "ident")
            pe.wait_ge(consts_ready.sem, 6)
            pe.wait_ge(loaded_small.sem, 16 * NSMALL)
            with pe.Fori(0, PAIRS) as pair:
                it[0] = pair
                for kind, args in steps:
                    if kind in parts:
                        parts[kind](*args)
            it[0] = 0

        @block.scalar
        def _(act):
            def f(out, in_, func, **kw):
                return nc.scalar.activation(out, in_, func, **kw)

            def norm_turn(l, s, i):
                act.wait_ge(*filled[i].at("norm", l, s))
                if l == 2:
                    last = f(xnT[:, s, :], slot(i, L), ACT.Identity, scale=V("gl"), bias=V("bl"))
                else:
                    last = f(xnT[:, s, :], slot(i, L), ACT.Copy)
                last.then_inc(*free[i].mark("norm", l, s))
                act.wait_ge(*free[i].at("norm", l, s))
                act.sem_inc(*xnT_ready.mark(l, s))

            def head_norm(s, k, i):
                p = KEYS if k == 4 else 128
                act.wait_ge(*filled[i].at("q0", s, k))
                if prev_sq[0] is not None:
                    act.wait_ge(*hvar_ready.at(*prev_sq[0]))
                prev_sq[0] = (s, k)
                f(sq[0:p, :], slot(i, 1024, p), ACT.Square).then_inc(*squares.mark(s, k))

            prev_sq = [None]

            def turn_queries(s, k, h, i):
                p = KEYS if k == 4 else 128
                act.wait_ge(*filled[i].at("tq", s, k, h))
                src = slot(i).rearrange("p (m c) -> p m c", m=4)[:, :, 0:p] if k < 4 else \
                    slot(i)[:, :].rearrange("p (m c) -> p m c", m=4)[:, :, 0:KEYS]
                if k == 4:
                    last = f(kT0[:, 4 * h:4 * h + 4, :], src, ACT.Identity, scale=V("kw"), bias=V("kb"))
                else:
                    last = f(qT0[:, 4 * h:4 * h + 4, k * 128:(k + 1) * 128], src, ACT.Identity,
                             scale=scaled[:, 0:1], bias=scaled[:, 1:2])
                last.then_inc(*free[i].mark("tq", s, k, h))
                if k == 3 and h == 1:
                    act.wait_ge(*free[i].at("tq", s, k, h))
                    act.sem_inc(*qT_ready.mark(s, 3, 1))

            def exp(l, s, hf, t, k):
                act.wait_ge(*less_ready.at(l, s, hf, t))
                f(unit_probs[k % 4], unit_probs[k % 4], ACT.Exp).then_inc(*exp_ready.mark(l, s, hf, t))

            def turn_probs(l, s, hf, t, k, r, i):
                act.wait_ge(*filled[i].at("tp", l, s, hf, t, r))
                f(pT[hf][:, r, :, t * 128:(t + 1) * 128], slot(i, 512, KEYS).rearrange("p (j q) -> p j q", j=4),
                  ACT.Copy).then_inc(*free[i].mark("tp", l, s, hf, t, r))
                if t == 3 and r == 1:
                    act.wait_ge(*free[i].at("tp", l, s, hf, t, r))
                    act.sem_inc(*pT_ready.mark(l, s, hf, t, r))

            def mix_values(l, s, hf, j, i):
                act.wait_ge(*filled[i].at("pv", l, s, hf, j))
                if l == 0:
                    last = f(oT[:, 4 * hf + j, :], slot(i, L), ACT.Copy)
                elif l == 4:
                    last = f(oT[64 * hf:64 * hf + 64, 0, :], slot(i, L, 64, p0=64 * hf), ACT.Copy)
                else:
                    a = vcols["vb3"][0]
                    last = f(oT[64 * hf:64 * hf + 64, 0, :], slot(i, L, 64, p0=64 * hf), ACT.Identity,
                             bias=vec[64 * hf:64 * hf + 64, a:a + 1])
                last.then_inc(*free[i].mark("pv", l, s, hf, j))
                if hf == 1 and j == (3 if l == 0 else 0):
                    act.wait_ge(*free[i].at("pv", l, s, hf, j))
                    act.sem_inc(*oT_ready.mark(l, s, "last"))

            def hidden(l, s, e, fi, i):
                act.wait_ge(*filled[i].at("hid", l, s, e, fi))
                kw = {1: dict(func=ACT.Relu, bias=V("b1_0", fi)), 3: dict(func=ACT.Gelu),
                      7: dict(func=ACT.Relu, bias=V("b1_3", 4 * e + fi))}[l]
                func = kw.pop("func")
                f(hid[:, (e + s) % 2, fi, :], slot(i, L), func, **kw).then_inc(*free[i].mark("hid", l, s, e, fi))
                if fi == FT - 1:
                    act.wait_ge(*free[i].at("hid", l, s, e, fi))
                    act.sem_inc(*hid_ready.mark(l, s, e, fi))

            def media_turn(s, i):
                act.wait_ge(*filled[i].at("media", s))
                f(mnT[:, s, :], slot(i, KEYS), ACT.Identity, scale=V("gm"), bias=V("bm"))\
                    .then_inc(*free[i].mark("media", s))
                act.wait_ge(*free[i].at("media", s))
                act.sem_inc(*mnT_ready.mark(s))

            def values1(s, c, h, i):
                if h == 1:
                    return
                p = KEYS if c == 4 else 128
                act.wait_ge(*filled[i].at("v1", s, c, h))
                f(v1[0:p, c, 512 * h:512 * h + 512], slot(i, 512, p), ACT.Copy).then_inc(*free[i].mark("v1", s, c, h))

            def media_keys1(s, h, i):
                act.wait_ge(*filled[i].at("km1", s, h))
                for m in range(4):
                    last = f(kmedia[:, 4 * h + m, :], slot(i, KEYS, at=KEYS * m), ACT.Identity,
                             bias=V("bk1", 4 * h + m))
                last.then_inc(*free[i].mark("km1", s, h))
                if h == 1:
                    act.wait_ge(*free[i].at("km1", s, h))
                    act.sem_inc(*km_ready.mark(s, 1))

            def queries1(s, h, i):
                act.wait_ge(*filled[i].at("q1", s, h))
                f(qh[:, h % 2, :], slot(i, L), ACT.Identity, scale=float(128 ** -0.5), bias=scaled[:, 2 + h:3 + h])\
                    .then_inc(*free[i].mark("q1", s, h))
                act.wait_ge(*free[i].at("q1", s, h))
                act.sem_inc(*qh_ready.mark(s, h))

            def softmax1(s, h, t, i):
                k = 4 * (h % 2) + t
                act.wait_ge(*nmax_ready.at(s, h, t))
                if h >= 2:
                    act.wait_ge(*tensor_did("tp1", s, h - 2, 4))
                f(row_probs[k], slot(i, 589), ACT.Exp, bias=nmax[:, t, 0:1], accum_out=rsum[:, t, 0, 0:1])\
                    .then_inc(*free[i].mark("s1", s, h, t))
                act.wait_ge(*free[i].at("s1", s, h, t))
                act.sem_inc(*exp_ready.mark(2, s, h, t))

            def turn_probs1(s, h, c, i):
                if c % 2:
                    return
                p = KEYS if c == 4 else 128
                act.wait_ge(*filled[i].at("tp1", s, h, c))
                f(pT1[h % 2][0:p, c, :], slot(i, 512, p), ACT.Copy).then_inc(*free[i].mark("tp1", s, h, c))
                if c == 4:
                    act.wait_ge(*free[i].at("tp1", s, h, c))
                    act.wait_ge(*dve_step.at("tp1", s, h, 3))
                    act.sem_inc(*pT1_ready.mark(s, h, 4))

            def gates(l, s):
                act.wait_ge(*gate_less.at(l, s))
                f(gt[:, s, 1, :], gt[:, s, 0, :], ACT.Exp).then_inc(*gate_exp.mark(l, s))

            def global_net(s, i):
                for n, (p, b) in enumerate(((64, "gb1"), (32, "gb2"))):
                    act.wait_ge(*filled[i].at("g", s, n))
                    f(gl[0:p, s, n + 1:n + 2], slot(i, 1, p), ACT.Gelu, bias=V(b, p=p))\
                        .then_inc(*free[i].mark("g", s, n))
                    act.wait_ge(*free[i].at("g", s, n))
                    act.sem_inc(*gnet_ready.mark(s, n))
                act.wait_ge(*filled[i].at("g", s, 2))
                f(gl[:, s, 3:4], slot(i, 1), ACT.Tanh, scale=0.5, bias=scaled[:, 11:12])\
                    .then_inc(*free[i].mark("g", s, 2))
                act.wait_ge(*free[i].at("g", s, 2))
                act.sem_inc(*gnet_ready.mark(s, 2))

            def cycle(s, c, stage, i):
                if stage == 4:
                    return
                act.wait_ge(*filled[i].at("cy", s, c, stage))
                if stage == 3 and c:
                    act.wait_ge(*coup_ready.at(s, c - 1))
                p, b = ((128, "cb1"), (64, "cb2"), (32, "cb3"), (128, None))[stage]
                if stage < 3:
                    last = f(net[0:p, 4 * s + stage, :], slot(i, L, p), ACT.Gelu, bias=V(b, p=p))
                else:
                    last = f(net[:, 4 * s + 3, :], slot(i, L), ACT.Tanh, scale=0.5, bias=scaled[:, 10:11])
                last.then_inc(*free[i].mark("cy", s, c, stage))
                act.wait_ge(*free[i].at("cy", s, c, stage))
                act.sem_inc(*stage_ready.mark(s, c, stage))

            parts = dict(norm_turn=norm_turn, head_norm=head_norm, turn_queries=turn_queries, exp=exp,
                         turn_probs=turn_probs, mix_values=mix_values, hidden=hidden, media_turn=media_turn,
                         values1=values1, media_keys1=media_keys1, queries1=queries1, softmax1=softmax1,
                         turn_probs1=turn_probs1, gates=gates, global_net=global_net, cycle=cycle)
            for g in ("l1", "l2", "l3"):
                act.dma_start(group_tiles[g][:], dram["w_" + g]).then_inc(loaded[g].sem, 16)
            act.wait_ge(loaded_small.sem, 16 * NSMALL)
            a = vcols["g"][0]
            f(gates_t[:, :], vec[:, a:a + 8], ACT.Tanh).then_inc(gates_tanh.sem, 1)
            act.wait_ge(consts_ready.sem, 6)
            with act.Fori(0, PAIRS) as pair:
                it[0] = pair
                for kind, args in steps:
                    if kind in parts:
                        parts[kind](*args)
            it[0] = 0

        @block.gpsimd
        def _(pool):
            def norm_stats(l, s, again=False):
                pool.wait_ge(*var_ready.at(l, s, again))
                nc.gpsimd.tensor_tensor(rs[:, s, int(again), :], ve[:, s, int(again), :], half_power[:, 0:NT], ALU.pow)\
                    .then_inc(*rstd_ready.mark(l, s, again))

            def norm_again(l, s):
                norm_stats(l, s, True)

            def media_norm(s):
                pool.wait_ge(*mvar_ready.at(s))
                nc.gpsimd.tensor_tensor(mmv[:, s, 3:4], mmv[:, s, 2:3], half_power[0:KEYS, 0:1], ALU.pow)\
                    .then_inc(*mrstd_ready.mark(s))

            def head_norm(s, k, i):
                p = KEYS if k == 4 else 128
                pool.wait_ge(*hvar_ready.at(s, k))
                nc.gpsimd.tensor_tensor(hn[0:p, 2, :], hn[0:p, 1, :], half_power[0:p, 0:16], ALU.pow)\
                    .then_inc(*hrstd_ready.mark(s, k))

            def normalise(l, s, hf, t, k):
                pool.wait_ge(*rsum_ready.at(l, s, hf, t))
                pr = unit_probs[k % 4].rearrange("p (h k) -> p h k", h=8)
                nc.gpsimd.tensor_tensor(pr, pr, rsum[:, k % 4, 1, :].unsqueeze(2).broadcast_to([128, 8, KEYS]), ALU.mult)\
                    .then_inc(*probs_ready.mark(l, s, hf, t))

            parts = dict(norm_stats=norm_stats, norm_again=norm_again, media_norm=media_norm, head_norm=head_norm,
                         normalise=normalise)
            pool.memset(half_power[:], -0.5).then_inc(consts_ready.sem, 1)
            pool.wait_ge(consts_ready.sem, 6)
            with pool.Fori(0, PAIRS) as pair:
                it[0] = pair
                for kind, args in steps:
                    if kind in parts:
                        parts[kind](*args)
            it[0] = 0

        @block.vector
        def _(dve):
            auto = [0]

            def link(ins):
                auto[0] += 1
                ins.then_inc(*dve_step.mark("link", auto[0]))
                dve.wait_ge(*dve_step.at("link", auto[0]))

            v = nc.vector

            def norm_stats(l, s):
                if l == 0 and s == 0:
                    dve.wait_ge(loaded_x.sem, it[0] * 16 + 16)
                for t in range(NT):
                    last = v.bn_stats(stat[:, s, t, :], x[:, s, t, :])
                link(last)
                dve.sem_inc(held_dve.sem, 1)
                for t in range(NT):
                    last = v.bn_aggr(mv[:, s, t, :], stat[:, s, t, :])
                link(last)
                v.tensor_scalar(ve[:, s, 0, :], mv[:, s, :, 1], EPS, None, ALU.add)\
                    .then_inc(*var_ready.mark(l, s, False))

            def norm_again(l, s):
                dve.wait_ge(*rstd_ready.at(l, s, False))
                link(v.tensor_tensor(rs[:, s, 2, :], rs[:, s, 0, :], rs[:, s, 0, :], ALU.mult))
                link(v.tensor_tensor(rs[:, s, 2, :], rs[:, s, 2, :], mv[:, s, :, 1], ALU.mult))
                v.tensor_scalar(ve[:, s, 1, :], rs[:, s, 2, :], EPS, None, ALU.add)\
                    .then_inc(*var_ready.mark(l, s, True))

            def norm_apply(l, s):
                r = 0
                dve.wait_ge(*rstd_ready.at(l, s, l == 2))
                if l == 2:
                    link(v.tensor_tensor(rs[:, s, 2, :], rs[:, s, 0, :], rs[:, s, 1, :], ALU.mult))
                    r = 2
                for t in range(NT):
                    last = v.tensor_scalar(xn[:, s, t, :], x[:, s, t, :], mv[:, s, t, 0:1], rs[:, s, r, t:t + 1],
                                           ALU.subtract, ALU.mult)
                last.then_inc(*xn_ready.mark(l, s))

            def media_norm(s):
                if s == 0:
                    dve.wait_ge(loaded_ctx.sem, it[0] * 32 + 32)
                link(v.bn_stats(mstat[:, s, :], ctx_rows[:, s, :]))
                dve.sem_inc(held_dve.sem, 1)
                link(v.bn_aggr(mmv[:, s, 0:2], mstat[:, s, :]))
                v.tensor_scalar(mmv[:, s, 2:3], mmv[:, s, 1:2], EPS, None, ALU.add).then_inc(*mvar_ready.mark(s))
                dve.wait_ge(*mrstd_ready.at(s))
                v.tensor_scalar(mn[:, s, :], ctx_rows[:, s, :], mmv[:, s, 0:1], mmv[:, s, 3:4],
                                ALU.subtract, ALU.mult).then_inc(*mn_ready.mark(s))

            def values0(s, h, i):
                dve.wait_ge(*filled[i].at("v0", s, h))
                v.tensor_copy(v0[:, 512 * h:512 * h + 512], slot(i, 512, KEYS)).then_inc(*free[i].mark("v0", s, h))
                if h == 1:
                    dve.wait_ge(*free[i].at("v0", s, h))
                    dve.sem_inc(*v_ready.mark(s, 1))

            def head_norm(s, k, i):
                p = KEYS if k == 4 else 128
                dve.wait_ge(*squares.at(s, k))
                link(v.tensor_reduce(hn[0:p, 0, :], sq[0:p, :].rearrange("p (h d) -> p h d", h=16), AX, ALU.add))
                v.tensor_scalar(hn[0:p, 1, :], hn[0:p, 0, :], 1.0 / DH0, EPS, ALU.mult, ALU.add)\
                    .then_inc(*hvar_ready.mark(s, k))
                dve.wait_ge(*hrstd_ready.at(s, k))
                if k in (1, 2, 3):
                    dve.wait_ge(*tensor_did("tq", s, 4 if k == 1 else k - 2, 1))
                v.tensor_tensor(qn[0:p, turn_of(k), :].rearrange("p (h d) -> p h d", h=16),
                                slot(i, 1024, p).rearrange("p (h d) -> p h d", h=16),
                                hn[0:p, 2, :].unsqueeze(2).broadcast_to([p, 16, DH0]), ALU.mult)\
                    .then_inc(*free[i].mark("q0", s, k))
                dve.wait_ge(*free[i].at("q0", s, k))
                dve.sem_inc(*qn_ready.mark(s, k))

            def less_max(l, s, hf, t, i, k):
                dve.wait_ge(*filled[i].at("sc", l, s, hf, t))
                sc = scores_of(i).rearrange("p r (j k) -> p r j k", j=4)
                if l == 6:
                    m = mask[:, t * KEYS:(t + 1) * KEYS]
                    dve.sem_inc(held_dve.sem, 1)
                    for r in range(2):
                        last = v.copy_predicated(
                            sc[:, r, :, :], m.unsqueeze(1).broadcast_to([128, 4, KEYS]),
                            low[:, 0:1].unsqueeze(2).broadcast_to([128, 4, KEYS]))
                    link(last)
                link(v.tensor_reduce(nmax[:, k % 4, :], sc, AX, ALU.max, negate=True))
                nm = nmax[:, k % 4, :].rearrange("p (r j) -> p r j", r=2).unsqueeze(3).broadcast_to([128, 2, 4, KEYS])
                v.tensor_tensor(unit_probs[k % 4].rearrange("p (r j k) -> p r j k", r=2, j=4), sc, nm, ALU.add)\
                    .then_inc(*free[i].mark("sc", l, s, hf, t))
                dve.wait_ge(*free[i].at("sc", l, s, hf, t))
                dve.sem_inc(*less_ready.mark(l, s, hf, t))

            def normalise(l, s, hf, t, k):
                dve.wait_ge(*exp_ready.at(l, s, hf, t))
                link(v.tensor_reduce(rsum[:, k % 4, 0, :], unit_probs[k % 4].rearrange("p (h k) -> p h k", h=8),
                                     AX, ALU.add))
                v.reciprocal(rsum[:, k % 4, 1, :], rsum[:, k % 4, 0, :]).then_inc(*rsum_ready.mark(l, s, hf, t))

            def add_to_x(l, s, i, label):
                dve.wait_ge(*filled[i].at(*label))
                xs = x[:, s, :, :].rearrange("p t d -> p (t d)")
                v.scalar_tensor_tensor(xs, slot(i, L), gates_t[:, l:l + 1], xs, ALU.mult, ALU.add)\
                    .then_inc(*free[i].mark(*label))
                dve.wait_ge(*free[i].at(*label))

            def project(l, s, i):
                add_to_x(l, s, i, ("proj", l, s))

            def ffn_out(s, i):
                add_to_x(1, s, i, ("out", 1, s, 0))

            def cycle_out(s, i):
                add_to_x(5, s, i, ("cyo", s))

            def expert_out(l, s, e, i):
                dve.wait_ge(*filled[i].at("out", l, s, e))
                for t in range(NT):
                    last = v.scalar_tensor_tensor(x[:, s, t, :], slot(i, 128, at=128 * t),
                                                  gt[:, s, 7, E * t + e:E * t + e + 1], x[:, s, t, :],
                                                  ALU.mult, ALU.add)
                last.then_inc(*free[i].mark("out", l, s, e))
                dve.wait_ge(*free[i].at("out", l, s, e))
                if l == 3 and s == 1 and e == E - 1:
                    dve.sem_inc(*res_ready.mark("moe1"))
                if l == 7 and e == E - 1:
                    dve.sem_inc(*res_ready.mark("done", s))

            def values1(s, c, h, i):
                if h == 0:
                    return
                p = KEYS if c == 4 else 128
                dve.wait_ge(*filled[i].at("v1", s, c, h))
                v.tensor_copy(v1[0:p, c, 512 * h:512 * h + 512], slot(i, 512, p)).then_inc(*free[i].mark("v1", s, c, h))
                if c == 4:
                    dve.wait_ge(*free[i].at("v1", s, c, h))
                    dve.wait_ge(*free[G0 + G1 - i].at("v1", s, c, 0))
                    dve.sem_inc(*v_ready.mark(2, s))

            def keys1(s, h, i):
                dve.wait_ge(*filled[i].at("k1", s, h))
                v.tensor_scalar(kh[:, h % 2, :], slot(i, L), V("bk1", h), None, ALU.add).then_inc(*free[i].mark("k1", s, h))
                dve.wait_ge(*free[i].at("k1", s, h))
                dve.sem_inc(*kh_ready.mark(s, h))

            def softmax1(s, h, t, i):
                k = 4 * (h % 2) + t
                dve.wait_ge(*filled[i].at("s1", s, h, t))
                v.tensor_reduce(nmax[:, t, 0:1], slot(i, 589), AX, ALU.max, negate=True).then_inc(*nmax_ready.mark(s, h, t))
                if t or h:
                    scale_row(s, *((h, t - 1) if t else (h - 1, 3)))

            def scale_row(s, h, t):
                k = 4 * (h % 2) + t
                dve.wait_ge(*exp_ready.at(2, s, h, t))
                link(v.reciprocal(rsum[:, t, 1, 0:1], rsum[:, t, 0, 0:1]))
                v.tensor_scalar(row_probs[k], row_probs[k], rsum[:, t, 1, 0:1], None, ALU.mult)\
                    .then_inc(*probs1_ready.mark(s, h, t))

            def turn_probs1(s, h, c, i):
                if h == H1 - 1 and c == 0:
                    scale_row(s, H1 - 1, 3)
                if c % 2 == 0:
                    return
                dve.wait_ge(*filled[i].at("tp1", s, h, c))
                v.tensor_copy(pT1[h % 2][:, c, :], slot(i, 512)).then_inc(*free[i].mark("tp1", s, h, c))
                if c == 3:
                    dve.wait_ge(*free[i].at("tp1", s, h, c))
                    dve.sem_inc(*dve_step.mark("tp1", s, h, c))

            def mix_values1(s, h, i):
                dve.wait_ge(*filled[i].at("pv1", s, h))
                v.tensor_scalar(oT[:, h, :], slot(i, L), V("bv1", h), None, ALU.add).then_inc(*free[i].mark("pv1", s, h))
                if h == H1 - 1:
                    dve.wait_ge(*free[i].at("pv1", s, h))
                    dve.sem_inc(*oT1_ready.mark(s))

            def logits(l, s, i):
                dve.wait_ge(*filled[i].at("logits", l, s))
                lg = slot(i, NT * E).rearrange("p (t e) -> p t e", t=NT)
                mx = gt[:, s, 2, 0:NT]
                link(v.tensor_reduce(mx, lg, AX, ALU.max, negate=True))
                v.tensor_tensor(gt[:, s, 0, :].rearrange("p (t e) -> p t e", t=NT), lg,
                                mx.unsqueeze(2).broadcast_to([128, NT, E]), ALU.add).then_inc(*free[i].mark("logits", l, s))
                dve.wait_ge(*free[i].at("logits", l, s))
                dve.sem_inc(*gate_less.mark(l, s))

            def gates(l, s):
                te = "p (t e) -> p t e"
                p3 = gt[:, s, 3, :].rearrange(te, t=NT)
                by_j = gt[:, s, 3, :].rearrange(te, t=NT).unsqueeze(2).broadcast_to([128, NT, E, E])
                by_e = gt[:, s, 3, :].rearrange(te, t=NT).unsqueeze(3).broadcast_to([128, NT, E, E])
                c = [cmp[:, n, :].rearrange("p (t e j) -> p t e j", t=NT, e=E) for n in range(3)]
                rank = gt[:, s, 4, :].rearrange(te, t=NT)
                tmp = gt[:, s, 5, :].rearrange(te, t=NT)
                out = gt[:, s, 7, :].rearrange(te, t=NT)
                one = gt[:, s, 2, 0:NT]
                need(dve, "before")
                dve.wait_ge(*gate_exp.at(l, s))
                link(v.tensor_reduce(one, gt[:, s, 1, :].rearrange(te, t=NT), AX, ALU.add))
                link(v.reciprocal(gt[:, s, 2, NT:2 * NT], one))
                link(v.tensor_tensor(p3, gt[:, s, 1, :].rearrange(te, t=NT),
                                     gt[:, s, 2, NT:2 * NT].unsqueeze(2).broadcast_to([128, NT, E]), ALU.mult))
                v.tensor_tensor(c[0], by_j, by_e, ALU.is_gt)
                link(v.tensor_tensor(c[1], by_j, by_e, ALU.is_equal))
                tri = W["before"].rearrange("p (e j) -> p e j", e=E).unsqueeze(1).broadcast_to([128, NT, E, E])
                link(v.tensor_tensor(c[1], c[1], tri, ALU.mult))
                link(v.tensor_tensor(c[0], c[0], c[1], ALU.add))
                link(v.tensor_reduce(rank, c[0], AX, ALU.add))
                if l == 3:
                    link(v.scalar_tensor_tensor(tmp, rank, 2.0, p3, ALU.is_lt, ALU.mult))
                    link(v.tensor_reduce(one, tmp, AX, ALU.add))
                    link(v.reciprocal(gt[:, s, 2, NT:2 * NT], one))
                    link(v.scalar_tensor_tensor(out, tmp, gates_t[:, l:l + 1],
                                                gt[:, s, 2, NT:2 * NT].unsqueeze(2).broadcast_to([128, NT, E]),
                                                ALU.mult, ALU.mult))
                else:
                    link(v.tensor_tensor(c[2], c[0], by_j, ALU.mult))
                    link(v.tensor_reduce(tmp, c[2], AX, ALU.add))
                    link(v.tensor_tensor(tmp, tmp, p3, ALU.add))
                    link(v.tensor_scalar(tmp, tmp, 0.8, None, ALU.is_lt))
                    link(v.tensor_scalar(rank, rank, 1.0, None, ALU.is_lt))
                    link(v.tensor_tensor(tmp, tmp, rank, ALU.max))
                    v.scalar_tensor_tensor(out, tmp, gates_t[:, l:l + 1], p3, ALU.mult, ALU.mult)\
                        .then_inc(*gate_ready.mark(l, s))
                    dve.wait_ge(*gate_ready.at(l, s))

            def gate_bias(s, i):
                dve.wait_ge(*filled[i].at("gT", s))
                v.tensor_copy(gT[:, :], slot(i, 512, E)).then_inc(*free[i].mark("gT", s))
                dve.wait_ge(*free[i].at("gT", s))
                dve.sem_inc(*gT_ready.mark(s))
                dve.wait_ge(*filled[i].at("gb", s))
                xs = x[:, s, :, :].rearrange("p t d -> p (t d)")
                v.tensor_tensor(xs, slot(i, L), xs, ALU.add).then_inc(*free[i].mark("gb", s))
                dve.wait_ge(*free[i].at("gb", s))

            def project_heads(l, s, i, j, k):
                kb = kbd[:, :, :]
                blk = W["block"].unsqueeze(2).broadcast_to([128, 4, KEYS])
                dve.wait_ge(*filled[i].at("kv", l, s))
                kk = rot[:, 1, 0:KEYS]
                if l == 4:
                    v.tensor_tensor(kk, slot(i, KEYS), W["cos"][:, 0:KEYS], ALU.mult)
                    link(v.tensor_tensor(rot[:, 1, 128:128 + KEYS], slot(i, KEYS, at=KEYS), W["sin"][:, 0:KEYS], ALU.mult))
                    link(v.tensor_tensor(kk, kk, rot[:, 1, 128:128 + KEYS], ALU.add))
                else:
                    link(v.tensor_scalar(kk, slot(i, KEYS), V("kb3"), None, ALU.add))
                v.tensor_tensor(kb, kk.unsqueeze(1).broadcast_to([128, 4, KEYS]), blk, ALU.mult)\
                    .then_inc(*heads_ready.mark(l, s, "k"))
                for a in range(4):
                    last = v.tensor_copy(vpad[:, :, :].rearrange("p (g j) c -> p g j c", g=4)[:, :, a, 8 * a:8 * a + 8],
                                         slot(i, 128, KEYS, at=256).rearrange("p (g c) -> p g c", g=4)[:, :, 8 * a:8 * a + 8])
                last.then_inc(*free[i].mark("kv", l, s))
                dve.wait_ge(*free[i].at("kv", l, s))
                dve.sem_inc(*heads_ready.mark(l, s, "v"))
                dve.wait_ge(*filled[j].at("q", l, s))
                if l == 4:
                    v.tensor_tensor(rot[:, 0, :], slot(j, L), W["cos"], ALU.mult).then_inc(*free[j].mark("q", l, s))
                    dve.wait_ge(*filled[k].at("qr", l, s))
                    dve.wait_ge(*free[j].at("q", l, s))
                    v.tensor_tensor(rot[:, 1, :], slot(k, L), W["sin"], ALU.mult).then_inc(*free[k].mark("qr", l, s))
                    dve.wait_ge(*free[k].at("qr", l, s))
                    link(v.tensor_tensor(rot[:, 0, :], rot[:, 0, :], rot[:, 1, :], ALU.add))
                else:
                    v.tensor_scalar(rot[:, 0, :], slot(j, L), V("qb3"), float(8 ** -0.5), ALU.add, ALU.mult)\
                        .then_inc(*free[j].mark("q", l, s))
                    dve.wait_ge(*free[j].at("q", l, s))
                dve.sem_inc(*heads_ready.mark(l, s, "q"))

            def global_net(s, i):
                dve.wait_ge(*xnT_ready.at(5, s))
                link(v.tensor_reduce(gl[:, s, 4:5], xnT[:, s, :], AX, ALU.add))
                v.tensor_scalar(gl[:, s, 0:1], gl[:, s, 4:5], 1.0 / L, None, ALU.mult).then_inc(*mean_ready.mark(s))
                dve.wait_ge(*gnet_ready.at(s, 2))
                link(v.tensor_scalar(gl[:, s, 5:6], gl[:, s, 3:4], scaled[:, 12:13], 0.1, ALU.mult, ALU.add))

            def cycle(s, c, stage, i):
                if stage != 4:
                    return
                src = xnT[:, s, :] if c == 0 else cur[:, s, :]
                th = net[:, 4 * s + 3, :]
                dve.wait_ge(*stage_ready.at(s, c, 3))
                link(v.tensor_scalar(th, th, scaled[:, 13:14], gl[:, s, 5:6], ALU.mult, ALU.add))
                dve.wait_ge(*filled[i].at("cy", s, c, 4))
                v.tensor_tensor(th, slot(i, L), th, ALU.mult).then_inc(*free[i].mark("cy", s, c, 4))
                dve.wait_ge(*free[i].at("cy", s, c, 4))
                v.tensor_tensor(cur[:, s, :], src, th, ALU.add).then_inc(*coup_ready.mark(s, c))
                dve.wait_ge(*coup_ready.at(s, c))
                dve.sem_inc(*cur_ready.mark(s, c))

            parts = dict(norm_stats=norm_stats, norm_again=norm_again, norm_apply=norm_apply, media_norm=media_norm,
                         values0=values0, head_norm=head_norm, less_max=less_max, normalise=normalise,
                         project=project, ffn_out=ffn_out, cycle_out=cycle_out, expert_out=expert_out,
                         values1=values1, keys1=keys1, softmax1=softmax1, turn_probs1=turn_probs1,
                         mix_values1=mix_values1, logits=logits, gates=gates, gate_bias=gate_bias,
                         project_heads=project_heads, global_net=global_net, cycle=cycle)

            for i in range(6):
                dve.sem_inc(free[i].sem, 1)
            dve.sem_inc(stored.sem, 16)
            v.memset(ones[:], 1.0).then_inc(consts_ready.sem, 1)
            v.memset(low[:], NEG).then_inc(consts_ready.sem, 1)
            v.memset(vpad[:], 0.0).then_inc(consts_ready.sem, 1)
            dve.wait_ge(loaded_small.sem, 16 * NSMALL)
            v.tensor_scalar(mask[:], mask[:], 0, None, ALU.is_equal).then_inc(consts_ready.sem, 1)
            a = vcols["qw"][0]
            v.tensor_scalar(scaled[:, 0:2], vec[:, a:a + 2], 0.125, None, ALU.mult).then_inc(centred_small.sem, 1)
            a = vcols["bq1"][0]
            v.tensor_scalar(scaled[:, 2:10], vec[:, a:a + 8], float(128 ** -0.5), None, ALU.mult).then_inc(centred_small.sem, 1)
            v.tensor_scalar(scaled[:, 10:11], V("cb4"), 0.5, None, ALU.mult).then_inc(centred_small.sem, 1)
            v.tensor_scalar(scaled[:, 11:12], V("gb3"), 0.5, None, ALU.mult).then_inc(centred_small.sem, 1)
            v.tensor_scalar(scaled[:, 12:13], V("ar"), 0.7, None, ALU.mult).then_inc(centred_small.sem, 1)
            v.tensor_scalar(scaled[:, 13:14], V("ar"), 0.3, None, ALU.mult).then_inc(centred_small.sem, 1)
            dve.wait_ge(centred_small.sem, 6)
            dve.sem_inc(consts_ready.sem, 1)
            need(dve, "wq0")
            for n, w in enumerate(("wk0", "wq0")):
                w3 = W[w].rearrange("p (h d) -> p h d", h=16)
                v.tensor_reduce(centre[:], w3, AX, ALU.add).then_inc(centring.sem, 1)
                dve.wait_ge(centring.sem, 3 * n + 1)
                v.tensor_scalar(centre[:], centre[:], -1.0 / DH0, None, ALU.mult).then_inc(centring.sem, 1)
                dve.wait_ge(centring.sem, 3 * n + 2)
                v.tensor_tensor(w3, w3, centre[:].unsqueeze(2).broadcast_to([128, 16, DH0]), ALU.add)\
                    .then_inc(centring.sem, 1)
                dve.wait_ge(centring.sem, 3 * n + 3)
                dve.sem_inc(centred.sem, 1)
            dve.wait_ge(gates_tanh.sem, 1)
            dve.wait_ge(consts_ready.sem, 6)
            with dve.Fori(0, PAIRS) as pair:
                it[0] = pair
                for kind, args in steps:
                    if kind in parts:
                        parts[kind](*args)
            it[0] = 0
    for name, sg in signals.items():
        known[name].update(sg.seen)
        known[name]["total"] = sg.n
    for i in range(6):
        assert signals[f"filled_{i}"].seen.keys() == signals[f"free_{i}"].seen.keys()


def kernel(**inputs):
    import numpy as _np
    import concourse.bacc as _bacc
    from concourse.bass_utils import run_bass_kernel_spmd as _run

    a = {k: _np.asarray(v) for k, v in inputs.items()}

    def padded(w):
        out = _np.zeros((128, w.shape[1]), _np.float32)
        out[:w.shape[0]] = w
        return out

    def experts_in(w):
        return w.transpose(1, 0, 2).reshape(D, -1)

    def rows_by_tile(w):
        return w.reshape(-1, 128, w.shape[-1]).transpose(1, 0, 2).reshape(128, -1)

    heads = _np.arange(D)
    wkv = a["L2_xattn_Wkv"].reshape(16, 2, 8, D)
    wk2, wv2 = wkv[:, 0].reshape(D, D), wkv[:, 1].reshape(D, D)
    swap = heads ^ 1
    pos = _np.arange(L, dtype=_np.float32)[None, :]
    theta = _np.power(_np.float32(10000), _np.float32(2) * ((heads % 8) // 2).astype(_np.float32) / _np.float32(8))
    ang = (pos / theta[:, None]).astype(_np.float32)
    sign = _np.where(heads % 2 == 0, -1, 1).astype(_np.float32)[:, None]
    twist = _np.zeros((128, 128), _np.float32)
    q = _np.arange(32)
    twist[64 + q, q] = 1
    twist[96 + q, 32 + q] = -1
    twist[q, 64 + q] = -1
    twist[32 + q, 96 + q] = 1
    before = _np.broadcast_to((_np.arange(8)[None, :] < _np.arange(8)[:, None]).astype(_np.float32).reshape(1, 64), (128, 64))
    block = ((heads[:, None] % 32) // 8 == _np.arange(4)[None, :]).astype(_np.float32)
    w = {
        "ident": _np.eye(128, dtype=_np.float32),
        "wq0": a["L0_xattn_Wq"].T, "wk0": a["L0_xattn_Wk"].T, "wv0": a["L0_xattn_Wv"].T,
        "wu0": rows_by_tile(a["L0_xattn_Wu"].T), "f0a": a["L0_ffn_W1"], "f0b": rows_by_tile(a["L0_ffn_W2"]),
        "wq1": a["L1_xattn_Wq"], "wk1": a["L1_xattn_Wkv"][:, :1024], "wv1": a["L1_xattn_Wkv"][:, 1024:],
        "wo1": rows_by_tile(a["L1_xattn_Wo"]),
        "gate1": a["L1_ffn_gate_w"],
        "wq2": a["L2_xattn_Wq"].T, "wqr2": a["L2_xattn_Wq"][swap].T, "wk2": wk2.T, "wkr2": wk2[swap].T, "wv2": wv2.T,
        "wo2": a["L2_xattn_Wo"].T,
        "cw1": a["L2_ffn_cn_w1"], "cw2": a["L2_ffn_cn_w2"], "cw3": padded(a["L2_ffn_cn_w3"]),
        "cw4": padded(_np.tile(a["L2_ffn_cn_w4"], (1, 128))), "gw1": a["L2_ffn_gc_w1"], "gw2": padded(a["L2_ffn_gc_w2"]),
        "gw3": padded(_np.tile(a["L2_ffn_gc_w3"], (1, 128))),
        "twist": twist, "cos": _np.cos(ang), "sin": _np.sin(ang) * sign, "block": block, "before": before,
        "wq3": a["L3_xattn_wq_w"].T, "wk3": a["L3_xattn_wk_w"].T, "wv3": a["L3_xattn_wv_w"].T, "wo3": a["L3_xattn_wo_w"].T,
        "gate3": a["L3_ffn_Wr"],
    }

    def col(v):
        v = v.reshape(-1)
        return padded(v[:, None]) if v.size < 128 else v.reshape(-1, 128).T

    def same(v):
        return _np.tile(v.reshape(1, -1), (128, 1))

    gates = _np.stack([a["g_xattn"], a["g_ffn"]], 1).reshape(-1)
    vecs = {
        "qw": col(_np.tile(a["L0_xattn_qn_w"], 2)), "qb": col(_np.tile(a["L0_xattn_qn_b"], 2)),
        "kw": col(_np.tile(a["L0_xattn_kn_w"], 2)), "kb": col(_np.tile(a["L0_xattn_kn_b"], 2)),
        "b1_0": col(a["L0_ffn_b1"]), "gm": col(a["L1_xattn_gamma_media"]), "bm": col(a["L1_xattn_beta_media"]),
        "gl": col(a["L1_xattn_gamma_lat"]), "bl": col(a["L1_xattn_beta_lat"]), "bq1": col(a["L1_xattn_bq"]),
        "bk1": col(a["L1_xattn_bkv"][:1024]), "bv1": col(a["L1_xattn_bkv"][1024:]),
        "cb1": col(a["L2_ffn_cn_b1"]), "cb2": col(a["L2_ffn_cn_b2"]), "cb3": col(a["L2_ffn_cn_b3"]),
        "cb4": same(a["L2_ffn_cn_b4"]), "gb1": col(a["L2_ffn_gc_b1"]), "gb2": col(a["L2_ffn_gc_b2"]),
        "gb3": same(a["L2_ffn_gc_b3"]), "ar": same(a["L2_ffn_adaptive_range"]),
        "qb3": col(a["L3_xattn_wq_b"]), "kb3": col(a["L3_xattn_wk_b"]), "vb3": col(a["L3_xattn_wv_b"]),
        "b1_3": col(a["L3_ffn_b1"]), "g": same(gates),
    }
    rws = _np.zeros((E, sum(n for _, n in ROWS)), _np.float32)
    at = columns(ROWS)[0]
    for name, v in (("bu", a["L0_xattn_bu"]), ("b2_0", a["L0_ffn_b2"]), ("bo1", a["L1_xattn_bo"]),
                    ("bo3", a["L3_xattn_wo_b"]), ("br3", a["L3_ffn_br"])):
        rws[0, at[name][0]:at[name][0] + at[name][1]] = v
    rws[:, at["b2_3"][0]:at["b2_3"][0] + 128] = a["L3_ffn_b2"]
    mask = a["mask_1x1xSxS2_ik0"].reshape(NT, 128, KEYS).transpose(1, 0, 2).reshape(128, NT * KEYS)
    arrays = {
        "x": a["x"].reshape(B * NT, 128, D).transpose(1, 0, 2).reshape(128, -1),
        "ctxT": a["ctx_1024"].transpose(2, 0, 1).reshape(D, -1),
        "ctx": a["ctx_1024"].transpose(1, 0, 2).reshape(KEYS, -1),
        "vec": _np.concatenate([vecs[n] for n, _ in VECS], 1),
        "rows": rws, "mask": mask,
        "w_moe1": _np.concatenate([experts_in(a["L1_ffn_fc_w"]), rows_by_tile(a["L1_ffn_proj_w"].reshape(-1, 128))], 1),
        "w_moe3": _np.concatenate([experts_in(a["L3_ffn_W1"]), rows_by_tile(a["L3_ffn_W2"].reshape(-1, 128))], 1),
    }
    for g, parts in W_GROUPS:
        arrays["w_" + g] = _np.concatenate([w[n] for n, _ in parts], 1)
    arrays = {k: _np.ascontiguousarray(v) for k, v in arrays.items()}

    known = {}
    for final in (False, True):
        nc = _bacc.Bacc("TRN2", target_bir_lowering=False, num_devices=1)
        dram = {k: nc.dram_tensor(f"in_{k}_dram", v.shape, mybir.dt.from_np(v.dtype), kind="ExternalInput").ap()
                for k, v in arrays.items()}
        dram["out"] = nc.dram_tensor("out_dram", (128, B * L), F32, kind="ExternalOutput").ap()
        program(nc, dram, known)
    r = _run(nc, [{f"in_{k}_dram": v for k, v in arrays.items()}], core_ids=[0])
    out = r.results[0]["out_dram"]
    return out.reshape(128, B * NT, D).transpose(1, 0, 2).reshape(B, L, D)
```

```python
from contextlib import ExitStack

import numpy as np

import concourse.bass as bass
from concourse import mybir

B, L, D = 4, 512, 128
PAIRS, NS = 2, 2
NT = L // 128
KEYS = 77
H0, DH0 = 16, 64
H1 = 8
E, FT = 8, 4
PC = 8
EPS = 1e-5
NEG = -1e9

ALU = mybir.AluOpType
ACT = mybir.ActivationFunctionType
F32 = mybir.dt.float32
I32 = mybir.dt.int32
AX = mybir.AxisListType.X

W_FIRST = [("ident", 128), ("wk0", 1024), ("wq0", 1024)]
W_REST0 = [("wv0", 1024), ("wu0", 1024), ("f0a", 512), ("f0b", 512)]
W_L1 = [("wq1", 1024), ("wk1", 1024), ("wv1", 1024), ("wo1", 1024)]
W_MOE = [("fc", 4096), ("pj", 4096)]
W_L2 = [("wq2", 128), ("wqr2", 128), ("wk2", 128), ("wkr2", 128), ("wv2", 128), ("wo2", 128),
        ("cw1", 128), ("cw2", 128), ("cw3", 128), ("cw4", 128), ("gw1", 64), ("gw2", 32), ("gw3", 128),
        ("twist", 128), ("cos", 512), ("sin", 512), ("block", 16), ("before", 64), ("gate1", 8)]
W_L3 = [("wq3", 128), ("wk3", 128), ("wv3", 128), ("wo3", 128), ("gate3", 8)]
W_GROUPS = [("first", W_FIRST), ("rest0", W_REST0), ("l1", W_L1), ("l2", W_L2), ("l3", W_L3)]
VECS = [("qw", 1), ("qb", 1), ("kw", 1), ("kb", 1), ("b1_0", 4), ("gm", 1), ("bm", 1), ("gl", 1), ("bl", 1),
        ("bq1", 8), ("bk1", 8), ("bv1", 8), ("cb1", 1), ("cb2", 1), ("cb3", 1), ("cb4", 1), ("gb1", 1),
        ("gb2", 1), ("gb3", 1), ("ar", 1), ("qb3", 1), ("kb3", 1), ("vb3", 1), ("b1_3", 32), ("g", 8)]
ROWS = [("bu", 128), ("b2_0", 128), ("bo1", 128), ("bo3", 128), ("b2_3", 128), ("br3", 8)]


def columns(parts):
    at, out = 0, {}
    for name, n in parts:
        out[name] = (at, n)
        at += n
    return out, at


class Signal:

    def __init__(self, sem, known, it, name, order=None, credit=0):
        self.sem, self.known, self.it, self.credit = sem, known.setdefault(name, {}), it, credit
        self.order = known.setdefault(order or name, {})
        self.n = 0
        self.seen = {}

    def mark(self, *event):
        self.n += 1
        assert event not in self.seen
        self.seen[event] = self.n
        return self.sem, 1

    def at(self, *event):
        return self.value(self.order.get(event, 1) + self.credit)

    def value(self, n):
        it = self.it[0]
        return (self.sem, n if isinstance(it, int) else it * self.known.get("total", 0) + n)


S0, S1, T0, T1, G0, G1 = range(6)
TILES0 = [(s, k) for s in range(NS) for k in (4, 0, 1, 2, 3)]


class Rotor:
    def __init__(self, *slots):
        self.slots, self.n = slots, 0

    def __call__(self):
        self.n += 1
        return self.slots[(self.n - 1) % len(self.slots)]


def schedule():
    big, turn, gen = Rotor(S0, S1), Rotor(T0, T1), Rotor(G0, G1)
    wide = Rotor(S0, S1, T0, T1)
    st = []

    def do(kind, *args):
        st.append((kind, args))

    def norm(l, s):
        do("norm_stats", l, s)
        if l == 2:
            do("norm_again", l, s)
        do("norm_apply", l, s)

    def norm_turn(l, s):
        do("norm_turn", l, s, gen())

    def small_attention(l, before={}):
        units = [(s, hf, t) for s in range(NS) for hf in range(2) for t in range(NT)]
        n, mixes = len(units), 4 if l == 0 else 1
        for k in range(n + 6):
            for step in before.get(k, ()):
                step()
            if k < n:
                slot = big()
                do("scores", l, *units[k], slot)
                do("less_max", l, *units[k], slot, k)
                do("exp", l, *units[k], k)
            if 1 <= k < n + 1:
                do("normalise", l, *units[k - 1], k - 1)
            if k >= 7 and k % 4 == 3:
                s, hf, _ = units[k - 7]
                for j in range(mixes):
                    do("mix_values", l, s, hf, j, gen())
            if k in (12, 20):
                project(l, 0 if k == 12 else 1)
            if k == 13:
                norm(l + 1, 0)
            if 3 <= k < n + 3:
                for r in range(2):
                    do("turn_probs", l, *units[k - 3], k - 3, r, turn())
        norm(l + 1, 1)

    def project(l, s):
        do("project", l, s, gen())

    for s in range(NS):
        norm(0, s)
    for s in range(NS):
        norm_turn(0, s)
        do("clear_keys0", s)
        for h in range(2):
            do("values0", s, h, gen())
    tiles = TILES0
    for n in range(len(tiles) + 2):
        if n < len(tiles):
            slot = big()
            do("queries0", *tiles[n], slot)
            do("head_norm", *tiles[n], slot)
        if 1 <= n < len(tiles) + 1:
            do("head_scale", *tiles[n - 1], n - 1, before)
        if n >= 2:
            for h in range(2):
                do("turn_queries", *tiles[n - 2], n - 2, h, turn())
        before = slot
    small_attention(0)
    for s in range(NS):
        norm_turn(1, s)
        for f in range(FT):
            do("hidden", 1, s, 0, f, wide())
        do("ffn_out", s, gen())
        norm(2, s)
        do("media_norm", s)
    for s in range(NS):
        norm_turn(2, s)
        do("media_turn", s, gen())
        for c in range(5):
            for h in range(2):
                do("values1", s, c, h, gen())
        for h in range(2):
            do("media_keys1", s, h, gen())
        do("queries1", s, 0, gen())
        do("keys1", s, 0, gen())
        for h in range(H1 + 1):
            for t in range(NT):
                if h < H1:
                    slot = big()
                    do("scores1", s, h, t, slot)
                    do("softmax1", s, h, t, slot)
                if t == 0 and h >= 2:
                    do("mix_values1", s, h - 2, gen())
                if t == 1 and h + 1 < H1:
                    do("queries1", s, h + 1, gen())
                    do("keys1", s, h + 1, gen())
                if h:
                    for c in ((), (0, 1), (2, 3), (4,))[t]:
                        do("turn_probs1", s, h - 1, c, turn())
        do("mix_values1", s, H1 - 1, gen())
        project(2, s)
        norm(3, s)

    def moe(l, s):
        norm_turn(l, s)
        do("logits", l, s, gen())
        do("gates", l, s)
        for e in range(E + 1):
            if e < E:
                for f in range(FT):
                    do("hidden", l, s, e, f, wide())
            if e == 1 and l == 7:
                do("gate_bias", s, gen())
            if e:
                do("expert_out", l, s, e - 1, gen())

    for s in range(NS):
        moe(3, s)
        norm(4, s)
    norm_turn(4, 0)
    for s in range(NS):
        do("clear_values", s)
    do("project_heads", 4, 0, gen(), big(), big())
    small_attention(4, {2: (lambda: norm_turn(4, 1),), 3: (lambda: do("project_heads", 4, 1, gen(), gen(), turn()),)})
    for s in range(NS):
        norm_turn(5, s)
        do("global_net", s, gen())
    for c in range(3):
        twists = {}
        for stage in (0, 4, 1, 2, 3):
            for s in range(NS):
                twists[stage, s] = gen() if stage == 4 else wide()
                do("cycle", s, c, stage, twists[stage, s])
                if stage == 3:
                    do("couple", s, c, twists[4, s])
    for s in range(NS):
        do("cycle_out", s, gen())
        norm(6, s)
    norm_turn(6, 0)
    do("project_heads", 6, 0, gen(), big(), big())
    small_attention(6, {2: (lambda: norm_turn(6, 1),), 3: (lambda: do("project_heads", 6, 1, gen(), gen(), turn()),)})
    for s in range(NS):
        moe(7, s)
        do("store", s)
    return st


def program(nc, dram, known):
    steps = schedule()
    it = [0]
    signals = {}
    with ExitStack() as ctx:
        def sb(name, shape, dt=F32):
            return ctx.enter_context(nc.sbuf_tensor(name, shape, dt))

        def signal(name, order=None, credit=0):
            signals[name] = Signal(ctx.enter_context(nc.semaphore(name)), known, it, name, order, credit)
            return signals[name]

        W = {}
        group_of = {}
        group_tiles = {}
        for gname, parts in W_GROUPS:
            cols, total = columns(parts)
            group_tiles[gname] = sb("w_" + gname, [128, total])
            for name, (a, n) in cols.items():
                W[name] = group_tiles[gname][:, a:a + n]
                group_of[name] = gname
        vcols, nv = columns(VECS)
        vec = sb("vec", [128, nv])
        rcols, nr = columns(ROWS)
        rows = sb("rows", [E, nr])

        def V(name, i=0, p=128):
            a = vcols[name][0] + i
            return vec[0:p, a:a + 1]

        def R(name, p=1):
            a, n = rcols[name]
            return rows[0:p, a:a + n]

        ident = W["ident"]
        ones = sb("ones", [1, 128])
        half_power = sb("half_power", [128, 16])
        low = sb("low", [128, 1])
        mask = sb("mask", [128, NT * KEYS], I32)
        moe = sb("moe", [128, 8192])
        centre = sb("centre", [128, 16])
        scaled = sb("scaled", [128, 16])
        gates_t = sb("gates_t", [128, 8])
        x = sb("x", [128, NS, NT, 128])
        ctxT = sb("ctxT", [128, NS * KEYS])
        ctx_rows = sb("ctx_rows", [KEYS, NS, 128])
        xn = sb("xn", [128, NS, NT, 128])
        xnT = sb("xnT", [128, NS, L])
        stat = sb("stat", [128, NS, NT, 6])
        mv = sb("mv", [128, NS, NT, 2])
        ve = sb("ve", [128, NS, 2, NT])
        rs = sb("rs", [128, NS, 3, NT])
        mstat = sb("mstat", [KEYS, NS, 6])
        mmv = sb("mmv", [KEYS, NS, 4])
        mn = sb("mn", [KEYS, NS, 128])
        mnT = sb("mnT", [128, NS, KEYS])
        hn = sb("hn", [128, 5, 16])
        arenaA = sb("arenaA", [128, 5120])
        arenaB = sb("arenaB", [128, 2, 8 * L])
        arenaC = sb("arenaC", [128, 8 * L])
        probs = sb("probs", [128, 8 * 616])
        nmax = sb("nmax", [128, 4, 8])
        rsum = sb("rsum", [128, 4, 2, 8])
        qh = sb("qh", [128, 2, L])
        kh = sb("kh", [128, 2, L])
        kmedia = sb("kmedia", [128, H1, KEYS])
        gt = sb("gt", [128, NS, 8, NT * E])
        gl = sb("gl", [128, NS, 8])
        psum = ctx.enter_context(nc.psum_tensor("psum", [128, 8 * 512], F32))

        qT0 = [a[:, 0:4096].rearrange("p (m q) -> p m q", m=8) for a in (arenaA, moe)]
        sq = arenaC[:, 0:1024]
        qn = arenaC[:, 1024:3072].rearrange("p (i n) -> p i n", i=2)
        rot, cur = [qh, kh], kh
        W["fc"], W["pj"] = moe[:, 0:4096], moe[:, 4096:8192]
        v0 = [a[:, 4096:5120] for a in (arenaA, moe)]
        kbd0_flat = [probs[:, 2464:2464 + 16 * KEYS], moe[:, 5120:5120 + 16 * KEYS]]
        kbd0 = [a.rearrange("p (m r k) -> p m r k", m=8, r=2) for a in kbd0_flat]
        kbd = [arenaA[:, 1280 * s:1280 * s + 16 * KEYS].rearrange("p (h k) -> p h k", h=16) for s in range(NS)]
        vpad_flat = [arenaA[:, 2560 + 512 * s:3072 + 512 * s] for s in range(NS)]
        vpad = [a.rearrange("p (h c) -> p h c", h=16) for a in vpad_flat]
        cmp = arenaB[:, 0, 0:3 * NT * E * E].rearrange("p (n c) -> p n c", n=3)
        gT = arenaB[0:E, 1, 0:L]
        v1 = arenaA[:, :].rearrange("p (c n) -> p c n", c=5)
        pT = [arenaB[:, i, :].rearrange("p (r j q) -> p r j q", r=2, j=4) for i in range(2)]
        pT1 = [arenaB[:, i, 0:5 * L].rearrange("p (c q) -> p c q", c=5) for i in range(2)]
        oT = arenaC[:, :].rearrange("p (m q) -> p m q", m=8)
        hid = arenaC[:, :].rearrange("p (i f q) -> p i f q", i=2, f=FT)
        net = arenaC[:, :].rearrange("p (i q) -> p i q", i=8)
        unit_probs = [probs[:, i * 616:(i + 1) * 616] for i in range(4)]
        row_probs = [probs[:, i * 589:(i + 1) * 589] for i in range(8)]

        def slot(i, cols=None, p=128, at=0, p0=0):
            base = 1024 * i if i < 2 else 2048 + 512 * (i - 2)
            cols = cols if cols is not None else (1024 if i < 2 else 512)
            return psum[p0:p0 + p, base + at:base + at + cols]

        def scores_of(i):
            return slot(i).rearrange("p (r c) -> p r c", r=2)[:, :, 0:4 * KEYS]

        loaded = {g: signal("loaded_" + g) for g, _ in W_GROUPS}
        held_dve = signal("held_dve")
        held_pe = signal("held_pe")
        loaded_moe = signal("loaded_moe")
        loaded_small = signal("loaded_small")
        loaded_x = signal("loaded_x")
        loaded_ctx = signal("loaded_ctx")
        stored = signal("stored")
        consts_ready = signal("consts_ready")
        gates_tanh = signal("gates_tanh")
        centred = signal("centred")
        centring = signal("centring")
        centred_small = signal("centred_small")
        filled = [signal(f"filled_{i}") for i in range(6)]
        free = [signal(f"free_{i}", order=f"filled_{i}", credit=1) for i in range(6)]
        dve_step = signal("dve_step")
        var_ready = signal("var_ready")
        rstd_ready = signal("rstd_ready")
        xn_ready = signal("xn_ready")
        mvar_ready = signal("mvar_ready")
        mrstd_ready = signal("mrstd_ready")
        mn_ready = signal("mn_ready")
        squares = signal("squares")
        hvar_ready = signal("hvar_ready")
        hrstd_ready = signal("hrstd_ready")
        exp_ready = signal("exp_ready")
        rsum_ready = signal("rsum_ready")
        probs_ready = signal("probs_ready")
        probs1_ready = signal("probs1_ready")
        nmax_ready = signal("nmax_ready")
        kbd0_clear = signal("kbd0_clear")
        vpad_clear = signal("vpad_clear")
        keys_ready = signal("keys_ready")
        gate_exp = signal("gate_exp")
        gate_ready = signal("gate_ready")
        rotated = signal("rotated")
        heads_ready = signal("heads_ready")
        mean_ready = signal("mean_ready")
        coup_ready = signal("coup_ready")

        def tensor_did(*event):
            for i in range(6):
                if event in known[f"filled_{i}"]:
                    return filled[i].at(*event)
            return filled[0].at(*event)

        def reader_did(*event):
            for i in range(6):
                if event in known[f"filled_{i}"]:
                    return free[i].at(*event)
            return free[0].at(*event)

        def need(eng, *names):
            for g in sorted({group_of[n] for n in names}):
                eng.wait_ge(loaded[g].sem, 16)

        NSMALL = 3
        block = ctx.enter_context(nc.Block())

        @block.sync
        def _(sp):
            sp.dma_start(vec[:], dram["vec"]).then_inc(loaded_small.sem, 16)
            sp.dma_start(rows[:], dram["rows"]).then_inc(loaded_small.sem, 16)
            sp.dma_start(mask[:], dram["mask"]).then_inc(loaded_small.sem, 16)
            with sp.Fori(0, PAIRS) as pair:
                it[0] = pair
                sp.wait_ge(stored.sem, pair * (16 * NS) + 16)
                sp.dma_start(x[:].rearrange("p s t d -> p (s t d)"),
                             dram["x"][:, bass.ds(pair * (NS * L), NS * L)]).then_inc(loaded_x.sem, 16)
                sp.dma_start(ctxT[:], dram["ctxT"][:, bass.ds(pair * (NS * KEYS), NS * KEYS)]).then_inc(loaded_ctx.sem, 16)
                sp.dma_start(ctx_rows[:].rearrange("p s d -> p (s d)"),
                             dram["ctx"][:, bass.ds(pair * (NS * 128), NS * 128)]).then_inc(loaded_ctx.sem, 16)
                sp.wait_ge(*tensor_did("pv", 0, 1, 1, 3))
                sp.dma_start(moe[:], dram["w_moe1"]).then_inc(loaded_moe.sem, 16)
                sp.wait_ge(*reader_did("out", 3, 1, E - 1))
                sp.dma_start(moe[:], dram["w_moe3"]).then_inc(loaded_moe.sem, 16)
                for s in range(NS):
                    sp.wait_ge(*reader_did("out", 7, s, E - 1))
                    sp.dma_start(dram["out"][:, bass.ds(pair * (NS * L) + s * L, L)],
                                 x[:, s, :, :].rearrange("p t d -> p (t d)")).then_inc(stored.sem, 16)
            it[0] = 0
            sp.wait_ge(stored.sem, 16 * NS * PAIRS + 16)

        @block.tensor
        def _(pe):
            used = [0] * 6

            def take(i):
                used[i] += 1
                pe.wait_ge(*free[i].value(used[i]))

            def read(i, *event):
                if event not in known[f"filled_{i}"]:
                    pe.wait_ge(*reader_did(*event))

            def mm(out, lhsT, rhs, start=True, stop=True):
                return nc.tensor.matmul(out, lhsT, rhs, start=start, stop=stop)

            def tr(out, in_, p):
                return nc.tensor.transpose(out, in_, ident[0:p, 0:p])

            def norm_turn(l, s, i):
                pe.wait_ge(*xn_ready.at(l, s))
                take(i)
                for t in range(NT):
                    last = tr(slot(i, 128, at=128 * t), xn[:, s, t, :], 128)
                last.then_inc(*filled[i].mark("norm", l, s))

            def values0(s, h, i):
                if s == 0 and h == 0:
                    pe.wait_ge(loaded_ctx.sem, it[0] * 32 + 32)
                    need(pe, "wv0")
                take(i)
                mm(slot(i, 512, KEYS), ctxT[:, s * KEYS:(s + 1) * KEYS], W["wv0"][:, h * 512:(h + 1) * 512])\
                    .then_inc(*filled[i].mark("v0", s, h))

            def queries0(s, k, i):
                pe.wait_ge(centred.sem, 2)
                read(i, "norm", 0, s)
                take(i)
                lhs, p, w = (ctxT[:, s * KEYS:(s + 1) * KEYS], KEYS, "wk0") if k == 4 else \
                    (xnT[:, s, k * 128:(k + 1) * 128], 128, "wq0")
                for h in range(2):
                    last = mm(slot(i, 512, p, 512 * h), lhs, W[w][:, h * 512:(h + 1) * 512])
                last.then_inc(*filled[i].mark("q0", s, k))

            def turn_queries(s, k, n, h, i):
                p = KEYS if k == 4 else 128
                read(i, "q0", s, k)
                take(i)
                for m in range(4):
                    c = 512 * h + 128 * m
                    last = tr(slot(i, p, at=128 * m), qn[0:p, n % 2, c:c + 128], p)
                last.then_inc(*filled[i].mark("tq", s, k, h))

            def scores(l, s, hf, t, i):
                if l == 0:
                    read(i, "tq", s, 3, 1)
                else:
                    pe.wait_ge(*(rotated.at(l, s) if l == 4 else reader_did("q", l, s)))
                    pe.wait_ge(*heads_ready.at(l, s))
                take(i)
                if l == 0:
                    for j in range(4):
                        m = 4 * hf + j
                        last = mm(slot(i, 2 * KEYS, at=512 * (j // 2) + 2 * KEYS * (j % 2)),
                                  qT0[s][:, m, t * 128:(t + 1) * 128], kbd0[s][:, m, :, :].rearrange("p r k -> p (r k)"))
                else:
                    for r in range(2):
                        h = 4 * (2 * hf + r)
                        last = mm(slot(i, 4 * KEYS, at=512 * r), rot[s][:, 0, t * 128:(t + 1) * 128],
                                  kbd[s][:, h:h + 4, :].rearrange("p j k -> p (j k)"))
                last.then_inc(*filled[i].mark("sc", l, s, hf, t))

            def turn_probs(l, s, hf, t, k, r, i):
                pe.wait_ge(*probs_ready.at(l, s, hf, t))
                take(i)
                for j in range(4):
                    c = 308 * r + KEYS * j
                    last = tr(slot(i, 128, KEYS, 128 * j), unit_probs[k % 4][:, c:c + KEYS], 128)
                last.then_inc(*filled[i].mark("tp", l, s, hf, t, r))

            def mix_values(l, s, hf, j, i):
                read(i, "tp", l, s, hf, 3, 1)
                if l == 0:
                    read(i, "v0", s, 1)
                    take(i)
                    for r in range(2):
                        h = 2 * (4 * hf + j) + r
                        last = mm(slot(i, L, 64, p0=64 * r), v0[s][:, 64 * h:64 * h + 64],
                                  pT[hf][:, j // 2, 2 * (j % 2) + r, :])
                else:
                    read(i, "kv", l, s)
                    take(i)
                    for jj in range(4):
                        for r in range(2):
                            g = 2 * hf + r
                            last = mm(slot(i, L, 32, p0=32 * g), vpad[s][:, 4 * g + jj, :], pT[hf][:, r, jj, :],
                                      start=jj == 0, stop=jj == 3)
                last.then_inc(*filled[i].mark("pv", l, s, hf, j))

            def project(l, s, i):
                w, n, bias = {0: ("wu0", 8, "bu"), 2: ("wo1", 8, "bo1"), 4: ("wo2", 1, None), 6: ("wo3", 1, "bo3")}[l]
                need(pe, w)
                read(i, *(("pv1", s, H1 - 1) if l == 2 else ("pv", l, s, 1, 3 if l == 0 else 0)))
                take(i)
                for t in range(NT):
                    out = slot(i, 128, at=128 * t)
                    for m in range(n):
                        last = mm(out, oT[:, s if n == 1 else m, t * 128:(t + 1) * 128], W[w][:, m * 128:(m + 1) * 128],
                                  start=m == 0, stop=bias is None and m == n - 1)
                    if bias:
                        last = mm(out, ones[:, :], R(bias), start=False)
                last.then_inc(*filled[i].mark("proj", l, s))

            def hidden(l, s, e, f, i):
                w = {1: "f0a", 3: "fc", 7: "fc"}[l]
                if l == 1:
                    need(pe, w)
                elif e == 0 and f == 0:
                    pe.wait_ge(loaded_moe.sem, it[0] * 32 + (16 if l == 3 else 32))
                read(i, "norm", l, s)
                take(i)
                c = 512 * e + 128 * f
                mm(slot(i, L), W[w][:, c:c + 128], xnT[:, s, :]).then_inc(*filled[i].mark("hid", l, s, e, f))

            def out_of(l, s, e, i, w, bias):
                read(i, "hid", l, s, e, FT - 1)
                take(i)
                for t in range(NT):
                    out = slot(i, 128, at=128 * t)
                    for f in range(FT):
                        c = 512 * e + 128 * f
                        last = mm(out, hid[:, (e + s) % 2, f, t * 128:(t + 1) * 128], W[w][:, c:c + 128],
                                  start=f == 0, stop=not bias and f == FT - 1)
                    if bias:
                        last = mm(out, ones[:, :], R(bias), start=False)
                last.then_inc(*filled[i].mark("out", l, s, e))

            def ffn_out(s, i):
                out_of(1, s, 0, i, "f0b", "b2_0")

            def expert_out(l, s, e, i):
                out_of(l, s, e, i, "pj", None)

            def media_turn(s, i):
                pe.wait_ge(*mn_ready.at(s))
                take(i)
                tr(slot(i, KEYS), mn[:, s, :], KEYS).then_inc(*filled[i].mark("media", s))

            def values1(s, c, h, i):
                need(pe, "wv1")
                read(i, "norm", 2, s)
                if c == 4:
                    read(i, "media", s)
                take(i)
                lhs, p = (mnT[:, s, :], KEYS) if c == 4 else (xnT[:, s, c * 128:(c + 1) * 128], 128)
                mm(slot(i, 512, p), lhs, W["wv1"][:, 512 * h:512 * h + 512]).then_inc(*filled[i].mark("v1", s, c, h))

            def media_keys1(s, h, i):
                take(i)
                for m in range(4):
                    c = 128 * (4 * h + m)
                    last = mm(slot(i, KEYS, at=KEYS * m), W["wk1"][:, c:c + 128], mnT[:, s, :])
                last.then_inc(*filled[i].mark("km1", s, h))

            def queries1(s, h, i):
                take(i)
                mm(slot(i, L), W["wq1"][:, 128 * h:128 * h + 128], xnT[:, s, :]).then_inc(*filled[i].mark("q1", s, h))

            def keys1(s, h, i):
                take(i)
                mm(slot(i, L), W["wk1"][:, 128 * h:128 * h + 128], xnT[:, s, :]).then_inc(*filled[i].mark("k1", s, h))

            def scores1(s, h, t, i):
                read(i, "q1", s, h)
                read(i, "k1", s, h)
                take(i)
                q = qh[:, h % 2, t * 128:(t + 1) * 128]
                mm(slot(i, L), q, kh[:, h % 2, :])
                mm(slot(i, KEYS, at=512), q, kmedia[:, h, :]).then_inc(*filled[i].mark("s1", s, h, t))

            def turn_probs1(s, h, c, i):
                pe.wait_ge(*probs1_ready.at(s, h, NT - 1))
                take(i)
                p = KEYS if c == 4 else 128
                for t in range(NT):
                    last = tr(slot(i, 128, p, 128 * t), row_probs[4 * (h % 2) + t][:, 128 * c:128 * c + p], 128)
                last.then_inc(*filled[i].mark("tp1", s, h, c))

            def mix_values1(s, h, i):
                read(i, "v1", s, 4, 0)
                read(i, "v1", s, 4, 1)
                read(i, "tp1", s, h, 4)
                read(i, "tp1", s, h, 3)
                take(i)
                for c in range(5):
                    last = mm(slot(i, L), v1[:, c, 128 * h:128 * h + 128], pT1[h % 2][:, c, :],
                              start=c == 0, stop=c == 4)
                last.then_inc(*filled[i].mark("pv1", s, h))

            def logits(l, s, i):
                w = {3: "gate1", 7: "gate3"}[l]
                need(pe, w)
                read(i, "norm", l, s)
                take(i)
                for t in range(NT):
                    last = mm(slot(i, E, at=E * t), xnT[:, s, t * 128:(t + 1) * 128], W[w], stop=l == 3)
                    if l == 7:
                        last = mm(slot(i, E, at=E * t), ones[:, :], R("br3"), start=False)
                last.then_inc(*filled[i].mark("logits", l, s))

            def gate_bias(s, i):
                pe.wait_ge(*gate_ready.at(7, s))
                take(i)
                for t in range(NT):
                    last = tr(slot(i, 128, E, 128 * t), gt[:, s, 7, E * t:E * t + E], 128)
                last.then_inc(*filled[i].mark("gT", s))
                read(i, "gT", s)
                take(i)
                for t in range(NT):
                    last = mm(slot(i, 128, at=128 * t), gT[:, t * 128:(t + 1) * 128], R("b2_3", E))
                last.then_inc(*filled[i].mark("gb", s))

            def project_heads(l, s, i, j, k):
                wq, wqr, wk, wkr, wv = ("wq2", "wqr2", "wk2", "wkr2", "wv2") if l == 4 else ("wq3", None, "wk3", None, "wv3")
                need(pe, wq)
                cT = ctxT[:, s * KEYS:(s + 1) * KEYS]
                read(i, "norm", l, s)
                take(i)
                last = mm(slot(i, KEYS), W[wk], cT)
                if l == 4:
                    last = mm(slot(i, KEYS, at=KEYS), W[wkr], cT)
                last = mm(slot(i, 128, KEYS, at=256), cT, W[wv])
                last.then_inc(*filled[i].mark("kv", l, s))
                take(j)
                mm(slot(j, L), W[wq], xnT[:, s, :]).then_inc(*filled[j].mark("q", l, s))
                if l == 4:
                    take(k)
                    mm(slot(k, L), W[wqr], xnT[:, s, :]).then_inc(*filled[k].mark("qr", l, s))

            def global_net(s, i):
                pe.wait_ge(*mean_ready.at(s))
                take(i)
                mm(slot(i, 1, 64), W["gw1"], gl[:, s, 0:1]).then_inc(*filled[i].mark("g", s, 0))
                read(i, "g", s, 0)
                take(i)
                pe.sem_inc(held_pe.sem, 1)
                mm(slot(i, 1, 32), W["gw2"][0:64, :], gl[0:64, s, 1:2]).then_inc(*filled[i].mark("g", s, 1))
                read(i, "g", s, 1)
                take(i)
                mm(slot(i, 1), W["gw3"][0:32, :], gl[0:32, s, 2:3]).then_inc(*filled[i].mark("g", s, 2))

            def cycle(s, c, stage, i):
                src = xnT[:, s, :] if c == 0 else cur[:, s, :]
                if stage == 0 and c:
                    pe.wait_ge(*coup_ready.at(s, c - 1))
                if stage in (1, 2, 3):
                    read(i, "cy", s, c, stage - 1)
                take(i)
                if stage == 0:
                    last = mm(slot(i, L), W["cw1"], src)
                elif stage == 1:
                    last = mm(slot(i, L), W["cw2"], net[:, 4 * s, :])
                elif stage == 2:
                    last = mm(slot(i, L), W["cw3"], net[:, 4 * s + 1, :])
                elif stage == 3:
                    last = mm(slot(i, L), W["cw4"], net[:, 4 * s + 2, :])
                else:
                    last = mm(slot(i, L), W["twist"], src)
                last.then_inc(*filled[i].mark("cy", s, c, stage))

            def cycle_out(s, i):
                pe.wait_ge(*coup_ready.at(s, 2))
                take(i)
                for t in range(NT):
                    last = tr(slot(i, 128, at=128 * t), cur[:, s, t * 128:(t + 1) * 128], 128)
                last.then_inc(*filled[i].mark("cyo", s))

            parts = dict(norm_turn=norm_turn, values0=values0, queries0=queries0, turn_queries=turn_queries,
                         scores=scores, turn_probs=turn_probs, mix_values=mix_values, project=project,
                         hidden=hidden, ffn_out=ffn_out, expert_out=expert_out, media_turn=media_turn,
                         values1=values1, media_keys1=media_keys1, queries1=queries1, keys1=keys1,
                         scores1=scores1, turn_probs1=turn_probs1, mix_values1=mix_values1, logits=logits,
                         gate_bias=gate_bias, project_heads=project_heads, global_net=global_net,
                         cycle=cycle, cycle_out=cycle_out)
            need(pe, "ident")
            pe.wait_ge(consts_ready.sem, 6)
            pe.wait_ge(loaded_small.sem, 16 * NSMALL)
            with pe.Fori(0, PAIRS) as pair:
                it[0] = pair
                for kind, args in steps:
                    if kind in parts:
                        parts[kind](*args)
            it[0] = 0

        @block.scalar
        def _(act):
            def f(out, in_, func, **kw):
                return nc.scalar.activation(out, in_, func, **kw)

            def norm_turn(l, s, i):
                act.wait_ge(*filled[i].at("norm", l, s))
                if l == 2:
                    last = f(xnT[:, s, :], slot(i, L), ACT.Identity, scale=V("gl"), bias=V("bl"))
                else:
                    last = f(xnT[:, s, :], slot(i, L), ACT.Copy)
                last.then_inc(*free[i].mark("norm", l, s))

            def head_norm(s, k, i):
                p = KEYS if k == 4 else 128
                act.wait_ge(*filled[i].at("q0", s, k))
                if prev_sq[0] is not None:
                    act.wait_ge(*hvar_ready.at(*prev_sq[0]))
                prev_sq[0] = (s, k)
                f(sq[0:p, :], slot(i, 1024, p), ACT.Square).then_inc(*squares.mark(s, k))

            prev_sq = [None]

            def turn_queries(s, k, n, h, i):
                p = KEYS if k == 4 else 128
                act.wait_ge(*filled[i].at("tq", s, k, h))
                src = slot(i).rearrange("p (m c) -> p m c", m=4)[:, :, 0:p] if k < 4 else \
                    slot(i)[:, :].rearrange("p (m c) -> p m c", m=4)[:, :, 0:KEYS]
                if k == 4:
                    act.wait_ge(*kbd0_clear.at(s))
                    for r in range(2):
                        half, a, b = slice(64 * r, 64 * r + 64), vcols["kw"][0], vcols["kb"][0]
                        last = f(kbd0[s][half, 4 * h:4 * h + 4, r, :], src[half, :, :], ACT.Identity,
                                 scale=vec[half, a:a + 1], bias=vec[half, b:b + 1])
                else:
                    last = f(qT0[s][:, 4 * h:4 * h + 4, k * 128:(k + 1) * 128], src, ACT.Identity,
                             scale=scaled[:, 0:1], bias=scaled[:, 1:2])
                last.then_inc(*free[i].mark("tq", s, k, h))

            def exp(l, s, hf, t, k):
                act.wait_ge(*reader_did("sc", l, s, hf, t))
                f(unit_probs[k % 4], unit_probs[k % 4], ACT.Exp).then_inc(*exp_ready.mark(l, s, hf, t))

            def turn_probs(l, s, hf, t, k, r, i):
                act.wait_ge(*filled[i].at("tp", l, s, hf, t, r))
                f(pT[hf][0:KEYS, r, :, t * 128:(t + 1) * 128], slot(i, 512, KEYS).rearrange("p (j q) -> p j q", j=4),
                  ACT.Copy).then_inc(*free[i].mark("tp", l, s, hf, t, r))

            def mix_values(l, s, hf, j, i):
                act.wait_ge(*filled[i].at("pv", l, s, hf, j))
                if l == 0:
                    last = f(oT[:, 4 * hf + j, :], slot(i, L), ACT.Copy)
                elif l == 4:
                    last = f(oT[64 * hf:64 * hf + 64, s, :], slot(i, L, 64, p0=64 * hf), ACT.Copy)
                else:
                    a = vcols["vb3"][0]
                    last = f(oT[64 * hf:64 * hf + 64, s, :], slot(i, L, 64, p0=64 * hf), ACT.Identity,
                             bias=vec[64 * hf:64 * hf + 64, a:a + 1])
                last.then_inc(*free[i].mark("pv", l, s, hf, j))

            def hidden(l, s, e, fi, i):
                act.wait_ge(*filled[i].at("hid", l, s, e, fi))
                kw = {1: dict(func=ACT.Relu, bias=V("b1_0", fi)), 3: dict(func=ACT.Gelu),
                      7: dict(func=ACT.Relu, bias=V("b1_3", 4 * e + fi))}[l]
                func = kw.pop("func")
                f(hid[:, (e + s) % 2, fi, :], slot(i, L), func, **kw).then_inc(*free[i].mark("hid", l, s, e, fi))

            def media_turn(s, i):
                act.wait_ge(*filled[i].at("media", s))
                f(mnT[:, s, :], slot(i, KEYS), ACT.Identity, scale=V("gm"), bias=V("bm"))\
                    .then_inc(*free[i].mark("media", s))

            def values1(s, c, h, i):
                if h == 1:
                    return
                p = KEYS if c == 4 else 128
                act.wait_ge(*filled[i].at("v1", s, c, h))
                f(v1[0:p, c, 512 * h:512 * h + 512], slot(i, 512, p), ACT.Copy).then_inc(*free[i].mark("v1", s, c, h))

            def media_keys1(s, h, i):
                act.wait_ge(*filled[i].at("km1", s, h))
                for m in range(4):
                    last = f(kmedia[:, 4 * h + m, :], slot(i, KEYS, at=KEYS * m), ACT.Identity,
                             bias=V("bk1", 4 * h + m))
                last.then_inc(*free[i].mark("km1", s, h))

            def queries1(s, h, i):
                act.wait_ge(*filled[i].at("q1", s, h))
                f(qh[:, h % 2, :], slot(i, L), ACT.Identity, scale=float(128 ** -0.5), bias=scaled[:, 2 + h:3 + h])\
                    .then_inc(*free[i].mark("q1", s, h))

            def softmax1(s, h, t, i):
                k = 4 * (h % 2) + t
                act.wait_ge(*nmax_ready.at(s, h, t))
                if h >= 2:
                    act.wait_ge(*tensor_did("tp1", s, h - 2, 4))
                f(row_probs[k], slot(i, 589), ACT.Exp, bias=nmax[:, t, 0:1], accum_out=rsum[:, t, 0, 0:1])\
                    .then_inc(*free[i].mark("s1", s, h, t))

            def turn_probs1(s, h, c, i):
                if c % 2:
                    return
                p = KEYS if c == 4 else 128
                act.wait_ge(*filled[i].at("tp1", s, h, c))
                f(pT1[h % 2][0:p, c, :], slot(i, 512, p), ACT.Copy).then_inc(*free[i].mark("tp1", s, h, c))

            def gates(l, s):
                act.wait_ge(*reader_did("logits", l, s))
                f(gt[:, s, 1, :], gt[:, s, 0, :], ACT.Exp).then_inc(*gate_exp.mark(l, s))

            def global_net(s, i):
                for n, (p, b) in enumerate(((64, "gb1"), (32, "gb2"))):
                    act.wait_ge(*filled[i].at("g", s, n))
                    f(gl[0:p, s, n + 1:n + 2], slot(i, 1, p), ACT.Gelu, bias=V(b, p=p))\
                        .then_inc(*free[i].mark("g", s, n))
                act.wait_ge(*filled[i].at("g", s, 2))
                f(gl[:, s, 3:4], slot(i, 1), ACT.Tanh, scale=0.5, bias=scaled[:, 11:12])\
                    .then_inc(*free[i].mark("g", s, 2))

            def cycle(s, c, stage, i):
                if stage == 4:
                    return
                act.wait_ge(*filled[i].at("cy", s, c, stage))
                if stage == 3 and c:
                    act.wait_ge(*coup_ready.at(s, c - 1))
                if stage < 3:
                    last = f(net[:, 4 * s + stage, :], slot(i, L), ACT.Gelu, bias=V(("cb1", "cb2", "cb3")[stage]))
                else:
                    last = f(net[:, 4 * s + 3, :], slot(i, L), ACT.Tanh, scale=0.5, bias=scaled[:, 10:11])
                last.then_inc(*free[i].mark("cy", s, c, stage))

            parts = dict(norm_turn=norm_turn, head_norm=head_norm, turn_queries=turn_queries, exp=exp,
                         turn_probs=turn_probs, mix_values=mix_values, hidden=hidden, media_turn=media_turn,
                         values1=values1, media_keys1=media_keys1, queries1=queries1, softmax1=softmax1,
                         turn_probs1=turn_probs1, gates=gates, global_net=global_net, cycle=cycle)
            for g in ("first", "rest0", "l1", "l2", "l3"):
                act.dma_start(group_tiles[g][:], dram["w_" + g]).then_inc(loaded[g].sem, 16)
            act.wait_ge(loaded_small.sem, 16 * NSMALL)
            a = vcols["g"][0]
            f(gates_t[:, :], vec[:, a:a + 8], ACT.Tanh).then_inc(gates_tanh.sem, 1)
            act.wait_ge(consts_ready.sem, 6)
            with act.Fori(0, PAIRS) as pair:
                it[0] = pair
                for kind, args in steps:
                    if kind in parts:
                        parts[kind](*args)
            it[0] = 0

        @block.gpsimd
        def _(pool):
            def norm_stats(l, s, again=False):
                pool.wait_ge(*var_ready.at(l, s, again))
                nc.gpsimd.tensor_tensor(rs[:, s, int(again), :], ve[:, s, int(again), :], half_power[:, 0:NT], ALU.pow)\
                    .then_inc(*rstd_ready.mark(l, s, again))

            def norm_again(l, s):
                norm_stats(l, s, True)

            def clear_keys0(s):
                nc.gpsimd.memset(kbd0_flat[s], 0.0)
                nc.gpsimd.memset(v0[s], 0.0).then_inc(*kbd0_clear.mark(s))

            def project_heads(l, s, i, j, k):
                need(pool, "block")
                pool.wait_ge(*keys_ready.at(l, s))
                nc.gpsimd.tensor_tensor(kbd[s], rot[s][:, 1, 0:KEYS].unsqueeze(1).broadcast_to([128, 16, KEYS]),
                                        W["block"].unsqueeze(2).broadcast_to([128, 16, KEYS]), ALU.mult)\
                    .then_inc(*heads_ready.mark(l, s))

            def clear_values(s):
                nc.gpsimd.memset(vpad_flat[s], 0.0).then_inc(*vpad_clear.mark(s))

            def media_norm(s):
                pool.wait_ge(*mvar_ready.at(s))
                nc.gpsimd.tensor_tensor(mmv[:, s, 3:4], mmv[:, s, 2:3], half_power[0:KEYS, 0:1], ALU.pow)\
                    .then_inc(*mrstd_ready.mark(s))

            def head_norm(s, k, i):
                p = KEYS if k == 4 else 128
                pool.wait_ge(*hvar_ready.at(s, k))
                n = TILES0.index((s, k)) % 2
                nc.gpsimd.tensor_tensor(hn[0:p, 2 + 2 * n, :], hn[0:p, 1 + 2 * n, :], half_power[0:p, 0:16], ALU.pow)\
                    .then_inc(*hrstd_ready.mark(s, k))

            def normalise(l, s, hf, t, k):
                pool.wait_ge(*rsum_ready.at(l, s, hf, t))
                pr = unit_probs[k % 4].rearrange("p (h k) -> p h k", h=8)
                nc.gpsimd.tensor_tensor(pr, pr, rsum[:, k % 4, 1, :].unsqueeze(2).broadcast_to([128, 8, KEYS]), ALU.mult)\
                    .then_inc(*probs_ready.mark(l, s, hf, t))

            parts = dict(norm_stats=norm_stats, norm_again=norm_again, media_norm=media_norm, head_norm=head_norm,
                         normalise=normalise, clear_keys0=clear_keys0, clear_values=clear_values, project_heads=project_heads)
            pool.memset(half_power[:], -0.5).then_inc(consts_ready.sem, 1)
            pool.wait_ge(consts_ready.sem, 6)
            with pool.Fori(0, PAIRS) as pair:
                it[0] = pair
                for kind, args in steps:
                    if kind in parts:
                        parts[kind](*args)
            it[0] = 0

        @block.vector
        def _(dve):
            auto = [0]

            def link(ins):
                auto[0] += 1
                ins.then_inc(*dve_step.mark("link", auto[0]))
                dve.wait_ge(*dve_step.at("link", auto[0]))

            v = nc.vector

            def norm_stats(l, s):
                if l == 0 and s == 0:
                    dve.wait_ge(loaded_x.sem, it[0] * 16 + 16)
                for t in range(NT):
                    last = v.bn_stats(stat[:, s, t, :], x[:, s, t, :])
                link(last)
                dve.sem_inc(held_dve.sem, 1)
                for t in range(NT):
                    last = v.bn_aggr(mv[:, s, t, :], stat[:, s, t, :])
                link(last)
                v.tensor_scalar(ve[:, s, 0, :], mv[:, s, :, 1], EPS, None, ALU.add)\
                    .then_inc(*var_ready.mark(l, s, False))

            def norm_again(l, s):
                dve.wait_ge(*rstd_ready.at(l, s, False))
                link(v.tensor_tensor(rs[:, s, 2, :], rs[:, s, 0, :], rs[:, s, 0, :], ALU.mult))
                link(v.tensor_tensor(rs[:, s, 2, :], rs[:, s, 2, :], mv[:, s, :, 1], ALU.mult))
                v.tensor_scalar(ve[:, s, 1, :], rs[:, s, 2, :], EPS, None, ALU.add)\
                    .then_inc(*var_ready.mark(l, s, True))

            def norm_apply(l, s):
                r = 0
                dve.wait_ge(*rstd_ready.at(l, s, l == 2))
                if l == 2:
                    link(v.tensor_tensor(rs[:, s, 2, :], rs[:, s, 0, :], rs[:, s, 1, :], ALU.mult))
                    r = 2
                for t in range(NT):
                    last = v.tensor_scalar(xn[:, s, t, :], x[:, s, t, :], mv[:, s, t, 0:1], rs[:, s, r, t:t + 1],
                                           ALU.subtract, ALU.mult)
                last.then_inc(*xn_ready.mark(l, s))

            def media_norm(s):
                if s == 0:
                    dve.wait_ge(loaded_ctx.sem, it[0] * 32 + 32)
                link(v.bn_stats(mstat[:, s, :], ctx_rows[:, s, :]))
                dve.sem_inc(held_dve.sem, 1)
                link(v.bn_aggr(mmv[:, s, 0:2], mstat[:, s, :]))
                v.tensor_scalar(mmv[:, s, 2:3], mmv[:, s, 1:2], EPS, None, ALU.add).then_inc(*mvar_ready.mark(s))
                dve.wait_ge(*mrstd_ready.at(s))
                v.tensor_scalar(mn[:, s, :], ctx_rows[:, s, :], mmv[:, s, 0:1], mmv[:, s, 3:4],
                                ALU.subtract, ALU.mult).then_inc(*mn_ready.mark(s))

            def values0(s, h, i):
                dve.wait_ge(*filled[i].at("v0", s, h))
                dve.wait_ge(*kbd0_clear.at(s))
                v.tensor_copy(v0[s][0:KEYS, 512 * h:512 * h + 512], slot(i, 512, KEYS)).then_inc(*free[i].mark("v0", s, h))

            def head_norm(s, k, i):
                p = KEYS if k == 4 else 128
                dve.wait_ge(*squares.at(s, k))
                link(v.tensor_reduce(hn[0:p, 0, :], sq[0:p, :].rearrange("p (h d) -> p h d", h=16), AX, ALU.add))
                v.tensor_scalar(hn[0:p, 1 + 2 * (TILES0.index((s, k)) % 2), :], hn[0:p, 0, :], 1.0 / DH0, EPS, ALU.mult, ALU.add)\
                    .then_inc(*hvar_ready.mark(s, k))

            def head_scale(s, k, n, i):
                p = KEYS if k == 4 else 128
                dve.wait_ge(*hrstd_ready.at(s, k))
                if n >= 2:
                    dve.wait_ge(*tensor_did("tq", *TILES0[n - 2], 1))
                v.tensor_tensor(qn[0:p, n % 2, :].rearrange("p (h d) -> p h d", h=16),
                                slot(i, 1024, p).rearrange("p (h d) -> p h d", h=16),
                                hn[0:p, 2 + 2 * (n % 2), :].unsqueeze(2).broadcast_to([p, 16, DH0]), ALU.mult)\
                    .then_inc(*free[i].mark("q0", s, k))

            def less_max(l, s, hf, t, i, k):
                dve.wait_ge(*filled[i].at("sc", l, s, hf, t))
                sc = scores_of(i).rearrange("p r (j k) -> p r j k", j=4)
                if l == 6:
                    m = mask[:, t * KEYS:(t + 1) * KEYS]
                    dve.sem_inc(held_dve.sem, 1)
                    for r in range(2):
                        last = v.copy_predicated(
                            sc[:, r, :, :], m.unsqueeze(1).broadcast_to([128, 4, KEYS]),
                            low[:, 0:1].unsqueeze(2).broadcast_to([128, 4, KEYS]))
                    link(last)
                link(v.tensor_reduce(nmax[:, k % 4, :], sc, AX, ALU.max, negate=True))
                nm = nmax[:, k % 4, :].rearrange("p (r j) -> p r j", r=2).unsqueeze(3).broadcast_to([128, 2, 4, KEYS])
                v.tensor_tensor(unit_probs[k % 4].rearrange("p (r j k) -> p r j k", r=2, j=4), sc, nm, ALU.add)\
                    .then_inc(*free[i].mark("sc", l, s, hf, t))

            def normalise(l, s, hf, t, k):
                dve.wait_ge(*exp_ready.at(l, s, hf, t))
                link(v.tensor_reduce(rsum[:, k % 4, 0, :], unit_probs[k % 4].rearrange("p (h k) -> p h k", h=8),
                                     AX, ALU.add))
                v.reciprocal(rsum[:, k % 4, 1, :], rsum[:, k % 4, 0, :]).then_inc(*rsum_ready.mark(l, s, hf, t))

            def add_to_x(l, s, i, label):
                dve.wait_ge(*filled[i].at(*label))
                xs = x[:, s, :, :].rearrange("p t d -> p (t d)")
                v.scalar_tensor_tensor(xs, slot(i, L), gates_t[:, l:l + 1], xs, ALU.mult, ALU.add)\
                    .then_inc(*free[i].mark(*label))
                dve.wait_ge(*free[i].at(*label))

            def project(l, s, i):
                add_to_x(l, s, i, ("proj", l, s))

            def ffn_out(s, i):
                add_to_x(1, s, i, ("out", 1, s, 0))

            def cycle_out(s, i):
                add_to_x(5, s, i, ("cyo", s))

            def expert_out(l, s, e, i):
                dve.wait_ge(*filled[i].at("out", l, s, e))
                for t in range(NT):
                    last = v.scalar_tensor_tensor(x[:, s, t, :], slot(i, 128, at=128 * t),
                                                  gt[:, s, 7, E * t + e:E * t + e + 1], x[:, s, t, :],
                                                  ALU.mult, ALU.add)
                last.then_inc(*free[i].mark("out", l, s, e))
                dve.wait_ge(*free[i].at("out", l, s, e))

            def values1(s, c, h, i):
                if h == 0:
                    return
                p = KEYS if c == 4 else 128
                dve.wait_ge(*filled[i].at("v1", s, c, h))
                v.tensor_copy(v1[0:p, c, 512 * h:512 * h + 512], slot(i, 512, p)).then_inc(*free[i].mark("v1", s, c, h))

            def keys1(s, h, i):
                dve.wait_ge(*filled[i].at("k1", s, h))
                v.tensor_scalar(kh[:, h % 2, :], slot(i, L), V("bk1", h), None, ALU.add).then_inc(*free[i].mark("k1", s, h))

            def softmax1(s, h, t, i):
                k = 4 * (h % 2) + t
                dve.wait_ge(*filled[i].at("s1", s, h, t))
                v.tensor_reduce(nmax[:, t, 0:1], slot(i, 589), AX, ALU.max, negate=True).then_inc(*nmax_ready.mark(s, h, t))
                if t or h:
                    scale_row(s, *((h, t - 1) if t else (h - 1, 3)))

            def scale_row(s, h, t):
                k = 4 * (h % 2) + t
                dve.wait_ge(*reader_did("s1", s, h, t))
                link(v.reciprocal(rsum[:, t, 1, 0:1], rsum[:, t, 0, 0:1]))
                v.tensor_scalar(row_probs[k], row_probs[k], rsum[:, t, 1, 0:1], None, ALU.mult)\
                    .then_inc(*probs1_ready.mark(s, h, t))

            def turn_probs1(s, h, c, i):
                if h == H1 - 1 and c == 0:
                    scale_row(s, H1 - 1, 3)
                if c % 2 == 0:
                    return
                dve.wait_ge(*filled[i].at("tp1", s, h, c))
                v.tensor_copy(pT1[h % 2][:, c, :], slot(i, 512)).then_inc(*free[i].mark("tp1", s, h, c))

            def mix_values1(s, h, i):
                dve.wait_ge(*filled[i].at("pv1", s, h))
                v.tensor_scalar(oT[:, h, :], slot(i, L), V("bv1", h), None, ALU.add).then_inc(*free[i].mark("pv1", s, h))

            def logits(l, s, i):
                dve.wait_ge(*filled[i].at("logits", l, s))
                lg = slot(i, NT * E).rearrange("p (t e) -> p t e", t=NT)
                mx = gt[:, s, 2, 0:NT]
                link(v.tensor_reduce(mx, lg, AX, ALU.max, negate=True))
                v.tensor_tensor(gt[:, s, 0, :].rearrange("p (t e) -> p t e", t=NT), lg,
                                mx.unsqueeze(2).broadcast_to([128, NT, E]), ALU.add).then_inc(*free[i].mark("logits", l, s))

            def gates(l, s):
                te = "p (t e) -> p t e"
                p3 = gt[:, s, 3, :].rearrange(te, t=NT)
                by_j = gt[:, s, 3, :].rearrange(te, t=NT).unsqueeze(2).broadcast_to([128, NT, E, E])
                by_e = gt[:, s, 3, :].rearrange(te, t=NT).unsqueeze(3).broadcast_to([128, NT, E, E])
                c = [cmp[:, n, :].rearrange("p (t e j) -> p t e j", t=NT, e=E) for n in range(3)]
                rank = gt[:, s, 4, :].rearrange(te, t=NT)
                tmp = gt[:, s, 5, :].rearrange(te, t=NT)
                out = gt[:, s, 7, :].rearrange(te, t=NT)
                one = gt[:, s, 2, 0:NT]
                need(dve, "before")
                dve.wait_ge(*gate_exp.at(l, s))
                link(v.tensor_reduce(one, gt[:, s, 1, :].rearrange(te, t=NT), AX, ALU.add))
                link(v.reciprocal(gt[:, s, 2, NT:2 * NT], one))
                link(v.tensor_tensor(p3, gt[:, s, 1, :].rearrange(te, t=NT),
                                     gt[:, s, 2, NT:2 * NT].unsqueeze(2).broadcast_to([128, NT, E]), ALU.mult))
                v.tensor_tensor(c[0], by_j, by_e, ALU.is_gt)
                link(v.tensor_tensor(c[1], by_j, by_e, ALU.is_equal))
                tri = W["before"].rearrange("p (e j) -> p e j", e=E).unsqueeze(1).broadcast_to([128, NT, E, E])
                link(v.tensor_tensor(c[1], c[1], tri, ALU.mult))
                link(v.tensor_tensor(c[0], c[0], c[1], ALU.add))
                link(v.tensor_reduce(rank, c[0], AX, ALU.add))
                if l == 3:
                    link(v.scalar_tensor_tensor(tmp, rank, 2.0, p3, ALU.is_lt, ALU.mult))
                    link(v.tensor_reduce(one, tmp, AX, ALU.add))
                    link(v.reciprocal(gt[:, s, 2, NT:2 * NT], one))
                    link(v.scalar_tensor_tensor(out, tmp, gates_t[:, l:l + 1],
                                                gt[:, s, 2, NT:2 * NT].unsqueeze(2).broadcast_to([128, NT, E]),
                                                ALU.mult, ALU.mult))
                else:
                    link(v.tensor_tensor(c[2], c[0], by_j, ALU.mult))
                    link(v.tensor_reduce(tmp, c[2], AX, ALU.add))
                    link(v.tensor_tensor(tmp, tmp, p3, ALU.add))
                    link(v.tensor_scalar(tmp, tmp, 0.8, None, ALU.is_lt))
                    link(v.tensor_scalar(rank, rank, 1.0, None, ALU.is_lt))
                    link(v.tensor_tensor(tmp, tmp, rank, ALU.max))
                    v.scalar_tensor_tensor(out, tmp, gates_t[:, l:l + 1], p3, ALU.mult, ALU.mult)\
                        .then_inc(*gate_ready.mark(l, s))
                    dve.wait_ge(*gate_ready.at(l, s))

            def gate_bias(s, i):
                dve.wait_ge(*filled[i].at("gT", s))
                v.tensor_copy(gT[:, :], slot(i, 512, E)).then_inc(*free[i].mark("gT", s))
                dve.wait_ge(*filled[i].at("gb", s))
                xs = x[:, s, :, :].rearrange("p t d -> p (t d)")
                v.tensor_tensor(xs, slot(i, L), xs, ALU.add).then_inc(*free[i].mark("gb", s))
                dve.wait_ge(*free[i].at("gb", s))

            def project_heads(l, s, i, j, k):
                dve.wait_ge(*filled[i].at("kv", l, s))
                rt = rot[s]
                kk = rt[:, 1, 0:KEYS]
                if l == 4:
                    v.tensor_tensor(kk, slot(i, KEYS), W["cos"][:, 0:KEYS], ALU.mult)
                    link(v.tensor_tensor(rt[:, 1, 128:128 + KEYS], slot(i, KEYS, at=KEYS), W["sin"][:, 0:KEYS], ALU.mult))
                    v.tensor_tensor(kk, kk, rt[:, 1, 128:128 + KEYS], ALU.add).then_inc(*keys_ready.mark(l, s))
                else:
                    v.tensor_scalar(kk, slot(i, KEYS), V("kb3"), None, ALU.add).then_inc(*keys_ready.mark(l, s))
                if l == 4:
                    dve.wait_ge(*vpad_clear.at(s))
                for a in range(4):
                    last = v.tensor_copy(vpad[s][0:KEYS, :, :].rearrange("p (g j) c -> p g j c", g=4)[:, :, a, 8 * a:8 * a + 8],
                                         slot(i, 128, KEYS, at=256).rearrange("p (g c) -> p g c", g=4)[:, :, 8 * a:8 * a + 8])
                last.then_inc(*free[i].mark("kv", l, s))
                dve.wait_ge(*filled[j].at("q", l, s))
                if l == 4:
                    v.tensor_tensor(rt[:, 0, :], slot(j, L), W["cos"], ALU.mult).then_inc(*free[j].mark("q", l, s))
                    dve.wait_ge(*filled[k].at("qr", l, s))
                    dve.wait_ge(*free[j].at("q", l, s))
                    dve.wait_ge(*heads_ready.at(l, s))
                    v.tensor_tensor(rt[:, 1, :], slot(k, L), W["sin"], ALU.mult).then_inc(*free[k].mark("qr", l, s))
                    dve.wait_ge(*free[k].at("qr", l, s))
                    v.tensor_tensor(rt[:, 0, :], rt[:, 0, :], rt[:, 1, :], ALU.add).then_inc(*rotated.mark(l, s))
                else:
                    v.tensor_scalar(rt[:, 0, :], slot(j, L), V("qb3"), float(8 ** -0.5), ALU.add, ALU.mult)\
                        .then_inc(*free[j].mark("q", l, s))

            def global_net(s, i):
                dve.wait_ge(*reader_did("norm", 5, s))
                link(v.tensor_reduce(gl[:, s, 4:5], xnT[:, s, :], AX, ALU.add))
                v.tensor_scalar(gl[:, s, 0:1], gl[:, s, 4:5], 1.0 / L, None, ALU.mult).then_inc(*mean_ready.mark(s))
                dve.wait_ge(*reader_did("g", s, 2))
                link(v.tensor_scalar(gl[:, s, 5:6], gl[:, s, 3:4], scaled[:, 12:13], 0.1, ALU.mult, ALU.add))

            def couple(s, c, i):
                src = xnT[:, s, :] if c == 0 else cur[:, s, :]
                th = net[:, 4 * s + 3, :]
                dve.wait_ge(*reader_did("cy", s, c, 3))
                link(v.tensor_scalar(th, th, scaled[:, 13:14], gl[:, s, 5:6], ALU.mult, ALU.add))
                dve.wait_ge(*filled[i].at("cy", s, c, 4))
                v.tensor_tensor(th, slot(i, L), th, ALU.mult).then_inc(*free[i].mark("cy", s, c, 4))
                dve.wait_ge(*free[i].at("cy", s, c, 4))
                v.tensor_tensor(cur[:, s, :], src, th, ALU.add).then_inc(*coup_ready.mark(s, c))

            parts = dict(norm_stats=norm_stats, norm_again=norm_again, norm_apply=norm_apply, media_norm=media_norm,
                         values0=values0, head_norm=head_norm, head_scale=head_scale, less_max=less_max, normalise=normalise,
                         project=project, ffn_out=ffn_out, cycle_out=cycle_out, expert_out=expert_out,
                         values1=values1, keys1=keys1, softmax1=softmax1, turn_probs1=turn_probs1,
                         mix_values1=mix_values1, logits=logits, gates=gates, gate_bias=gate_bias,
                         project_heads=project_heads, global_net=global_net, couple=couple)

            for i in range(6):
                dve.sem_inc(free[i].sem, 1)
            dve.sem_inc(stored.sem, 16)
            v.memset(ones[:], 1.0).then_inc(consts_ready.sem, 1)
            v.memset(low[:], NEG).then_inc(consts_ready.sem, 1)
            v.memset(arenaB[:], 0.0).then_inc(consts_ready.sem, 1)
            dve.wait_ge(loaded_small.sem, 16 * NSMALL)
            v.tensor_scalar(mask[:], mask[:], 0, None, ALU.is_equal).then_inc(consts_ready.sem, 1)
            a = vcols["qw"][0]
            v.tensor_scalar(scaled[:, 0:2], vec[:, a:a + 2], 0.125, None, ALU.mult).then_inc(centred_small.sem, 1)
            a = vcols["bq1"][0]
            v.tensor_scalar(scaled[:, 2:10], vec[:, a:a + 8], float(128 ** -0.5), None, ALU.mult).then_inc(centred_small.sem, 1)
            v.tensor_scalar(scaled[:, 10:11], V("cb4"), 0.5, None, ALU.mult).then_inc(centred_small.sem, 1)
            v.tensor_scalar(scaled[:, 11:12], V("gb3"), 0.5, None, ALU.mult).then_inc(centred_small.sem, 1)
            v.tensor_scalar(scaled[:, 12:13], V("ar"), 0.7, None, ALU.mult).then_inc(centred_small.sem, 1)
            v.tensor_scalar(scaled[:, 13:14], V("ar"), 0.3, None, ALU.mult).then_inc(centred_small.sem, 1)
            dve.wait_ge(centred_small.sem, 6)
            dve.sem_inc(consts_ready.sem, 1)
            need(dve, "wq0")
            for n, w in enumerate(("wk0", "wq0")):
                w3 = W[w].rearrange("p (h d) -> p h d", h=16)
                v.tensor_reduce(centre[:], w3, AX, ALU.add).then_inc(centring.sem, 1)
                dve.wait_ge(centring.sem, 3 * n + 1)
                v.tensor_scalar(centre[:], centre[:], -1.0 / DH0, None, ALU.mult).then_inc(centring.sem, 1)
                dve.wait_ge(centring.sem, 3 * n + 2)
                v.tensor_tensor(w3, w3, centre[:].unsqueeze(2).broadcast_to([128, 16, DH0]), ALU.add)\
                    .then_inc(centring.sem, 1)
                dve.wait_ge(centring.sem, 3 * n + 3)
                dve.sem_inc(centred.sem, 1)
            dve.wait_ge(gates_tanh.sem, 1)
            dve.wait_ge(consts_ready.sem, 6)
            with dve.Fori(0, PAIRS) as pair:
                it[0] = pair
                for kind, args in steps:
                    if kind in parts:
                        parts[kind](*args)
            it[0] = 0
    for name, sg in signals.items():
        known[name].update(sg.seen)
        known[name]["total"] = sg.n
    for i in range(6):
        assert signals[f"filled_{i}"].seen.keys() == signals[f"free_{i}"].seen.keys()


def kernel(**inputs):
    import numpy as _np
    import concourse.bacc as _bacc
    from concourse.bass_utils import run_bass_kernel_spmd as _run

    a = {k: _np.asarray(v) for k, v in inputs.items()}

    def padded(w, n=None):
        out = _np.zeros((128, n or w.shape[1]), _np.float32)
        out[:w.shape[0], :w.shape[1]] = w
        return out

    def experts_in(w):
        return w.transpose(1, 0, 2).reshape(D, -1)

    def rows_by_tile(w):
        return w.reshape(-1, 128, w.shape[-1]).transpose(1, 0, 2).reshape(128, -1)

    heads = _np.arange(D)
    wkv = a["L2_xattn_Wkv"].reshape(16, 2, 8, D)
    wk2, wv2 = wkv[:, 0].reshape(D, D), wkv[:, 1].reshape(D, D)
    swap = heads ^ 1
    pos = _np.arange(L, dtype=_np.float32)[None, :]
    theta = _np.power(_np.float32(10000), _np.float32(2) * ((heads % 8) // 2).astype(_np.float32) / _np.float32(8))
    ang = (pos / theta[:, None]).astype(_np.float32)
    sign = _np.where(heads % 2 == 0, -1, 1).astype(_np.float32)[:, None]
    twist = _np.zeros((128, 128), _np.float32)
    q = _np.arange(32)
    twist[64 + q, q] = 1
    twist[96 + q, 32 + q] = -1
    twist[q, 64 + q] = -1
    twist[32 + q, 96 + q] = 1
    before = _np.broadcast_to((_np.arange(8)[None, :] < _np.arange(8)[:, None]).astype(_np.float32).reshape(1, 64), (128, 64))
    block = (heads[:, None] // 8 == _np.arange(16)[None, :]).astype(_np.float32)
    w = {
        "ident": _np.eye(128, dtype=_np.float32),
        "wq0": a["L0_xattn_Wq"].T, "wk0": a["L0_xattn_Wk"].T, "wv0": a["L0_xattn_Wv"].T,
        "wu0": rows_by_tile(a["L0_xattn_Wu"].T), "f0a": a["L0_ffn_W1"], "f0b": rows_by_tile(a["L0_ffn_W2"]),
        "wq1": a["L1_xattn_Wq"], "wk1": a["L1_xattn_Wkv"][:, :1024], "wv1": a["L1_xattn_Wkv"][:, 1024:],
        "wo1": rows_by_tile(a["L1_xattn_Wo"]),
        "gate1": a["L1_ffn_gate_w"],
        "wq2": a["L2_xattn_Wq"].T, "wqr2": a["L2_xattn_Wq"][swap].T, "wk2": wk2.T, "wkr2": wk2[swap].T, "wv2": wv2.T,
        "wo2": a["L2_xattn_Wo"].T,
        "cw1": a["L2_ffn_cn_w1"], "cw2": padded(a["L2_ffn_cn_w2"], 128), "cw3": padded(a["L2_ffn_cn_w3"], 128),
        "cw4": padded(_np.tile(a["L2_ffn_cn_w4"], (1, 128))), "gw1": a["L2_ffn_gc_w1"], "gw2": padded(a["L2_ffn_gc_w2"]),
        "gw3": padded(_np.tile(a["L2_ffn_gc_w3"], (1, 128))),
        "twist": twist, "cos": _np.cos(ang), "sin": _np.sin(ang) * sign, "block": block, "before": before,
        "wq3": a["L3_xattn_wq_w"].T, "wk3": a["L3_xattn_wk_w"].T, "wv3": a["L3_xattn_wv_w"].T, "wo3": a["L3_xattn_wo_w"].T,
        "gate3": a["L3_ffn_Wr"],
    }

    def col(v):
        v = v.reshape(-1)
        return padded(v[:, None]) if v.size < 128 else v.reshape(-1, 128).T

    def same(v):
        return _np.tile(v.reshape(1, -1), (128, 1))

    gates = _np.stack([a["g_xattn"], a["g_ffn"]], 1).reshape(-1)
    vecs = {
        "qw": col(_np.tile(a["L0_xattn_qn_w"], 2)), "qb": col(_np.tile(a["L0_xattn_qn_b"], 2)),
        "kw": col(_np.tile(a["L0_xattn_kn_w"], 2)), "kb": col(_np.tile(a["L0_xattn_kn_b"], 2)),
        "b1_0": col(a["L0_ffn_b1"]), "gm": col(a["L1_xattn_gamma_media"]), "bm": col(a["L1_xattn_beta_media"]),
        "gl": col(a["L1_xattn_gamma_lat"]), "bl": col(a["L1_xattn_beta_lat"]), "bq1": col(a["L1_xattn_bq"]),
        "bk1": col(a["L1_xattn_bkv"][:1024]), "bv1": col(a["L1_xattn_bkv"][1024:]),
        "cb1": col(a["L2_ffn_cn_b1"]), "cb2": col(a["L2_ffn_cn_b2"]), "cb3": col(a["L2_ffn_cn_b3"]),
        "cb4": same(a["L2_ffn_cn_b4"]), "gb1": col(a["L2_ffn_gc_b1"]), "gb2": col(a["L2_ffn_gc_b2"]),
        "gb3": same(a["L2_ffn_gc_b3"]), "ar": same(a["L2_ffn_adaptive_range"]),
        "qb3": col(a["L3_xattn_wq_b"]), "kb3": col(a["L3_xattn_wk_b"]), "vb3": col(a["L3_xattn_wv_b"]),
        "b1_3": col(a["L3_ffn_b1"]), "g": same(gates),
    }
    rws = _np.zeros((E, sum(n for _, n in ROWS)), _np.float32)
    at = columns(ROWS)[0]
    for name, v in (("bu", a["L0_xattn_bu"]), ("b2_0", a["L0_ffn_b2"]), ("bo1", a["L1_xattn_bo"]),
                    ("bo3", a["L3_xattn_wo_b"]), ("br3", a["L3_ffn_br"])):
        rws[0, at[name][0]:at[name][0] + at[name][1]] = v
    rws[:, at["b2_3"][0]:at["b2_3"][0] + 128] = a["L3_ffn_b2"]
    mask = a["mask_1x1xSxS2_ik0"].reshape(NT, 128, KEYS).transpose(1, 0, 2).reshape(128, NT * KEYS)
    arrays = {
        "x": a["x"].reshape(B * NT, 128, D).transpose(1, 0, 2).reshape(128, -1),
        "ctxT": a["ctx_1024"].transpose(2, 0, 1).reshape(D, -1),
        "ctx": a["ctx_1024"].transpose(1, 0, 2).reshape(KEYS, -1),
        "vec": _np.concatenate([vecs[n] for n, _ in VECS], 1),
        "rows": rws, "mask": mask,
        "w_moe1": _np.concatenate([experts_in(a["L1_ffn_fc_w"]), rows_by_tile(a["L1_ffn_proj_w"].reshape(-1, 128))], 1),
        "w_moe3": _np.concatenate([experts_in(a["L3_ffn_W1"]), rows_by_tile(a["L3_ffn_W2"].reshape(-1, 128))], 1),
    }
    for g, parts in W_GROUPS:
        arrays["w_" + g] = _np.concatenate([w[n] for n, _ in parts], 1)
    arrays = {k: _np.ascontiguousarray(v) for k, v in arrays.items()}

    known = {}
    for final in (False, True):
        nc = _bacc.Bacc("TRN2", target_bir_lowering=False, num_devices=1)
        dram = {k: nc.dram_tensor(f"in_{k}_dram", v.shape, mybir.dt.from_np(v.dtype), kind="ExternalInput").ap()
                for k, v in arrays.items()}
        dram["out"] = nc.dram_tensor("out_dram", (128, B * L), F32, kind="ExternalOutput").ap()
        program(nc, dram, known)
    r = _run(nc, [{f"in_{k}_dram": v for k, v in arrays.items()}], core_ids=[0])
    out = r.results[0]["out_dram"]
    return out.reshape(128, B * NT, D).transpose(1, 0, 2).reshape(B, L, D)
```

```python
from contextlib import ExitStack

import numpy as np

import concourse.bass as bass
from concourse import mybir

B, L, D = 4, 512, 128
PAIRS, NS = 2, 2
NT = L // 128
KEYS = 77
CHUNKS = 5
ROWS8 = 8 * KEYS
H0, DH0 = 16, 64
H1 = 8
E, FT = 8, 4
PC = 8
EPS = 1e-5
NEG = -1e9

ALU = mybir.AluOpType
ACT = mybir.ActivationFunctionType
F32 = mybir.dt.float32
I32 = mybir.dt.int32
AX = mybir.AxisListType.X

W_FIRST = [("ident", 128), ("own_head", 40), ("wk0", 1024)]
W_SECOND = [("wv0", 1024), ("wq0", 1024)]
W_REST0 = [("wu0", 1024), ("f0a", 512), ("f0b", 512)]
W_L1 = [("wq1", 1024), ("wk1", 1024), ("wv1", 1024), ("wo1", 1024)]
W_MOE = [("fc", 4096), ("pj", 4096)]
W_L2 = [("wq2", 128), ("wqr2", 128), ("wk2", 128), ("wkr2", 128), ("wv2", 128), ("wo2", 128),
        ("cw1", 128), ("cw2", 128), ("cw3", 128), ("cw4", 128), ("gw1", 64), ("gw2", 32), ("gw3", 128),
        ("twist", 128), ("cos", 512), ("sin", 512), ("block", 16), ("before", 64), ("gate1", 8)]
W_L3 = [("wq3", 128), ("wk3", 128), ("wv3", 128), ("wo3", 128), ("gate3", 8)]
W_GROUPS = [("first", W_FIRST), ("second", W_SECOND), ("rest0", W_REST0), ("l1", W_L1), ("l2", W_L2), ("l3", W_L3)]
VECS = [("qw", 1), ("qb", 1), ("kw", 1), ("kb", 1), ("b1_0", 4), ("gm", 1), ("bm", 1), ("gl", 1), ("bl", 1),
        ("bq1", 8), ("bk1", 8), ("bv1", 8), ("cb1", 1), ("cb2", 1), ("cb3", 1), ("cb4", 1), ("gb1", 1),
        ("gb2", 1), ("gb3", 1), ("ar", 1), ("qb3", 1), ("kb3", 1), ("b1_3", 32), ("g", 8)]
ROWS = [("bu", 128), ("b2_0", 128), ("bo1", 128), ("bo3", 128), ("vb3", 128), ("b2_3", 128), ("br3", 8)]


def columns(parts):
    at, out = 0, {}
    for name, n in parts:
        out[name] = (at, n)
        at += n
    return out, at


class Signal:

    def __init__(self, sem, known, it, name, order=None, credit=0):
        self.sem, self.known, self.it, self.credit = sem, known.setdefault(name, {}), it, credit
        self.order = known.setdefault(order or name, {})
        self.n = 0
        self.seen = {}

    def mark(self, *event):
        self.n += 1
        assert event not in self.seen
        self.seen[event] = self.n
        return self.sem, 1

    def at(self, *event):
        return self.value(self.order.get(event, 1) + self.credit)

    def value(self, n):
        it = self.it[0]
        return (self.sem, it * self.known.get("total", 0) + n)


S0, S1, T0, T1, G0, G1 = range(6)
TILES0 = [(s, k) for s in range(NS) for k in (4, 0, 1, 2, 3)]


def in_parts(l, s, e):
    return l in (3, 7) and (s, e) not in ((0, 0), (0, 1))


PARTED = [(l, s, e) for l in (3, 7) for s in range(2) for e in range(E) if in_parts(l, s, e)]


class Rotor:

    def __init__(self, *slots):
        self.slots, self.n = slots, 0

    def __call__(self):
        self.n += 1
        return self.slots[(self.n - 1) % len(self.slots)]


def schedule():
    big, turn, gen = Rotor(S0, S1), Rotor(T0, T1), Rotor(G0, G1)
    wide = Rotor(S0, S1, T0, T1)
    st = []

    def do(kind, *args):
        st.append((kind, args))

    def norm_stats(l, s):
        do("norm_stats", l, s)

    def norm_apply(l, s):
        if l == 2:
            do("norm_again", l, s)
        do("norm_apply", l, s)

    def norm(l, s):
        norm_stats(l, s)
        norm_apply(l, s)

    def norm_turn(l, s):
        do("norm_turn", l, s, gen())

    def gates(l, s, part):
        do("gates", l, s, part)

    def hidden(l, s, e, *fs):
        for f in fs or range(FT):
            do("hidden", l, s, e, f, wide())

    def choosing(l, s):
        return {0: (lambda: norm_stats(l, s),), 1: (lambda: norm_apply(l, s),), 2: (lambda: norm_turn(l, s),),
                3: (lambda: do("split_tokens", l, s), lambda: do("logits", l, s, gen()), lambda: gates(l, s, 0)),
                4: (lambda: gates(l, s, 1),), 5: (lambda: gates(l, s, 2),)}

    def small_attention(l, between={}):
        units = [(s, hf, t) for s in range(NS) for t in range(NT) for hf in range(2)]
        n, late, slots = len(units), 5, {}
        lag = 3 if l == 0 else 2
        for k in range(n + late):
            for step in between.get(k, ()) if k < n else ():
                step()
            if k < n:
                slot = big()
                do("scores", l, *units[k], slot)
                do("less_max", l, *units[k], slot, k)
                slots[k] = slot
            if 1 <= k < n + 1:
                do("exp", l, *units[k - 1], slots[k - 1], k - 1)
            if l == 0 and 1 <= k < n + 1:
                do("normalise", l, *units[k - 1], k - 1)
            if k == 8 + late:
                norm_stats(l + 1, 0)
            if k == 9 + late:
                norm_apply(l + 1, 0)
            if k >= 5 and k % 2 and l:
                s, _, t = units[k - 4]
                do("turn_heads", l, s, t, gen())
            if k >= late and (k - late) % 2:
                s, _, t = units[k - late]
                do("project_tile", l, s, t, gen())
            if lag < k < n + lag + 1:
                do("mix_values", l, *units[k - lag - 1], k - lag - 1, gen())
            for step in between.get(k, ()) if k >= n else ():
                step()
            if lag <= k < n + lag:
                for r in range(2):
                    do("turn_probs", l, *units[k - lag], k - lag, r, turn())

    for s in range(NS):
        do("repeat_context", s)
    norm(0, 0)
    for s in range(NS):
        do("clear_keys0", s)

    def values0(s):
        for h in range(2):
            do("values0", s, h, big())

    values0(0)
    tiles = TILES0
    for n in range(len(tiles) + 2):
        if n < len(tiles):
            slot = big()
            do("queries0", *tiles[n], slot)
        if n == 0:
            norm_turn(0, 0)
        if n == 3:
            norm_stats(0, 1)
        if n == 4:
            norm_apply(0, 1)
        if n == 5:
            norm_turn(0, 1)
        if 1 <= n < len(tiles) + 1:
            do("head_scale", *tiles[n - 1], n - 1, before)
        if n < len(tiles):
            do("head_norm", *tiles[n], slot)
        if n >= 2:
            for h in range(2):
                do("turn_queries", *tiles[n - 2], n - 2, h, turn())
        if n < len(tiles):
            do("head_root", *tiles[n])
        before = slot
    for s in range(NS):
        do("media_norm", s)
    small_attention(0, {1: (lambda: values0(1),),
                        2: (lambda: do("media_turn", 0, gen()), lambda: do("media_turn", 1, gen())),
                        3: (lambda: do("media_keys1", 0, 0, gen()), lambda: do("media_keys1", 0, 1, gen())),
                        4: (lambda: do("media_keys1", 1, 0, gen()), lambda: do("media_keys1", 1, 1, gen())),
                        15: (lambda: norm_turn(1, 0),), 16: (lambda: hidden(1, 0, 0, 0),), 17: (lambda: hidden(1, 0, 0, 1),),
                        18: (lambda: hidden(1, 0, 0, 2),), 19: (lambda: hidden(1, 0, 0, 3),)})
    norm(1, 1)
    do("ffn_out", 0, gen())
    norm(2, 0)
    norm_turn(1, 1)
    hidden(1, 1, 0)
    do("ffn_out", 1, gen())

    def values1(s):
        return [("values1", s, c, h) for c in (4, 0, 1, 2, 3) for h in range(2)]

    def heads1(s, h):
        do("queries1", s, h, gen())
        do("keys1", s, h, gen())

    units = [(s, h, t) for s in range(NS) for h in range(H1) for t in range(NT)]
    n, half = len(units), H1 * NT
    norm_turn(2, 0)
    for step in values1(0):
        do(*step, gen())
    heads1(0, 0)
    for k in range(n + 5):
        if k < n:
            do("scores1", *units[k], big())
            do("softmax1", *units[k], k, st[-1][1][-1])
        if k == 3:
            norm_stats(2, 1)
        if k == 4:
            norm_apply(2, 1)
        if k == half // 4:
            norm_turn(2, 1)
        if 0 <= k - half // 4 - 4 < 10:
            do(*values1(1)[k - half // 4 - 4], gen())
        for s in range(NS):
            if 0 <= k - half * (s + 1) - 3 < NT:
                do("project_tile", 2, s, k - half * (s + 1) - 3, gen())
        if k == half + 9:
            norm_stats(3, 0)
        if k == half + 10:
            norm_apply(3, 0)
        if 3 <= k < n + 3:
            do("mix_values1", *units[k - 3], k - 3, gen())
        if k % NT == 1 and k + NT - 1 < n:
            heads1(*units[k + NT - 1][:2])
        if 2 <= k < n + 2:
            for r in range(2):
                do("turn_probs1", *units[k - 2], k - 2, r, turn())
        if k == half + 12:
            norm_turn(3, 0)
        if k == half + 13:
            do("logits", 3, 0, gen())
        if 0 <= k - half - 14 < 3:
            gates(3, 0, k - half - 14)
        if n < k < n + 5:
            hidden(3, 0, (k - n - 1) // 2, *((0, 1), (2, 3))[(k - n - 1) % 2])
    for t in range(2, NT):
        do("project_tile", 2, 1, t, gen())

    def moe(l, s, between={}):
        for e in range(E + 1):
            if s == 0 and e == 0:
                do("split_tokens", l, 0)
            if e + 1 < E and in_parts(l, s, e + 1):
                do("split_weights", l, s, e + 1)
            if s == 0 and e == E - 1:
                do("split_weights", l, 1, 0)
            if e < E and (s or e > 1):
                hidden(l, s, e)
            for step in between.get(e, ()):
                step()
            if e in (2, 3) and l == 7:
                do(("turn_gates", "gate_bias")[e - 2], s, gen())
            if e:
                do("expert_out", l, s, e - 1, gen())

    moe(3, 0, choosing(3, 1))
    moe(3, 1, {0: (lambda: norm_stats(4, 0), lambda: do("sum_columns", 0), lambda: do("sum_columns", 1)),
               1: (lambda: norm_apply(4, 0),), 3: (lambda: norm_turn(4, 0),),
               4: (lambda: do("project_heads", 4, 0, gen(), turn(), turn(), big()),)})
    twists = {}

    def cycle(s, n):
        c, stage = n // 5, n % 5
        if stage == 4:
            twists[s] = gen()
            do("cycle", s, c, 4, 0, twists[s])
        for half in range(2):
            if stage < 4:
                do("cycle", s, c, stage, half, wide())
            else:
                do("couple", s, c, half, twists[s])

    small_attention(4, {2: (lambda: norm_stats(4, 1),), 3: (lambda: norm_apply(4, 1),), 5: (lambda: norm_turn(4, 1),),
                        6: (lambda: do("project_heads", 4, 1, gen(), gen(), turn(), big()),),
                        15: (lambda: norm_turn(5, 0),), 17: (lambda: cycle(0, 0), lambda: do("global_net", 0, 0, gen())),
                        18: (lambda: cycle(0, 1), lambda: do("global_net", 0, 1, gen())),
                        19: (lambda: cycle(0, 2), lambda: do("global_net", 0, 2, gen())),
                        20: (lambda: do("global_net", 0, 3, None), lambda: cycle(0, 3))})
    late = 7
    for n in range(4, 15 + late):
        if n < 15:
            cycle(0, n)
        if n == 4:
            norm_stats(5, 1)
        if n == 5:
            norm_apply(5, 1)
        if n == 6:
            norm_turn(5, 1)
        if n == 15:
            do("cycle_out", 0, gen())
        if n >= late:
            cycle(1, n - late)
        if n == 16:
            norm_stats(6, 0)
        if n == 17:
            norm_apply(6, 0)
        if 0 <= n - late < 4:
            do("global_net", 1, n - late, gen() if n - late < 3 else None)
        if n == 19:
            norm_turn(6, 0)
        if n == 20:
            do("project_heads", 6, 0, gen(), turn(), turn(), big())
    small_attention(6, {1: (lambda: do("cycle_out", 1, gen()),), 2: (lambda: norm_stats(6, 1),),
                        3: (lambda: norm_apply(6, 1),), 5: (lambda: norm_turn(6, 1),),
                        6: (lambda: do("project_heads", 6, 1, gen(), gen(), turn(), big()),),
                        15: (lambda: norm_turn(7, 0),), 16: (lambda: hidden(7, 0, 0, 0, 1), lambda: do("logits", 7, 0, gen())),
                        17: (lambda: gates(7, 0, 0), lambda: hidden(7, 0, 0, 2)),
                        18: (lambda: gates(7, 0, 1), lambda: hidden(7, 0, 0, 3), lambda: hidden(7, 0, 1, 0)),
                        19: (lambda: gates(7, 0, 2), lambda: hidden(7, 0, 1, 1, 2)),
                        20: (lambda: hidden(7, 0, 1, 3),)})
    moe(7, 0, choosing(7, 1))
    moe(7, 1)
    return st


def program(nc, dram, known):
    steps = schedule()
    it = [0]
    signals = {}
    with ExitStack() as ctx:
        def sb(name, shape, dt=F32):
            return ctx.enter_context(nc.sbuf_tensor(name, shape, dt))

        def signal(name, order=None, credit=0):
            signals[name] = Signal(ctx.enter_context(nc.semaphore(name)), known, it, name, order, credit)
            return signals[name]

        W = {}
        group_of = {}
        group_tiles = {}
        for gname, parts in W_GROUPS:
            cols, total = columns(parts)
            group_tiles[gname] = sb("w_" + gname, [128, total])
            for name, (a, n) in cols.items():
                W[name] = group_tiles[gname][:, a:a + n]
                group_of[name] = gname
        vcols, nv = columns(VECS)
        vec = sb("vec", [128, nv])
        rcols, nr = columns(ROWS)
        rows = sb("rows", [E, nr])

        def V(name, i=0, p=128):
            a = vcols[name][0] + i
            return vec[0:p, a:a + 1]

        def R(name, p=1):
            a, n = rcols[name]
            return rows[0:p, a:a + n]

        ident = W["ident"]
        ones = sb("ones", [1, 128])
        half_power = sb("half_power", [128, 16])
        low = sb("low", [128, 1])
        eps = sb("eps", [128, 1])
        mask = sb("mask", [128, NT * KEYS], I32)
        moe = sb("moe", [128, 8192])
        centre = sb("centre", [128, 16])
        scaled = sb("scaled", [128, 16])
        gates_t = sb("gates_t", [128, 8])
        x = sb("x", [128, NS, NT, 128])
        ctxT = sb("ctxT", [128, NS * KEYS])
        ctx_again = sb("ctx_again", [128, NS, 128 * CHUNKS])
        ctx_rows = sb("ctx_rows", [KEYS, NS, 128])
        xn = sb("xn", [128, NS, NT, 128])
        xnT = sb("xnT", [128, NS, L])
        stat = sb("stat", [128, NS, NT, 6])
        mv = sb("mv", [128, NS, NT, 2])
        ve = sb("ve", [128, NS, 2, NT])
        rs = sb("rs", [128, NS, 3, NT])
        mstat = sb("mstat", [KEYS, NS, 6])
        mmv = sb("mmv", [KEYS, NS, 4])
        mn = sb("mn", [KEYS, NS, 128])
        mnT = sb("mnT", [128, NS, KEYS])
        hn = sb("hn", [128, 5, 16])
        arenaA = sb("arenaA", [128, 5120])
        arenaB = sb("arenaB", [128, 5 * L])
        arenaD = sb("arenaD", [128, 5120])
        probs = sb("probs", [128, 4464])
        nmax = sb("nmax", [128, 4, 8])
        rsum = sb("rsum", [128, 4, 2, 8])
        qh = sb("qh", [128, 2, L])
        kh = sb("kh", [128, 2, L])
        kmedia = sb("kmedia", [128, NS, H1, KEYS])
        gt = sb("gt", [128, NS, 8, NT * E])
        gl = sb("gl", [128, NS, 8])
        with nc.sbuf_tensor("arenaC", [128, 8 * L], F32) as arenaC:
            pass
        parts_all = sb("parts", [128, 8 * L], mybir.dt.float32r)
        psum = ctx.enter_context(nc.psum_tensor("psum", [128, 8 * 512], F32))

        qT0 = [a[:, 0:4096].rearrange("p (m q) -> p m q", m=8) for a in (arenaA, moe)]
        sq = arenaC[:, 0:1024]
        qn = arenaC[:, 1024:3072].rearrange("p (i n) -> p i n", i=2)
        rot, cur = [qh, kh], kh
        W["fc"], W["pj"] = moe[:, 0:4096], moe[:, 4096:8192]
        own_head = W["own_head"].rearrange("p (c h) -> p c h", h=8)
        own_pair = [W["own_head"].rearrange("p (m n) -> p m n", n=10)[:, :, 8 * d:8 * d + 2] for d in range(2)]
        v0 = [a.rearrange("p (g m d r c) -> p g m d r c", g=2, m=4, d=2, r=2)
              for a in (arenaD[:, 0:4 * L], moe[:, 5376:5376 + 4 * L])]
        kbd0_flat = [probs[:, 2464:2464 + 16 * KEYS], moe[:, 4096:4096 + 16 * KEYS]]
        kbd0 = [a.rearrange("p (m r k) -> p m r k", m=8, r=2) for a in kbd0_flat]
        kbd = [arenaD[:, 1280 * s:1280 * s + 16 * KEYS].rearrange("p (h k) -> p h k", h=16) for s in range(NS)]
        vsum = [arenaD[:, 2560 + 720 * s:3280 + 720 * s].rearrange("p (c g n) -> p c g n", c=CHUNKS, g=2)
                for s in range(NS)]
        cmp = probs[:, 3696:3696 + 3 * NT * E * E].rearrange("p (n c) -> p n c", n=3)
        gT = arenaD[0:E, 4096:4096 + L]
        v1 = [a[:, :].rearrange("p (c n) -> p c n", c=5) for a in (arenaA, arenaD)]
        pT = [arenaB[:, i * 640:(i + 1) * 640].rearrange("p (c q) -> p c q", c=CHUNKS) for i in range(4)]
        oT = arenaC[:, :].rearrange("p (m q) -> p m q", m=8)
        hid = arenaA[:, 0:8 * L].rearrange("p (i f q) -> p i f q", i=2, f=FT)
        hid_after = arenaC[:, 0:4 * L].rearrange("p (f q) -> p f q", f=FT)
        F32R = mybir.dt.float32r

        def parts_at(a):
            return parts_all[:, a:a + 512], parts_all[:, a + 512:a + 1024]

        weight_parts = [parts_at(1024 * i) for i in range(2)]
        token_parts = [parts_at(2048 + 1024 * s) for s in range(NS)]
        net = arenaA[:, 0:8 * L].rearrange("p (i q) -> p i q", i=8)
        unit_probs = [probs[:, i * 616:(i + 1) * 616] for i in range(4)]
        row_probs = [probs[:, i * 589:(i + 1) * 589] for i in range(4)]

        def slot(i, cols=None, p=128, at=0, p0=0):
            base = 1024 * i if i < 2 else 2048 + 512 * (i - 2)
            cols = cols if cols is not None else (1024 if i < 2 else 512)
            return psum[p0:p0 + p, base + at:base + at + cols]

        def scores_of(i):
            return slot(i).rearrange("p (r c) -> p r c", r=2)[:, :, 0:4 * KEYS]

        loaded = {g: signal("loaded_" + g) for g, _ in W_GROUPS}
        held_dve = signal("held_dve")
        held_pe = signal("held_pe")
        loaded_moe = signal("loaded_moe")
        loaded_small = signal("loaded_small")
        loaded_x = [signal(f"loaded_x{s}") for s in range(NS)]
        loaded_ctx = signal("loaded_ctx")
        stored = [signal(f"stored_{s}") for s in range(NS)]
        consts_ready = signal("consts_ready")
        gates_tanh = signal("gates_tanh")
        centred = signal("centred")
        centring = signal("centring")
        centred_small = signal("centred_small")
        filled = [signal(f"filled_{i}") for i in range(6)]
        free = [signal(f"free_{i}", order=f"filled_{i}", credit=1) for i in range(6)]
        dve_step = signal("dve_step")
        stats_ready = signal("stats_ready")
        var_ready = signal("var_ready")
        rstd_ready = signal("rstd_ready")
        xn_ready = signal("xn_ready")
        mvar_ready = signal("mvar_ready")
        mrstd_ready = signal("mrstd_ready")
        mn_ready = signal("mn_ready")
        squares = signal("squares")
        hsum_ready = signal("hsum_ready")
        hroot_ready = signal("hroot_ready")
        exp_ready = signal("exp_ready")
        rsum_ready = signal("rsum_ready")
        probs_ready = signal("probs_ready")
        probs1_ready = signal("probs1_ready")
        nmax_ready = signal("nmax_ready")
        kbd0_clear = signal("kbd0_clear")
        sums_set = signal("sums_set")
        context_set = signal("context_set")
        unit_max = signal("unit_max")
        gate_exp = signal("gate_exp")
        high_part = signal("high_part")
        low_part = signal("low_part")
        gate_ready = signal("gate_ready")
        rotated = signal("rotated")
        heads_ready = signal("heads_ready")
        mean_ready = signal("mean_ready")
        coup_ready = signal("coup_ready")

        def unknown(signal, event):
            assert "total" not in known["filled_0"], event
            return signal.at(*event)

        def tensor_did(*event):
            for i in range(6):
                if event in known[f"filled_{i}"]:
                    return filled[i].at(*event)
            return unknown(filled[0], event)

        def reader_did(*event):
            for i in range(6):
                if event in known[f"filled_{i}"]:
                    return free[i].at(*event)
            return unknown(free[0], event)

        def need(eng, *names):
            for g in sorted({group_of[n] for n in names}):
                eng.wait_ge(loaded[g].sem, 16)

        def by_head(l, k):
            return l == 6 and k % 2 == 1

        def parts_free(eng, l, s, e):
            n = PARTED.index((l, s, e))
            if n >= 2 and PARTED[n - 2][0] == l:
                eng.wait_ge(*tensor_did("hid", *PARTED[n - 2], FT - 1))

        NSMALL = 3
        block = ctx.enter_context(nc.Block())

        @block.sync
        def _(sp):
            def load_x(s, at):
                sp.dma_start(x[:, s, :, :].rearrange("p t d -> p (t d)"), dram["x"][:, bass.ds(at * (NS * L) + s * L, L)])\
                    .then_inc(loaded_x[s].sem, 16)

            def load_context(at):
                sp.dma_start(ctxT[:], dram["ctxT"][:, bass.ds(at * (NS * KEYS), NS * KEYS)]).then_inc(loaded_ctx.sem, 16)
                sp.dma_start(ctx_rows[:].rearrange("p s d -> p (s d)"),
                             dram["ctx"][:, bass.ds(at * (NS * 128), NS * 128)]).then_inc(loaded_ctx.sem, 16)

            def pair_moves(pair, last):
                it[0] = pair
                sp.wait_ge(*tensor_did("pv", 0, 1, 1, NT - 1))
                sp.dma_start(moe[:], dram["w_moe1"]).then_inc(loaded_moe.sem, 16)
                sp.wait_ge(*reader_did("out", 3, 1, E - 1))
                sp.dma_start(moe[:], dram["w_moe3"]).then_inc(loaded_moe.sem, 16)
                if not last:
                    sp.wait_ge(*tensor_did("val", 6, 1))
                    load_context(pair + 1)
                for s in range(NS):
                    sp.wait_ge(*reader_did("out", 7, s, E - 1))
                    sp.dma_start(dram["out"][:, bass.ds(pair * (NS * L) + s * L, L)],
                                 x[:, s, :, :].rearrange("p t d -> p (t d)")).then_inc(stored[s].sem, 16)
                    if not last:
                        sp.wait_ge(stored[s].sem, pair * 16 + 16)
                        load_x(s, pair + 1)

            load_x(0, 0)
            load_context(0)
            sp.dma_start(vec[:], dram["vec"]).then_inc(loaded_small.sem, 16)
            sp.dma_start(rows[:], dram["rows"]).then_inc(loaded_small.sem, 16)
            sp.dma_start(mask[:], dram["mask"]).then_inc(loaded_small.sem, 16)
            load_x(1, 0)
            with sp.Fori(0, PAIRS - 1) as pair:
                pair_moves(pair, False)
            pair_moves(PAIRS - 1, True)
            it[0] = 0
            for s in range(NS):
                sp.wait_ge(stored[s].sem, 16 * PAIRS)

        @block.tensor
        def _(pe):
            used = [0] * 6

            def take(i):
                used[i] += 1
                pe.wait_ge(*free[i].value(used[i]))

            def read(i, *event):
                if event not in known[f"filled_{i}"]:
                    pe.wait_ge(*reader_did(*event))

            def mm(out, lhsT, rhs, start=True, stop=True):
                return nc.tensor.matmul(out, lhsT, rhs, start=start, stop=stop)

            def tr(out, in_, p):
                return nc.tensor.transpose(out, in_, ident[0:p, 0:p])

            def norm_turn(l, s, i):
                pe.wait_ge(*xn_ready.at(l, s))
                take(i)
                for t in range(NT):
                    last = tr(slot(i, 128, at=128 * t), xn[:, s, t, :], 128)
                last.then_inc(*filled[i].mark("norm", l, s))

            def values0(s, h, i):
                if s == 0 and h == 0:
                    pe.wait_ge(loaded_ctx.sem, it[0] * 32 + 32)
                    need(pe, "wv0")
                pe.wait_ge(*context_set.at(s))
                take(i)
                for m in range(4):
                    for d in range(2):
                        last = mm(slot(i, 128, at=128 * (2 * m + d)), ctx_again[:, s, 128 * (m + d):128 * (m + d + 1)],
                                  W["wv0"][:, 128 * (4 * h + m):128 * (4 * h + m + 1)])
                last.then_inc(*filled[i].mark("v0", s, h))

            def queries0(s, k, i):
                pe.wait_ge(centred.sem, 1 if k == 4 else 2)
                if k < 4:
                    read(i, "norm", 0, s)
                take(i)
                lhs, p, w = (ctxT[:, s * KEYS:(s + 1) * KEYS], KEYS, "wk0") if k == 4 else \
                    (xnT[:, s, k * 128:(k + 1) * 128], 128, "wq0")
                for h in range(2):
                    last = mm(slot(i, 512, p, 512 * h), lhs, W[w][:, h * 512:(h + 1) * 512])
                last.then_inc(*filled[i].mark("q0", s, k))

            def turn_queries(s, k, n, h, i):
                p = KEYS if k == 4 else 128
                read(i, "q0", s, k)
                take(i)
                for m in range(4):
                    c = 512 * h + 128 * m
                    last = tr(slot(i, p, at=128 * m), qn[0:p, n % 2, c:c + 128], p)
                last.then_inc(*filled[i].mark("tq", s, k, h))

            def scores(l, s, hf, t, i):
                if l == 0:
                    read(i, "tq", s, 3, 1)
                else:
                    pe.wait_ge(*(rotated.at(l, s) if l == 4 else reader_did("q", l, s)))
                    pe.wait_ge(*heads_ready.at(l, s))
                take(i)
                if l == 0:
                    for j in range(4):
                        m = 4 * hf + j
                        last = mm(slot(i, 2 * KEYS, at=512 * (j // 2) + 2 * KEYS * (j % 2)),
                                  qT0[s][:, m, t * 128:(t + 1) * 128], kbd0[s][:, m, :, :].rearrange("p r k -> p (r k)"))
                else:
                    for r in range(2):
                        h = 4 * (2 * hf + r)
                        last = mm(slot(i, 4 * KEYS, at=512 * r), rot[s][:, 0, t * 128:(t + 1) * 128],
                                  kbd[s][:, h:h + 4, :].rearrange("p j k -> p (j k)"))
                last.then_inc(*filled[i].mark("sc", l, s, hf, t))

            def turn_probs(l, s, hf, t, k, r, i):
                if by_head(l, k):
                    read(i, "sc", l, s, hf, t)
                else:
                    pe.wait_ge(*(probs_ready if l == 0 else exp_ready).at(l, s, hf, t))
                take(i)
                for c in (range(4), (4,))[r]:
                    p = min(128, ROWS8 - 128 * c)
                    last = tr(slot(i, 128, p, 128 * (c % 4)), unit_probs[k % 4][:, 128 * c:128 * c + p], 128)
                last.then_inc(*filled[i].mark("tp", l, s, hf, t, r))

            def mix_values(l, s, hf, t, k, i):
                read(i, "tp", l, s, hf, t, 1)
                if l == 0:
                    read(i, "v0", s, 1)
                    take(i)
                    for m in range(4):
                        for d in range(2):
                            last = mm(slot(i, 128, at=128 * m), v0[s][:, hf, m, d, :, :].rearrange("p r c -> p (r c)"),
                                      pT[k % 4][:, m + d, :], start=d == 0, stop=d == 1)
                else:
                    read(i, "val", l, s)
                    pe.wait_ge(*sums_set.at(s))
                    take(i)
                    for c in range(CHUNKS):
                        last = mm(slot(i, 72), pT[k % 4][:, c, :], vsum[s][:, c, hf, :], start=c == 0, stop=c == CHUNKS - 1)
                last.then_inc(*filled[i].mark("pv", l, s, hf, t))

            def turn_heads(l, s, t, i):
                read(i, "pv", l, s, 1, t)
                take(i)
                tr(slot(i, 128), xn[:, s, t, :], 128).then_inc(*filled[i].mark("heads", l, s, t))

            def project_rows(out, l, s, t):
                w, n, bias = {0: ("wu0", 8, "bu"), 2: ("wo1", 8, "bo1"), 4: ("wo2", 1, None), 6: ("wo3", 1, "bo3")}[l]
                need(pe, w)
                for m in range(n):
                    last = mm(out, oT[:, s if n == 1 else m, t * 128:(t + 1) * 128], W[w][:, m * 128:(m + 1) * 128],
                              start=m == 0, stop=bias is None and m == n - 1)
                if bias:
                    last = mm(out, ones[:, :], R(bias), start=False)
                return last

            def project_tile(l, s, t, i):
                read(i, *{0: ("pv", l, s, 1, t), 2: ("pv1", s, H1 - 1, t)}.get(l, ("heads", l, s, t)))
                take(i)
                project_rows(slot(i, 128), l, s, t).then_inc(*filled[i].mark("proj", l, s, t))

            def hidden(l, s, e, f, i):
                w = {1: "f0a", 3: "fc", 7: "fc"}[l]
                if l == 1:
                    need(pe, w)
                elif e == 0 and f == 0:
                    pe.wait_ge(loaded_moe.sem, it[0] * 32 + (16 if l == 3 else 32))
                if in_parts(l, s, e):
                    if f == 0:
                        pe.wait_ge(*low_part.at("weights", l, s, e))
                    take(i)
                    wh, wl = [a[:, 128 * f:128 * f + 128] for a in weight_parts[PARTED.index((l, s, e)) % 2]]
                    xh, xl = [a for a in token_parts[s]]
                    mm(slot(i, L), wh, xh, stop=False)
                    mm(slot(i, L), wh, xl, start=False, stop=False)
                    mm(slot(i, L), wl, xh, start=False).then_inc(*filled[i].mark("hid", l, s, e, f))
                    return
                read(i, "norm", l, s)
                take(i)
                c = 512 * e + 128 * f
                mm(slot(i, L), W[w][:, c:c + 128], xnT[:, s, :]).then_inc(*filled[i].mark("hid", l, s, e, f))

            def out_of(l, s, e, i, w, bias):
                read(i, "hid", l, s, e, FT - 1)
                take(i)
                for t in range(NT):
                    out = slot(i, 128, at=128 * t)
                    for f in range(FT):
                        c = 512 * e + 128 * f
                        h = hid_after if (l, s) == (1, 1) else hid[:, (e + s) % 2]
                        last = mm(out, h[:, f, t * 128:(t + 1) * 128], W[w][:, c:c + 128],
                                  start=f == 0, stop=not bias and f == FT - 1)
                    if bias:
                        last = mm(out, ones[:, :], R(bias), start=False)
                last.then_inc(*filled[i].mark("out", l, s, e))

            def ffn_out(s, i):
                out_of(1, s, 0, i, "f0b", "b2_0")

            def expert_out(l, s, e, i):
                out_of(l, s, e, i, "pj", None)

            def media_turn(s, i):
                pe.wait_ge(*mn_ready.at(s))
                take(i)
                tr(slot(i, KEYS), mn[:, s, :], KEYS).then_inc(*filled[i].mark("media", s))

            def values1(s, c, h, i):
                need(pe, "wv1")
                read(i, "norm", 2, s)
                take(i)
                lhs, p = (mnT[:, s, :], KEYS) if c == 4 else (xnT[:, s, c * 128:(c + 1) * 128], 128)
                mm(slot(i, 512, p), lhs, W["wv1"][:, 512 * h:512 * h + 512]).then_inc(*filled[i].mark("v1", s, c, h))

            def media_keys1(s, h, i):
                need(pe, "wk1")
                read(i, "media", s)
                take(i)
                for m in range(4):
                    c = 128 * (4 * h + m)
                    last = mm(slot(i, KEYS, at=KEYS * m), W["wk1"][:, c:c + 128], mnT[:, s, :])
                last.then_inc(*filled[i].mark("km1", s, h))

            def queries1(s, h, i):
                take(i)
                mm(slot(i, L), W["wq1"][:, 128 * h:128 * h + 128], xnT[:, s, :]).then_inc(*filled[i].mark("q1", s, h))

            def keys1(s, h, i):
                take(i)
                mm(slot(i, L), W["wk1"][:, 128 * h:128 * h + 128], xnT[:, s, :]).then_inc(*filled[i].mark("k1", s, h))

            def scores1(s, h, t, i):
                read(i, "q1", s, h)
                read(i, "k1", s, h)
                take(i)
                q = qh[:, h % 2, t * 128:(t + 1) * 128]
                mm(slot(i, L), q, kh[:, h % 2, :])
                mm(slot(i, KEYS, at=512), q, kmedia[:, s, h, :]).then_inc(*filled[i].mark("s1", s, h, t))

            def turn_probs1(s, h, t, k, r, i):
                pe.wait_ge(*probs1_ready.at(s, h, t))
                take(i)
                for c in (range(4), (4,))[r]:
                    p = KEYS if c == 4 else 128
                    last = tr(slot(i, 128, p, 128 * (c % 4)), row_probs[k % 4][:, 128 * c:128 * c + p], 128)
                last.then_inc(*filled[i].mark("tp1", s, h, t, r))

            def mix_values1(s, h, t, k, i):
                if h == 0 and t == 0:
                    read(i, "v1", s, 3, 0)
                    read(i, "v1", s, 3, 1)
                read(i, "tp1", s, h, t, 1)
                take(i)
                for c in range(5):
                    last = mm(slot(i, 128), v1[s][:, c, 128 * h:128 * h + 128], pT[k % 4][:, c, :],
                              start=c == 0, stop=c == 4)
                last.then_inc(*filled[i].mark("pv1", s, h, t))

            def logits(l, s, i):
                w = {3: "gate1", 7: "gate3"}[l]
                need(pe, w)
                read(i, "norm", l, s)
                take(i)
                for t in range(NT):
                    last = mm(slot(i, E, at=E * t), xnT[:, s, t * 128:(t + 1) * 128], W[w], stop=l == 3)
                    if l == 7:
                        last = mm(slot(i, E, at=E * t), ones[:, :], R("br3"), start=False)
                last.then_inc(*filled[i].mark("logits", l, s))

            def turn_gates(s, i):
                pe.wait_ge(*gate_ready.at(7, s))
                take(i)
                for t in range(NT):
                    last = tr(slot(i, 128, E, 128 * t), gt[:, s, 7, E * t:E * t + E], 128)
                last.then_inc(*filled[i].mark("gT", s))

            def gate_bias(s, i):
                read(i, "gT", s)
                take(i)
                for t in range(NT):
                    last = mm(slot(i, 128, at=128 * t), gT[:, t * 128:(t + 1) * 128], R("b2_3", E))
                last.then_inc(*filled[i].mark("gb", s))

            def project_heads(l, s, i, j, k, n):
                wq, wqr, wk, wkr, wv = ("wq2", "wqr2", "wk2", "wkr2", "wv2") if l == 4 else ("wq3", None, "wk3", None, "wv3")
                need(pe, wq)
                cT = ctxT[:, s * KEYS:(s + 1) * KEYS]
                read(i, "norm", l, s)
                take(i)
                last = mm(slot(i, KEYS), W[wk], cT)
                if l == 4:
                    last = mm(slot(i, KEYS, at=KEYS), W[wkr], cT)
                last.then_inc(*filled[i].mark("kv", l, s))
                take(j)
                mm(slot(j, L), W[wq], xnT[:, s, :]).then_inc(*filled[j].mark("q", l, s))
                if l == 4:
                    take(k)
                    mm(slot(k, L), W[wqr], xnT[:, s, :]).then_inc(*filled[k].mark("qr", l, s))
                take(n)
                for c in range(CHUNKS):
                    last = mm(slot(n, 128, at=128 * c), ctx_again[:, s, 128 * c:128 * (c + 1)], W[wv], stop=l == 4)
                    if l == 6:
                        last = mm(slot(n, 128, at=128 * c), ones[:, :], R("vb3"), start=False)
                last.then_inc(*filled[n].mark("val", l, s))

            def global_net(s, part, i):
                if part == 3:
                    return
                if part == 0:
                    pe.wait_ge(*mean_ready.at(s))
                else:
                    read(i, "g", s, part - 1)
                take(i)
                pe.sem_inc(held_pe.sem, 1)
                lhs, p, q = ((W["gw1"], 128, 64), (W["gw2"], 64, 32), (W["gw3"], 32, 128))[part]
                mm(slot(i, 1, q), lhs[0:p, :], gl[0:p, s, part:part + 1]).then_inc(*filled[i].mark("g", s, part))

            def cycle(s, c, stage, half, i):
                src, q = (xnT if c == 0 else cur)[:, s, :], slice(256 * half, 256 * half + 256)
                if stage == 0 and c:
                    pe.wait_ge(*coup_ready.at(s, c - 1, half))
                if stage == 0 and not c:
                    read(i, "norm", 5, s)
                if stage in (1, 2, 3):
                    read(i, "cy", s, c, stage - 1, half)
                take(i)
                if stage == 0:
                    last = mm(slot(i, 256), W["cw1"], src[:, q])
                elif stage == 4:
                    last = mm(slot(i, L), W["twist"], src)
                else:
                    last = mm(slot(i, 256), W[("cw2", "cw3", "cw4")[stage - 1]], net[:, 4 * s + stage - 1, q])
                last.then_inc(*filled[i].mark("cy", s, c, stage, half))

            def cycle_out(s, i):
                pe.wait_ge(*coup_ready.at(s, 2, 1))
                take(i)
                for t in range(NT):
                    last = tr(slot(i, 128, at=128 * t), cur[:, s, t * 128:(t + 1) * 128], 128)
                last.then_inc(*filled[i].mark("cyo", s))

            parts = dict(norm_turn=norm_turn, values0=values0, queries0=queries0, turn_queries=turn_queries,
                         scores=scores, turn_probs=turn_probs, mix_values=mix_values, project_tile=project_tile, turn_heads=turn_heads,
                         hidden=hidden, ffn_out=ffn_out, expert_out=expert_out, media_turn=media_turn,
                         values1=values1, media_keys1=media_keys1, queries1=queries1, keys1=keys1,
                         scores1=scores1, turn_probs1=turn_probs1, mix_values1=mix_values1, logits=logits,
                         turn_gates=turn_gates, gate_bias=gate_bias, project_heads=project_heads, global_net=global_net,
                         cycle=cycle, cycle_out=cycle_out)
            need(pe, "ident")
            pe.wait_ge(consts_ready.sem, 6)
            pe.wait_ge(loaded_small.sem, 16 * NSMALL)
            with pe.Fori(0, PAIRS) as pair:
                it[0] = pair
                for kind, args in steps:
                    if kind in parts:
                        parts[kind](*args)
            it[0] = 0

        @block.scalar
        def _(act):
            def f(out, in_, func, **kw):
                return nc.scalar.activation(out, in_, func, **kw)

            def norm_turn(l, s, i):
                act.wait_ge(*filled[i].at("norm", l, s))
                if l == 2:
                    last = f(xnT[:, s, :], slot(i, L), ACT.Identity, scale=V("gl"), bias=V("bl"))
                else:
                    last = f(xnT[:, s, :], slot(i, L), ACT.Copy)
                last.then_inc(*free[i].mark("norm", l, s))

            def repeat_context(s):
                if s == 0:
                    act.wait_ge(loaded_ctx.sem, it[0] * 32 + 32)
                c = ctxT[:, s * KEYS:(s + 1) * KEYS]
                f(ctx_again[:, s, 0:ROWS8].rearrange("p (h k) -> p h k", h=8), c.unsqueeze(1).broadcast_to([128, 8, KEYS]),
                  ACT.Copy)
                f(ctx_again[:, s, ROWS8:], c[:, 0:128 * CHUNKS - ROWS8], ACT.Copy).then_inc(*context_set.mark(s))

            def head_norm(s, k, i):
                p = KEYS if k == 4 else 128
                act.wait_ge(*filled[i].at("q0", s, k))
                if prev_sq[0] is not None:
                    act.wait_ge(*hsum_ready.at(*prev_sq[0]))
                prev_sq[0] = (s, k)
                f(sq[0:p, :], slot(i, 1024, p), ACT.Square).then_inc(*squares.mark(s, k))

            def head_root(s, k):
                p = KEYS if k == 4 else 128
                act.wait_ge(*hsum_ready.at(s, k))
                n = TILES0.index((s, k)) % 2
                f(hn[0:p, 2 + 2 * n, :], hn[0:p, 1 + 2 * n, :], ACT.Sqrt, scale=1.0 / DH0, bias=eps[0:p, :]).then_inc(*hroot_ready.mark(s, k))

            prev_sq = [None]

            def turn_queries(s, k, n, h, i):
                p = KEYS if k == 4 else 128
                act.wait_ge(*filled[i].at("tq", s, k, h))
                src = slot(i).rearrange("p (m c) -> p m c", m=4)[:, :, 0:p] if k < 4 else \
                    slot(i)[:, :].rearrange("p (m c) -> p m c", m=4)[:, :, 0:KEYS]
                if k == 4:
                    act.wait_ge(*kbd0_clear.at(s))
                    for r in range(2):
                        half, a, b = slice(64 * r, 64 * r + 64), vcols["kw"][0], vcols["kb"][0]
                        last = f(kbd0[s][half, 4 * h:4 * h + 4, r, :], src[half, :, :], ACT.Identity,
                                 scale=vec[half, a:a + 1], bias=vec[half, b:b + 1])
                else:
                    last = f(qT0[s][:, 4 * h:4 * h + 4, k * 128:(k + 1) * 128], src, ACT.Identity,
                             scale=scaled[:, 0:1], bias=scaled[:, 1:2])
                last.then_inc(*free[i].mark("tq", s, k, h))

            def exp(l, s, hf, t, i, k):
                if by_head(l, k):
                    act.wait_ge(*unit_max.at(l, s, hf, t))
                    for h in range(8):
                        last = f(unit_probs[k % 4][:, KEYS * h:KEYS * (h + 1)], slot(i, KEYS, at=512 * (h // 4) + KEYS * (h % 4)),
                                 ACT.Exp, bias=nmax[:, k % 4, h:h + 1])
                    last.then_inc(*free[i].mark("sc", l, s, hf, t))
                    return
                act.wait_ge(*reader_did("sc", l, s, hf, t))
                f(unit_probs[k % 4], unit_probs[k % 4], ACT.Exp).then_inc(*exp_ready.mark(l, s, hf, t))

            def turn_probs(l, s, hf, t, k, r, i):
                act.wait_ge(*filled[i].at("tp", l, s, hf, t, r))
                out, src = (pT[k % 4][:, 0:4, :].rearrange("p c q -> p (c q)"), slot(i)) if r == 0 else \
                    (pT[k % 4][0:ROWS8 - 512, 4, :], slot(i, 128, ROWS8 - 512))
                f(out, src, ACT.Copy).then_inc(*free[i].mark("tp", l, s, hf, t, r))

            def mix_values(l, s, hf, t, k, i):
                if l:
                    return
                act.wait_ge(*filled[i].at("pv", l, s, hf, t))
                f(oT[:, 4 * hf:4 * hf + 4, t * 128:(t + 1) * 128], slot(i).rearrange("p (m q) -> p m q", m=4), ACT.Copy)\
                    .then_inc(*free[i].mark("pv", l, s, hf, t))

            def turn_heads(l, s, t, i):
                act.wait_ge(*filled[i].at("heads", l, s, t))
                f(oT[:, s, t * 128:(t + 1) * 128], slot(i, 128), ACT.Copy).then_inc(*free[i].mark("heads", l, s, t))

            def hidden(l, s, e, fi, i):
                act.wait_ge(*filled[i].at("hid", l, s, e, fi))
                kw = {1: dict(func=ACT.Relu, bias=V("b1_0", fi)), 3: dict(func=ACT.Gelu),
                      7: dict(func=ACT.Relu, bias=V("b1_3", 4 * e + fi))}[l]
                func = kw.pop("func")
                f((hid_after if (l, s) == (1, 1) else hid[:, (e + s) % 2])[:, fi, :], slot(i, L), func, **kw).then_inc(*free[i].mark("hid", l, s, e, fi))

            def split_tokens(l, s):
                act.wait_ge(*tensor_did("proj", l - 1, 1, NT - 1))
                act.wait_ge(*reader_did("norm", l, s))
                f(token_parts[s][0], xnT[:, s, :], ACT.Copy).then_inc(*high_part.mark("tokens", l, s))

            def split_weights(l, s, e):
                parts_free(act, l, s, e)
                act.wait_ge(loaded_moe.sem, it[0] * 32 + (16 if l == 3 else 32))
                f(weight_parts[PARTED.index((l, s, e)) % 2][0], W["fc"][:, 512 * e:512 * e + 512], ACT.Copy)\
                    .then_inc(*high_part.mark("weights", l, s, e))

            def media_turn(s, i):
                act.wait_ge(*filled[i].at("media", s))
                f(mnT[:, s, :], slot(i, KEYS), ACT.Identity, scale=V("gm"), bias=V("bm"))\
                    .then_inc(*free[i].mark("media", s))

            def values1(s, c, h, i):
                if h == 1:
                    return
                p = KEYS if c == 4 else 128
                act.wait_ge(*filled[i].at("v1", s, c, h))
                f(v1[s][0:p, c, 512 * h:512 * h + 512], slot(i, 512, p), ACT.Copy).then_inc(*free[i].mark("v1", s, c, h))

            def media_keys1(s, h, i):
                act.wait_ge(*filled[i].at("km1", s, h))
                for m in range(4):
                    last = f(kmedia[:, s, 4 * h + m, :], slot(i, KEYS, at=KEYS * m), ACT.Identity,
                             bias=V("bk1", 4 * h + m))
                last.then_inc(*free[i].mark("km1", s, h))

            def queries1(s, h, i):
                act.wait_ge(*filled[i].at("q1", s, h))
                f(qh[:, h % 2, :], slot(i, L), ACT.Identity, scale=float(128 ** -0.5), bias=scaled[:, 2 + h:3 + h])\
                    .then_inc(*free[i].mark("q1", s, h))

            def softmax1(s, h, t, k, i):
                act.wait_ge(*nmax_ready.at(s, h, t))
                f(row_probs[k % 4], slot(i, 589), ACT.Exp, bias=nmax[:, k % 4, 0:1], accum_out=rsum[:, k % 4, 0, 0:1])\
                    .then_inc(*free[i].mark("s1", s, h, t))

            def turn_probs1(s, h, t, k, r, i):
                act.wait_ge(*filled[i].at("tp1", s, h, t, r))
                out, src = (pT[k % 4][:, 0:4, :].rearrange("p c q -> p (c q)"), slot(i)) if r == 0 else \
                    (pT[k % 4][0:KEYS, 4, :], slot(i, 128, KEYS))
                f(out, src, ACT.Copy).then_inc(*free[i].mark("tp1", s, h, t, r))

            def gates(l, s, part):
                if part:
                    return
                act.wait_ge(*reader_did("logits", l, s))
                f(gt[:, s, 1, :], gt[:, s, 0, :], ACT.Exp).then_inc(*gate_exp.mark(l, s))

            def global_net(s, part, i):
                if part == 3:
                    return
                act.wait_ge(*filled[i].at("g", s, part))
                if part < 2:
                    p, b = ((64, "gb1"), (32, "gb2"))[part]
                    last = f(gl[0:p, s, part + 1:part + 2], slot(i, 1, p), ACT.Gelu, bias=V(b, p=p))
                else:
                    last = f(gl[:, s, 3:4], slot(i, 1), ACT.Tanh, scale=0.5, bias=scaled[:, 11:12])
                last.then_inc(*free[i].mark("g", s, part))

            def cycle(s, c, stage, half, i):
                if stage == 4:
                    return
                q = slice(256 * half, 256 * half + 256)
                act.wait_ge(*filled[i].at("cy", s, c, stage, half))
                if stage == 3 and c:
                    act.wait_ge(*coup_ready.at(s, c - 1, half))
                if stage < 3:
                    last = f(net[:, 4 * s + stage, q], slot(i, 256), ACT.Gelu, bias=V(("cb1", "cb2", "cb3")[stage]))
                else:
                    last = f(net[:, 4 * s + 3, q], slot(i, 256), ACT.Tanh, scale=0.5, bias=scaled[:, 10:11])
                last.then_inc(*free[i].mark("cy", s, c, stage, half))

            parts = dict(norm_turn=norm_turn, repeat_context=repeat_context, head_norm=head_norm, head_root=head_root,
                         turn_queries=turn_queries, exp=exp,
                         turn_probs=turn_probs, mix_values=mix_values, turn_heads=turn_heads, hidden=hidden, media_turn=media_turn,
                         split_tokens=split_tokens, split_weights=split_weights,
                         values1=values1, media_keys1=media_keys1, queries1=queries1, softmax1=softmax1,
                         turn_probs1=turn_probs1, gates=gates, global_net=global_net, cycle=cycle)
            def load(*groups):
                for g in groups:
                    act.dma_start(group_tiles[g][:], dram["w_" + g]).then_inc(loaded[g].sem, 16)

            load("first", "second")
            act.wait_ge(loaded_small.sem, 16 * NSMALL)
            load("rest0", "l1", "l2", "l3")
            a = vcols["g"][0]
            f(gates_t[:, :], vec[:, a:a + 8], ACT.Tanh).then_inc(gates_tanh.sem, 1)
            act.wait_ge(consts_ready.sem, 6)
            with act.Fori(0, PAIRS) as pair:
                it[0] = pair
                for kind, args in steps:
                    if kind in parts:
                        parts[kind](*args)
            it[0] = 0

        @block.gpsimd
        def _(pool):
            def norm_stats(l, s, again=False):
                pool.wait_ge(*var_ready.at(l, s, again))
                nc.gpsimd.tensor_tensor(rs[:, s, int(again), :], ve[:, s, int(again), :], half_power[:, 0:NT], ALU.pow)\
                    .then_inc(*rstd_ready.mark(l, s, again))

            def norm_again(l, s):
                norm_stats(l, s, True)

            def clear_keys0(s):
                if s == 1:
                    nc.gpsimd.memset(v1[0][:, 4, :], 0.0)
                nc.gpsimd.memset(kbd0_flat[s], 0.0).then_inc(*kbd0_clear.mark(s))

            def project_heads(l, s, i, j, k, n):
                need(pool, "block")
                pool.wait_ge(*reader_did("kv", l, s))
                nc.gpsimd.tensor_tensor(kbd[s], rot[s][:, 1, 0:KEYS].unsqueeze(1).broadcast_to([128, 16, KEYS]),
                                        W["block"].unsqueeze(2).broadcast_to([128, 16, KEYS]), ALU.mult)\
                    .then_inc(*heads_ready.mark(l, s))

            def sum_columns(s):
                for g in range(2):
                    last = nc.gpsimd.tensor_copy(vsum[s][:, :, g, 64:72], own_head)
                last.then_inc(*sums_set.mark(s))

            def media_norm(s):
                pool.wait_ge(*mvar_ready.at(s))
                nc.gpsimd.tensor_tensor(mmv[:, s, 3:4], mmv[:, s, 2:3], half_power[0:KEYS, 0:1], ALU.pow)\
                    .then_inc(*mrstd_ready.mark(s))

            def normalise(l, s, hf, t, k):
                pool.wait_ge(*rsum_ready.at(l, s, hf, t))
                pr = unit_probs[k % 4].rearrange("p (h k) -> p h k", h=8)
                nc.gpsimd.tensor_tensor(pr, pr, rsum[:, k % 4, 1, :].unsqueeze(2).broadcast_to([128, 8, KEYS]), ALU.mult)\
                    .then_inc(*probs_ready.mark(l, s, hf, t))

            parts = dict(norm_stats=norm_stats, norm_again=norm_again, media_norm=media_norm,
                         normalise=normalise, clear_keys0=clear_keys0, sum_columns=sum_columns, project_heads=project_heads)
            pool.memset(half_power[:], -0.5).then_inc(consts_ready.sem, 1)
            pool.wait_ge(consts_ready.sem, 6)
            with pool.Fori(0, PAIRS) as pair:
                it[0] = pair
                for kind, args in steps:
                    if kind in parts:
                        parts[kind](*args)
            it[0] = 0

        @block.vector
        def _(dve):
            auto = [0]

            def link(ins):
                auto[0] += 1
                ins.then_inc(*dve_step.mark("link", auto[0]))
                dve.wait_ge(*dve_step.at("link", auto[0]))

            v = nc.vector

            def norm_stats(l, s):
                if l == 0:
                    dve.wait_ge(loaded_x[s].sem, it[0] * 16 + 16)
                if l % 2:
                    dve.wait_ge(*stats_ready.at(l, s, NT - 1))
                else:
                    for t in range(NT):
                        last = v.bn_stats(stat[:, s, t, :], x[:, s, t, :])
                    link(last)
                dve.sem_inc(held_dve.sem, 1)
                for t in range(NT):
                    last = v.bn_aggr(mv[:, s, t, :], stat[:, s, t, :])
                link(last)
                v.tensor_scalar(ve[:, s, 0, :], mv[:, s, :, 1], EPS, None, ALU.add)\
                    .then_inc(*var_ready.mark(l, s, False))

            def norm_again(l, s):
                dve.wait_ge(*rstd_ready.at(l, s, False))
                link(v.tensor_tensor(rs[:, s, 2, :], rs[:, s, 0, :], rs[:, s, 0, :], ALU.mult))
                link(v.tensor_tensor(rs[:, s, 2, :], rs[:, s, 2, :], mv[:, s, :, 1], ALU.mult))
                v.tensor_scalar(ve[:, s, 1, :], rs[:, s, 2, :], EPS, None, ALU.add)\
                    .then_inc(*var_ready.mark(l, s, True))

            def norm_apply(l, s):
                r = 0
                dve.wait_ge(*rstd_ready.at(l, s, l == 2))
                if l == 2:
                    link(v.tensor_tensor(rs[:, s, 2, :], rs[:, s, 0, :], rs[:, s, 1, :], ALU.mult))
                    r = 2
                for t in range(NT):
                    last = v.tensor_scalar(xn[:, s, t, :], x[:, s, t, :], mv[:, s, t, 0:1], rs[:, s, r, t:t + 1],
                                           ALU.subtract, ALU.mult)
                last.then_inc(*xn_ready.mark(l, s))

            def media_norm(s):
                if s == 0:
                    dve.wait_ge(loaded_ctx.sem, it[0] * 32 + 32)
                link(v.bn_stats(mstat[:, s, :], ctx_rows[:, s, :]))
                dve.sem_inc(held_dve.sem, 1)
                link(v.bn_aggr(mmv[:, s, 0:2], mstat[:, s, :]))
                v.tensor_scalar(mmv[:, s, 2:3], mmv[:, s, 1:2], EPS, None, ALU.add).then_inc(*mvar_ready.mark(s))
                dve.wait_ge(*mrstd_ready.at(s))
                v.tensor_scalar(mn[:, s, :], ctx_rows[:, s, :], mmv[:, s, 0:1], mmv[:, s, 3:4],
                                ALU.subtract, ALU.mult).then_inc(*mn_ready.mark(s))

            def values0(s, h, i):
                dve.wait_ge(*filled[i].at("v0", s, h))
                src = slot(i).rearrange("p (m d r c) -> p m d r c", m=4, d=2, r=2)
                for d in range(2):
                    last = v.tensor_tensor(v0[s][:, h, :, d, :, :], src[:, :, d, :, :],
                                           own_pair[d].unsqueeze(3).broadcast_to([128, 4, 2, DH0]), ALU.mult)
                last.then_inc(*free[i].mark("v0", s, h))

            def head_norm(s, k, i):
                p = KEYS if k == 4 else 128
                dve.wait_ge(*squares.at(s, k))
                v.tensor_reduce(hn[0:p, 1 + 2 * (TILES0.index((s, k)) % 2), :],
                                sq[0:p, :].rearrange("p (h d) -> p h d", h=16), AX, ALU.add).then_inc(*hsum_ready.mark(s, k))

            def head_scale(s, k, n, i):
                p = KEYS if k == 4 else 128
                dve.wait_ge(*hroot_ready.at(s, k))
                if n >= 2:
                    dve.wait_ge(*tensor_did("tq", *TILES0[n - 2], 1))
                link(v.reciprocal(hn[0:p, 2 + 2 * (n % 2), :], hn[0:p, 2 + 2 * (n % 2), :]))
                v.tensor_tensor(qn[0:p, n % 2, :].rearrange("p (h d) -> p h d", h=16),
                                slot(i, 1024, p).rearrange("p (h d) -> p h d", h=16),
                                hn[0:p, 2 + 2 * (n % 2), :].unsqueeze(2).broadcast_to([p, 16, DH0]), ALU.mult)\
                    .then_inc(*free[i].mark("q0", s, k))

            def less_max(l, s, hf, t, i, k):
                dve.wait_ge(*filled[i].at("sc", l, s, hf, t))
                sc = scores_of(i).rearrange("p r (j k) -> p r j k", j=4)
                if l == 6:
                    m = mask[:, t * KEYS:(t + 1) * KEYS]
                    dve.sem_inc(held_dve.sem, 1)
                    for r in range(2):
                        last = v.copy_predicated(
                            sc[:, r, :, :], m.unsqueeze(1).broadcast_to([128, 4, KEYS]),
                            low[:, 0:1].unsqueeze(2).broadcast_to([128, 4, KEYS]))
                    link(last)
                v.tensor_reduce(nmax[:, k % 4, :], sc, AX, ALU.max, negate=True).then_inc(*unit_max.mark(l, s, hf, t))
                if not by_head(l, k):
                    dve.wait_ge(*unit_max.at(l, s, hf, t))
                    nm = nmax[:, k % 4, :].rearrange("p (r j) -> p r j", r=2).unsqueeze(3).broadcast_to([128, 2, 4, KEYS])
                    v.tensor_tensor(unit_probs[k % 4].rearrange("p (r j k) -> p r j k", r=2, j=4), sc, nm, ALU.add)\
                        .then_inc(*free[i].mark("sc", l, s, hf, t))

            def normalise(l, s, hf, t, k):
                dve.wait_ge(*exp_ready.at(l, s, hf, t))
                link(v.tensor_reduce(rsum[:, k % 4, 0, :], unit_probs[k % 4].rearrange("p (h k) -> p h k", h=8),
                                     AX, ALU.add))
                v.reciprocal(rsum[:, k % 4, 1, :], rsum[:, k % 4, 0, :]).then_inc(*rsum_ready.mark(l, s, hf, t))

            def mix_values(l, s, hf, t, k, i):
                if l == 0:
                    return
                dve.wait_ge(*filled[i].at("pv", l, s, hf, t))
                link(v.reciprocal(rsum[:, k % 4, 1, :], slot(i, 8, at=64)))
                v.tensor_tensor(xn[:, s, t, 64 * hf:64 * hf + 64].rearrange("p (h d) -> p h d", h=8),
                                slot(i, 64).rearrange("p (h d) -> p h d", h=8),
                                rsum[:, k % 4, 1, :].unsqueeze(2).broadcast_to([128, 8, 8]), ALU.mult)\
                    .then_inc(*free[i].mark("pv", l, s, hf, t))

            def add_to_x(l, s, i, label):
                dve.wait_ge(*filled[i].at(*label))
                xs = x[:, s, :, :].rearrange("p t d -> p (t d)")
                v.scalar_tensor_tensor(xs, slot(i, L), gates_t[:, l:l + 1], xs, ALU.mult, ALU.add)\
                    .then_inc(*free[i].mark(*label))
                dve.wait_ge(*free[i].at(*label))

            def project_tile(l, s, t, i):
                dve.wait_ge(*filled[i].at("proj", l, s, t))
                v.scalar_tensor_tensor(x[:, s, t, :], slot(i, 128), gates_t[:, l:l + 1], x[:, s, t, :], ALU.mult, ALU.add)\
                    .then_inc(*free[i].mark("proj", l, s, t))
                dve.wait_ge(*free[i].at("proj", l, s, t))
                v.bn_stats(stat[:, s, t, :], x[:, s, t, :]).then_inc(*stats_ready.mark(l + 1, s, t))

            def ffn_out(s, i):
                add_to_x(1, s, i, ("out", 1, s, 0))

            def cycle_out(s, i):
                add_to_x(5, s, i, ("cyo", s))

            def expert_out(l, s, e, i):
                dve.wait_ge(*filled[i].at("out", l, s, e))
                for t in range(NT):
                    last = v.scalar_tensor_tensor(x[:, s, t, :], slot(i, 128, at=128 * t),
                                                  gt[:, s, 7, E * t + e:E * t + e + 1], x[:, s, t, :],
                                                  ALU.mult, ALU.add)
                last.then_inc(*free[i].mark("out", l, s, e))
                dve.wait_ge(*free[i].at("out", l, s, e))

            def values1(s, c, h, i):
                if h == 0:
                    return
                p = KEYS if c == 4 else 128
                if c == 4:
                    dve.wait_ge(*kbd0_clear.at(1))
                dve.wait_ge(*filled[i].at("v1", s, c, h))
                v.tensor_copy(v1[s][0:p, c, 512 * h:512 * h + 512], slot(i, 512, p)).then_inc(*free[i].mark("v1", s, c, h))

            def keys1(s, h, i):
                dve.wait_ge(*filled[i].at("k1", s, h))
                v.tensor_scalar(kh[:, h % 2, :], slot(i, L), V("bk1", h), None, ALU.add).then_inc(*free[i].mark("k1", s, h))

            def softmax1(s, h, t, k, i):
                dve.wait_ge(*filled[i].at("s1", s, h, t))
                v.tensor_reduce(nmax[:, k % 4, 0:1], slot(i, 589), AX, ALU.max, negate=True).then_inc(*nmax_ready.mark(s, h, t))
                if k:
                    scale_row(k - 1)

            def scale_row(k):
                s, h, t = k // (H1 * NT), k // NT % H1, k % NT
                dve.wait_ge(*reader_did("s1", s, h, t))
                link(v.reciprocal(rsum[:, k % 4, 1, 0:1], rsum[:, k % 4, 0, 0:1]))
                v.tensor_scalar(row_probs[k % 4], row_probs[k % 4], rsum[:, k % 4, 1, 0:1], None, ALU.mult)\
                    .then_inc(*probs1_ready.mark(s, h, t))

            def mix_values1(s, h, t, k, i):
                if (s, h, t) == (NS - 1, H1 - 1, 0):
                    scale_row(NS * H1 * NT - 1)
                dve.wait_ge(*filled[i].at("pv1", s, h, t))
                v.tensor_scalar(oT[:, h, t * 128:(t + 1) * 128], slot(i, 128), V("bv1", h), None, ALU.add)\
                    .then_inc(*free[i].mark("pv1", s, h, t))

            def logits(l, s, i):
                dve.wait_ge(*filled[i].at("logits", l, s))
                lg = slot(i, NT * E).rearrange("p (t e) -> p t e", t=NT)
                mx = gt[:, s, 2, 0:NT]
                link(v.tensor_reduce(mx, lg, AX, ALU.max, negate=True))
                v.tensor_tensor(gt[:, s, 0, :].rearrange("p (t e) -> p t e", t=NT), lg,
                                mx.unsqueeze(2).broadcast_to([128, NT, E]), ALU.add).then_inc(*free[i].mark("logits", l, s))

            def gates(l, s, part):
                te = "p (t e) -> p t e"
                p3 = gt[:, s, 3, :].rearrange(te, t=NT)
                by_j = gt[:, s, 3, :].rearrange(te, t=NT).unsqueeze(2).broadcast_to([128, NT, E, E])
                by_e = gt[:, s, 3, :].rearrange(te, t=NT).unsqueeze(3).broadcast_to([128, NT, E, E])
                c = [cmp[:, n, :].rearrange("p (t e j) -> p t e j", t=NT, e=E) for n in range(3)]
                rank = gt[:, s, 4, :].rearrange(te, t=NT)
                tmp = gt[:, s, 5, :].rearrange(te, t=NT)
                out = gt[:, s, 7, :].rearrange(te, t=NT)
                one = gt[:, s, 2, 0:NT]
                if part == 0:
                    need(dve, "before")
                    dve.wait_ge(*gate_exp.at(l, s))
                    link(v.tensor_reduce(one, gt[:, s, 1, :].rearrange(te, t=NT), AX, ALU.add))
                    link(v.reciprocal(gt[:, s, 2, NT:2 * NT], one))
                    link(v.tensor_tensor(p3, gt[:, s, 1, :].rearrange(te, t=NT),
                                         gt[:, s, 2, NT:2 * NT].unsqueeze(2).broadcast_to([128, NT, E]), ALU.mult))
                elif part == 1:
                    v.tensor_tensor(c[0], by_j, by_e, ALU.is_gt)
                    link(v.tensor_tensor(c[1], by_j, by_e, ALU.is_equal))
                    tri = W["before"].rearrange("p (e j) -> p e j", e=E).unsqueeze(1).broadcast_to([128, NT, E, E])
                    link(v.tensor_tensor(c[1], c[1], tri, ALU.mult))
                    link(v.tensor_tensor(c[0], c[0], c[1], ALU.add))
                else:
                    link(v.tensor_reduce(rank, c[0], AX, ALU.add))
                    if l == 3:
                        link(v.scalar_tensor_tensor(tmp, rank, 2.0, p3, ALU.is_lt, ALU.mult))
                        link(v.tensor_reduce(one, tmp, AX, ALU.add))
                        link(v.reciprocal(gt[:, s, 2, NT:2 * NT], one))
                        link(v.scalar_tensor_tensor(out, tmp, gates_t[:, l:l + 1],
                                                    gt[:, s, 2, NT:2 * NT].unsqueeze(2).broadcast_to([128, NT, E]),
                                                    ALU.mult, ALU.mult))
                    else:
                        link(v.tensor_tensor(c[2], c[0], by_j, ALU.mult))
                        link(v.tensor_reduce(tmp, c[2], AX, ALU.add))
                        link(v.tensor_tensor(tmp, tmp, p3, ALU.add))
                        link(v.tensor_scalar(tmp, tmp, 0.8, None, ALU.is_lt))
                        link(v.tensor_scalar(rank, rank, 1.0, None, ALU.is_lt))
                        link(v.tensor_tensor(tmp, tmp, rank, ALU.max))
                        v.scalar_tensor_tensor(out, tmp, gates_t[:, l:l + 1], p3, ALU.mult, ALU.mult)\
                            .then_inc(*gate_ready.mark(l, s))
                        dve.wait_ge(*gate_ready.at(l, s))

            def split_tokens(l, s):
                dve.wait_ge(*high_part.at("tokens", l, s))
                high, low = token_parts[s]
                v.tensor_tensor(low, xnT[:, s, :], high.bitcast(F32), ALU.subtract).then_inc(*low_part.mark("tokens", l, s))

            def split_weights(l, s, e):
                dve.wait_ge(*high_part.at("weights", l, s, e))
                high, low = weight_parts[PARTED.index((l, s, e)) % 2]
                v.tensor_tensor(low, W["fc"][:, 512 * e:512 * e + 512], high.bitcast(F32), ALU.subtract)\
                    .then_inc(*low_part.mark("weights", l, s, e))

            def turn_gates(s, i):
                dve.wait_ge(*filled[i].at("gT", s))
                v.tensor_copy(gT[:, :], slot(i, 512, E)).then_inc(*free[i].mark("gT", s))

            def gate_bias(s, i):
                dve.wait_ge(*filled[i].at("gb", s))
                xs = x[:, s, :, :].rearrange("p t d -> p (t d)")
                v.tensor_tensor(xs, slot(i, L), xs, ALU.add).then_inc(*free[i].mark("gb", s))
                dve.wait_ge(*free[i].at("gb", s))

            def project_heads(l, s, i, j, k, n):
                dve.wait_ge(*filled[i].at("kv", l, s))
                rt = rot[s]
                kk = rt[:, 1, 0:KEYS]
                if l == 4:
                    v.tensor_tensor(kk, slot(i, KEYS), W["cos"][:, 0:KEYS], ALU.mult)
                    link(v.tensor_tensor(rt[:, 1, 128:128 + KEYS], slot(i, KEYS, at=KEYS), W["sin"][:, 0:KEYS], ALU.mult))
                    v.tensor_tensor(kk, kk, rt[:, 1, 128:128 + KEYS], ALU.add).then_inc(*free[i].mark("kv", l, s))
                else:
                    v.tensor_scalar(kk, slot(i, KEYS), V("kb3"), None, ALU.add).then_inc(*free[i].mark("kv", l, s))
                dve.wait_ge(*filled[j].at("q", l, s))
                if l == 4:
                    v.tensor_tensor(rt[:, 0, :], slot(j, L), W["cos"], ALU.mult).then_inc(*free[j].mark("q", l, s))
                    dve.wait_ge(*filled[k].at("qr", l, s))
                    dve.wait_ge(*free[j].at("q", l, s))
                    dve.wait_ge(*heads_ready.at(l, s))
                    v.tensor_tensor(rt[:, 1, :], slot(k, L), W["sin"], ALU.mult).then_inc(*free[k].mark("qr", l, s))
                    dve.wait_ge(*free[k].at("qr", l, s))
                    v.tensor_tensor(rt[:, 0, :], rt[:, 0, :], rt[:, 1, :], ALU.add).then_inc(*rotated.mark(l, s))
                else:
                    v.tensor_scalar(rt[:, 0, :], slot(j, L), V("qb3"), float(8 ** -0.5), ALU.add, ALU.mult)\
                        .then_inc(*free[j].mark("q", l, s))
                dve.wait_ge(*filled[n].at("val", l, s))
                for g in range(2):
                    last = v.tensor_tensor(
                        vsum[s][:, :, g, 0:64].rearrange("p c (h d) -> p c h d", h=8),
                        slot(n, 640).rearrange("p (c n) -> p c n", c=CHUNKS)[:, :, 64 * g:64 * g + 64]
                        .rearrange("p c (h d) -> p c h d", h=8),
                        own_head.unsqueeze(3).broadcast_to([128, CHUNKS, 8, 8]), ALU.mult)
                last.then_inc(*free[n].mark("val", l, s))

            def global_net(s, part, i):
                if part == 0:
                    dve.wait_ge(*reader_did("norm", 5, s))
                    link(v.tensor_reduce(gl[:, s, 4:5], xnT[:, s, :], AX, ALU.add))
                    v.tensor_scalar(gl[:, s, 0:1], gl[:, s, 4:5], 1.0 / L, None, ALU.mult).then_inc(*mean_ready.mark(s))
                if part == 3:
                    dve.wait_ge(*reader_did("g", s, 2))
                    link(v.tensor_scalar(gl[:, s, 5:6], gl[:, s, 3:4], scaled[:, 12:13], 0.1, ALU.mult, ALU.add))

            def couple(s, c, half, i):
                q = slice(256 * half, 256 * half + 256)
                src = (xnT if c == 0 else cur)[:, s, q]
                th = net[:, 4 * s + 3, q]
                dve.wait_ge(*reader_did("cy", s, c, 3, half))
                link(v.tensor_scalar(th, th, scaled[:, 13:14], gl[:, s, 5:6], ALU.mult, ALU.add))
                dve.wait_ge(*filled[i].at("cy", s, c, 4, 0))
                last = v.tensor_tensor(th, slot(i, 256, at=256 * half), th, ALU.mult)
                if half == 0:
                    link(last)
                else:
                    last.then_inc(*free[i].mark("cy", s, c, 4, 0))
                    dve.wait_ge(*free[i].at("cy", s, c, 4, 0))
                v.tensor_tensor(cur[:, s, q], src, th, ALU.add).then_inc(*coup_ready.mark(s, c, half))

            parts = dict(norm_stats=norm_stats, norm_again=norm_again, norm_apply=norm_apply, media_norm=media_norm,
                         values0=values0, head_norm=head_norm, head_scale=head_scale, less_max=less_max, normalise=normalise,
                         mix_values=mix_values, project_tile=project_tile, ffn_out=ffn_out, cycle_out=cycle_out, expert_out=expert_out,
                         values1=values1, keys1=keys1, softmax1=softmax1,
                         mix_values1=mix_values1, split_tokens=split_tokens, split_weights=split_weights,
                         logits=logits, gates=gates, turn_gates=turn_gates, gate_bias=gate_bias,
                         project_heads=project_heads, global_net=global_net, couple=couple)

            for i in range(6):
                dve.sem_inc(free[i].sem, 1)
            v.memset(ones[:], 1.0).then_inc(consts_ready.sem, 1)
            v.memset(eps[:], EPS)
            v.memset(low[:], NEG).then_inc(consts_ready.sem, 1)
            v.memset(v1[1][:, 4, :], 0.0)
            v.memset(arenaB[:], 0.0).then_inc(consts_ready.sem, 1)
            dve.wait_ge(loaded_small.sem, 16 * NSMALL)
            v.tensor_scalar(mask[:], mask[:], 0, None, ALU.is_equal).then_inc(consts_ready.sem, 1)
            a = vcols["qw"][0]
            v.tensor_scalar(scaled[:, 0:2], vec[:, a:a + 2], 0.125, None, ALU.mult).then_inc(centred_small.sem, 1)
            a = vcols["bq1"][0]
            v.tensor_scalar(scaled[:, 2:10], vec[:, a:a + 8], float(128 ** -0.5), None, ALU.mult).then_inc(centred_small.sem, 1)
            v.tensor_scalar(scaled[:, 10:11], V("cb4"), 0.5, None, ALU.mult).then_inc(centred_small.sem, 1)
            v.tensor_scalar(scaled[:, 11:12], V("gb3"), 0.5, None, ALU.mult).then_inc(centred_small.sem, 1)
            v.tensor_scalar(scaled[:, 12:13], V("ar"), 0.7, None, ALU.mult).then_inc(centred_small.sem, 1)
            v.tensor_scalar(scaled[:, 13:14], V("ar"), 0.3, None, ALU.mult).then_inc(centred_small.sem, 1)
            dve.wait_ge(centred_small.sem, 6)
            dve.sem_inc(consts_ready.sem, 1)
            for n, w in enumerate(("wk0", "wq0")):
                need(dve, w)
                w3 = W[w].rearrange("p (h d) -> p h d", h=16)
                v.tensor_reduce(centre[:], w3, AX, ALU.add).then_inc(centring.sem, 1)
                dve.wait_ge(centring.sem, 3 * n + 1)
                v.tensor_scalar(centre[:], centre[:], -1.0 / DH0, None, ALU.mult).then_inc(centring.sem, 1)
                dve.wait_ge(centring.sem, 3 * n + 2)
                v.tensor_tensor(w3, w3, centre[:].unsqueeze(2).broadcast_to([128, 16, DH0]), ALU.add)\
                    .then_inc(centring.sem, 1)
                dve.wait_ge(centring.sem, 3 * n + 3)
                dve.sem_inc(centred.sem, 1)
            dve.wait_ge(gates_tanh.sem, 1)
            dve.wait_ge(consts_ready.sem, 6)
            with dve.Fori(0, PAIRS) as pair:
                it[0] = pair
                for kind, args in steps:
                    if kind in parts:
                        parts[kind](*args)
            it[0] = 0
    for name, sg in signals.items():
        known[name].update(sg.seen)
        known[name]["total"] = sg.n
    for i in range(6):
        assert signals[f"filled_{i}"].seen.keys() == signals[f"free_{i}"].seen.keys()


def kernel(**inputs):
    import numpy as _np
    import concourse.bacc as _bacc
    from concourse.bass_utils import run_bass_kernel_spmd as _run

    a = {k: _np.asarray(v) for k, v in inputs.items()}

    def padded(w, n=None):
        out = _np.zeros((128, n or w.shape[1]), _np.float32)
        out[:w.shape[0], :w.shape[1]] = w
        return out

    def experts_in(w):
        return w.transpose(1, 0, 2).reshape(D, -1)

    def rows_by_tile(w):
        return w.reshape(-1, 128, w.shape[-1]).transpose(1, 0, 2).reshape(128, -1)

    heads = _np.arange(D)
    wkv = a["L2_xattn_Wkv"].reshape(16, 2, 8, D)
    wk2, wv2 = wkv[:, 0].reshape(D, D), wkv[:, 1].reshape(D, D)
    swap = heads ^ 1
    pos = _np.arange(L, dtype=_np.float32)[None, :]
    theta = _np.power(_np.float32(10000), _np.float32(2) * ((heads % 8) // 2).astype(_np.float32) / _np.float32(8))
    ang = (pos / theta[:, None]).astype(_np.float32)
    sign = _np.where(heads % 2 == 0, -1, 1).astype(_np.float32)[:, None]
    twist = _np.zeros((128, 128), _np.float32)
    q = _np.arange(32)
    twist[64 + q, q] = 1
    twist[96 + q, 32 + q] = -1
    twist[q, 64 + q] = -1
    twist[32 + q, 96 + q] = 1
    before = _np.broadcast_to((_np.arange(8)[None, :] < _np.arange(8)[:, None]).astype(_np.float32).reshape(1, 64), (128, 64))
    block = (heads[:, None] // 8 == _np.arange(16)[None, :]).astype(_np.float32)
    row = _np.arange(128)[:, None, None] + 128 * _np.arange(5)[None, :, None]
    own_head = (row // 77 == _np.arange(8)[None, None, :]).astype(_np.float32).reshape(128, 40)
    w = {
        "ident": _np.eye(128, dtype=_np.float32), "own_head": own_head,
        "wq0": a["L0_xattn_Wq"].T, "wk0": a["L0_xattn_Wk"].T, "wv0": a["L0_xattn_Wv"].T,
        "wu0": rows_by_tile(a["L0_xattn_Wu"].T), "f0a": a["L0_ffn_W1"], "f0b": rows_by_tile(a["L0_ffn_W2"]),
        "wq1": a["L1_xattn_Wq"], "wk1": a["L1_xattn_Wkv"][:, :1024], "wv1": a["L1_xattn_Wkv"][:, 1024:],
        "wo1": rows_by_tile(a["L1_xattn_Wo"]),
        "gate1": a["L1_ffn_gate_w"],
        "wq2": a["L2_xattn_Wq"].T, "wqr2": a["L2_xattn_Wq"][swap].T, "wk2": wk2.T, "wkr2": wk2[swap].T, "wv2": wv2.T,
        "wo2": a["L2_xattn_Wo"].T,
        "cw1": a["L2_ffn_cn_w1"], "cw2": padded(a["L2_ffn_cn_w2"], 128), "cw3": padded(a["L2_ffn_cn_w3"], 128),
        "cw4": padded(_np.tile(a["L2_ffn_cn_w4"], (1, 128))), "gw1": a["L2_ffn_gc_w1"], "gw2": padded(a["L2_ffn_gc_w2"]),
        "gw3": padded(_np.tile(a["L2_ffn_gc_w3"], (1, 128))),
        "twist": twist, "cos": _np.cos(ang), "sin": _np.sin(ang) * sign, "block": block, "before": before,
        "wq3": a["L3_xattn_wq_w"].T, "wk3": a["L3_xattn_wk_w"].T, "wv3": a["L3_xattn_wv_w"].T, "wo3": a["L3_xattn_wo_w"].T,
        "gate3": a["L3_ffn_Wr"],
    }

    def col(v):
        v = v.reshape(-1)
        return padded(v[:, None]) if v.size < 128 else v.reshape(-1, 128).T

    def same(v):
        return _np.tile(v.reshape(1, -1), (128, 1))

    gates = _np.stack([a["g_xattn"], a["g_ffn"]], 1).reshape(-1)
    vecs = {
        "qw": col(_np.tile(a["L0_xattn_qn_w"], 2)), "qb": col(_np.tile(a["L0_xattn_qn_b"], 2)),
        "kw": col(_np.tile(a["L0_xattn_kn_w"], 2)), "kb": col(_np.tile(a["L0_xattn_kn_b"], 2)),
        "b1_0": col(a["L0_ffn_b1"]), "gm": col(a["L1_xattn_gamma_media"]), "bm": col(a["L1_xattn_beta_media"]),
        "gl": col(a["L1_xattn_gamma_lat"]), "bl": col(a["L1_xattn_beta_lat"]), "bq1": col(a["L1_xattn_bq"]),
        "bk1": col(a["L1_xattn_bkv"][:1024]), "bv1": col(a["L1_xattn_bkv"][1024:]),
        "cb1": col(a["L2_ffn_cn_b1"]), "cb2": col(a["L2_ffn_cn_b2"]), "cb3": col(a["L2_ffn_cn_b3"]),
        "cb4": same(a["L2_ffn_cn_b4"]), "gb1": col(a["L2_ffn_gc_b1"]), "gb2": col(a["L2_ffn_gc_b2"]),
        "gb3": same(a["L2_ffn_gc_b3"]), "ar": same(a["L2_ffn_adaptive_range"]),
        "qb3": col(a["L3_xattn_wq_b"]), "kb3": col(a["L3_xattn_wk_b"]),
        "b1_3": col(a["L3_ffn_b1"]), "g": same(gates),
    }
    rws = _np.zeros((E, sum(n for _, n in ROWS)), _np.float32)
    at = columns(ROWS)[0]
    for name, v in (("bu", a["L0_xattn_bu"]), ("b2_0", a["L0_ffn_b2"]), ("bo1", a["L1_xattn_bo"]),
                    ("bo3", a["L3_xattn_wo_b"]), ("vb3", a["L3_xattn_wv_b"]), ("br3", a["L3_ffn_br"])):
        rws[0, at[name][0]:at[name][0] + at[name][1]] = v
    rws[:, at["b2_3"][0]:at["b2_3"][0] + 128] = a["L3_ffn_b2"]
    mask = a["mask_1x1xSxS2_ik0"].reshape(NT, 128, KEYS).transpose(1, 0, 2).reshape(128, NT * KEYS)
    arrays = {
        "x": a["x"].reshape(B * NT, 128, D).transpose(1, 0, 2).reshape(128, -1),
        "ctxT": a["ctx_1024"].transpose(2, 0, 1).reshape(D, -1),
        "ctx": a["ctx_1024"].transpose(1, 0, 2).reshape(KEYS, -1),
        "vec": _np.concatenate([vecs[n] for n, _ in VECS], 1),
        "rows": rws, "mask": mask,
        "w_moe1": _np.concatenate([experts_in(a["L1_ffn_fc_w"]), rows_by_tile(a["L1_ffn_proj_w"].reshape(-1, 128))], 1),
        "w_moe3": _np.concatenate([experts_in(a["L3_ffn_W1"]), rows_by_tile(a["L3_ffn_W2"].reshape(-1, 128))], 1),
    }
    for g, parts in W_GROUPS:
        arrays["w_" + g] = _np.concatenate([w[n] for n, _ in parts], 1)
    arrays = {k: _np.ascontiguousarray(v) for k, v in arrays.items()}

    known = {}
    for final in (False, True):
        nc = _bacc.Bacc("TRN2", target_bir_lowering=False, num_devices=1)
        dram = {k: nc.dram_tensor(f"in_{k}_dram", v.shape, mybir.dt.from_np(v.dtype), kind="ExternalInput").ap()
                for k, v in arrays.items()}
        dram["out"] = nc.dram_tensor("out_dram", (128, B * L), F32, kind="ExternalOutput").ap()
        program(nc, dram, known)
    r = _run(nc, [{f"in_{k}_dram": v for k, v in arrays.items()}], core_ids=[0])
    out = r.results[0]["out_dram"]
    return out.reshape(128, B * NT, D).transpose(1, 0, 2).reshape(B, L, D)
```
